# Optimizing a Trainium2 kernel written in Bass

```python
import numpy as np
import jax
import jax.numpy as jnp

def _softmax(x, axis=-1):
    return jax.nn.softmax(x, axis=axis)

def _gelu(x):
    return jax.nn.gelu(x, approximate=True)

def _silu(x):
    return jax.nn.silu(x)

def _sigmoid(x):
    return jax.nn.sigmoid(x)

def _layernorm(x, axis=-1, eps=1e-05):
    m = jnp.mean(x, axis=axis, keepdims=True)
    v = jnp.var(x, axis=axis, keepdims=True)
    return (x - m) / jnp.sqrt(v + eps)

def _scatter_add(tgt, idx, src, axis=0):
    return tgt.at[idx].add(src)

def _segment_sum(src, seg, n):
    return jax.ops.segment_sum(src, seg, n)
kernel_name = 'mk_conv_attn_hybrid_d2_conv_nhwc256_r4_748602'

def setup_inputs(seed: int=0):
    np.random.seed(seed)
    _w = jnp.asarray

    def _rec_inputs():
        import jax
        import jax.numpy as jnp
        _gk = jax.random.key(seed)
        x = 7.22e-05 + 1 * jax.random.normal(jax.random.fold_in(_gk, 1), (8, 16, 16, 64), jnp.float32)
        return x
    x = _rec_inputs()

    def _L0_conv_setup():
        import jax, jax.numpy as jnp
        import numpy as np
        from jax import lax
        K = 3
        PAD = 1
        STRIDE = 1
        DIL = 1
        OFFSET_SIZE = 2 * K * K

        def _dcnv2(x, om_kernel, om_bias, kernel, bias):
            B, H, W, C = x.shape
            om = lax.conv_general_dilated(x, om_kernel, window_strides=(STRIDE, STRIDE), padding=((PAD, PAD), (PAD, PAD)), rhs_dilation=(DIL, DIL), dimension_numbers=('NHWC', 'HWIO', 'NHWC')) + om_bias
            OH, OW = (om.shape[1], om.shape[2])
            KK = K * K
            offset = om[..., :OFFSET_SIZE].reshape(B, OH, OW, KK, 2)
            mask = jax.nn.sigmoid(om[..., OFFSET_SIZE:]) * 2.0
            kk = jnp.arange(KK)
            ky = (kk // K).astype(jnp.float32)
            kx = (kk % K).astype(jnp.float32)
            base_y = jnp.arange(OH, dtype=jnp.float32)[:, None] * STRIDE - PAD + ky[None, :] * DIL
            base_x = jnp.arange(OW, dtype=jnp.float32)[:, None] * STRIDE - PAD + kx[None, :] * DIL
            py = base_y[None, :, None, :] + offset[..., 0]
            px = base_x[None, None, :, :] + offset[..., 1]
            y0 = jnp.floor(py)
            x0 = jnp.floor(px)
            wy1 = py - y0
            wy0 = 1.0 - wy1
            wx1 = px - x0
            wx0 = 1.0 - wx1
            bi = jnp.arange(B)[:, None, None, None]

            def gather(yi, xi):
                valid = (yi >= 0) & (yi <= H - 1) & (xi >= 0) & (xi <= W - 1)
                yc = jnp.clip(yi, 0, H - 1).astype(jnp.int32)
                xc = jnp.clip(xi, 0, W - 1).astype(jnp.int32)
                v = x[bi, yc, xc]
                return v * valid[..., None].astype(x.dtype)
            y1 = y0 + 1.0
            x1 = x0 + 1.0
            cols = gather(y0, x0) * (wy0 * wx0)[..., None] + gather(y0, x1) * (wy0 * wx1)[..., None] + gather(y1, x0) * (wy1 * wx0)[..., None] + gather(y1, x1) * (wy1 * wx1)[..., None]
            cols = cols * mask[..., None]
            out = cols.reshape(B, OH, OW, KK * C) @ kernel
            return out + bias
        key = jax.random.key(seed)
        k1, k2, k3, k4 = jax.random.split(key, 4)
        B, H, W, C = (8, 16, 16, 64)
        F = 64
        inputs = jax.random.normal(k1, (B, H, W, C), dtype=jnp.float32)
        om_kernel = jax.random.normal(k2, (K, K, C, OFFSET_SIZE * 3 // 2), dtype=jnp.float32) * 0.01
        om_bias = jnp.zeros((OFFSET_SIZE * 3 // 2,), dtype=jnp.float32)
        stdv = 1.0 / np.sqrt(K * K * C)
        kernel = jax.random.uniform(k3, (K * K * C, F), dtype=jnp.float32, minval=-stdv, maxval=stdv)
        bias = jax.random.normal(k4, (1, 1, 1, F), dtype=jnp.float32) * 0.01
        return {'inputs': inputs, 'om_kernel': om_kernel, 'om_bias': om_bias, 'kernel': kernel, 'bias': bias}
    _L0_conv_all = _L0_conv_setup()
    _L0_conv_in = {k: v for k, v in _L0_conv_all.items() if k in ('om_kernel', 'om_bias', 'kernel', 'bias')}
    del _L0_conv_all

    def _L1_attn_setup():
        import jax, jax.numpy as jnp
        import numpy as np
        D_MODEL = 64
        D_STATE = 16
        D_CONV = 4
        D_INNER = 128
        DT_RANK = 16
        BN = 32
        M = 16
        PARAM_NAMES = ['in_proj_w', 'conv_w', 'conv_b', 'x_proj_w', 'dt_proj_w', 'dt_proj_b', 'A_log', 'D', 'out_proj_w']

        def _mamba(x, in_proj_w, conv_w, conv_b, x_proj_w, dt_proj_w, dt_proj_b, A_log, Dvec, out_proj_w):
            xz = x @ in_proj_w.T
            xs, z = jnp.split(xz, 2, axis=-1)
            xs_pad = jnp.pad(xs, ((0, 0), (D_CONV - 1, 0), (0, 0)))
            kern = jnp.transpose(conv_w, (2, 1, 0))
            xs = jax.lax.conv_general_dilated(xs_pad, kern, (1,), 'VALID', dimension_numbers=('NWC', 'WIO', 'NWC'), feature_group_count=D_INNER) + conv_b
            xs = jax.nn.silu(xs)
            dbc = xs @ x_proj_w.T
            dt = jax.nn.softplus(dbc[..., :DT_RANK] @ dt_proj_w.T + dt_proj_b)
            Bm = dbc[..., DT_RANK:DT_RANK + D_STATE]
            Cm = dbc[..., DT_RANK + D_STATE:]
            A = -jnp.exp(A_log)
            dA = jnp.exp(dt[..., None] * A)
            dBu = dt[..., None] * Bm[:, :, None, :] * xs[..., None]

            def combine(c1, c2):
                a1, b1 = c1
                a2, b2 = c2
                return (a1 * a2, a2 * b1 + b2)
            _, hs = jax.lax.associative_scan(combine, (dA, dBu), axis=1)
            y = jnp.einsum('blds,bls->bld', hs, Cm) + xs * Dvec
            y = y * jax.nn.silu(z)
            return y @ out_proj_w.T

        def _core(x, ln_gamma, ln_beta, fp, bp):
            mu = x.mean(-1, keepdims=True)
            var = x.var(-1, keepdims=True)
            xn = (x - mu) / jnp.sqrt(var + 1e-05) * ln_gamma + ln_beta
            y_fwd = _mamba(xn, *fp)
            y_bwd = jnp.flip(_mamba(jnp.flip(xn, 1), *bp), 1)
            return y_fwd + y_bwd + x

        def _mamba_params(key):
            ks = jax.random.split(key, 5)
            s = 0.02
            return {'in_proj_w': jax.random.normal(ks[0], (2 * D_INNER, D_MODEL)) * s, 'conv_w': jax.random.normal(ks[1], (D_INNER, 1, D_CONV)) * s, 'conv_b': jnp.zeros((D_INNER,)), 'x_proj_w': jax.random.normal(ks[2], (DT_RANK + 2 * D_STATE, D_INNER)) * s, 'dt_proj_w': jax.random.normal(ks[3], (D_INNER, DT_RANK)) * s, 'dt_proj_b': jnp.full((D_INNER,), -4.6), 'A_log': jnp.log(jnp.tile(jnp.arange(1, D_STATE + 1, dtype=jnp.float32), (D_INNER, 1))), 'D': jnp.ones((D_INNER,)), 'out_proj_w': jax.random.normal(ks[4], (D_MODEL, D_INNER)) * s}
        key = jax.random.key(seed)
        kx, kf, kb = jax.random.split(key, 3)
        inp = {'x': jax.random.normal(kx, (BN, M, D_MODEL), dtype=jnp.float32), 'ln_gamma': jnp.ones((D_MODEL,), jnp.float32), 'ln_beta': jnp.zeros((D_MODEL,), jnp.float32)}
        fp = _mamba_params(kf)
        bp = _mamba_params(kb)
        for n in PARAM_NAMES:
            inp['f_' + n] = fp[n]
            inp['b_' + n] = bp[n]
        return inp
    _L1_attn_all = _L1_attn_setup()
    _L1_attn_in = {k: v for k, v in _L1_attn_all.items() if k in ('ln_gamma', 'ln_beta', 'f_in_proj_w', 'f_conv_w', 'f_conv_b', 'f_x_proj_w', 'f_dt_proj_w', 'f_dt_proj_b', 'f_A_log', 'f_D', 'f_out_proj_w', 'b_in_proj_w', 'b_conv_w', 'b_conv_b', 'b_x_proj_w', 'b_dt_proj_w', 'b_dt_proj_b', 'b_A_log', 'b_D', 'b_out_proj_w')}
    del _L1_attn_all

    def _L1_ffn_setup():
        import jax, jax.numpy as jnp
        import numpy as np
        B, N, D = (16, 1024, 64)
        NUM_EXPERTS, TOP_K, HEADS = (4, 2, 4)
        N_EDGES = 262144
        LN_EPS = 1e-05

        def _layernorm(x, g, b):
            mu = x.mean(-1, keepdims=True)
            var = ((x - mu) ** 2).mean(-1, keepdims=True)
            return (x - mu) * jax.lax.rsqrt(var + LN_EPS) * g + b

        def _forward(x, edge_index, W_gat, att_src, att_dst, b_gat, ln_gamma, ln_beta, W1, b1, W2, b2):
            Bc, Nc, Dc = x.shape
            M = Bc * Nc
            x_flat = x.reshape(M, Dc)
            h = (x_flat @ W_gat).reshape(M, HEADS, NUM_EXPERTS)
            loops = jnp.arange(M, dtype=edge_index.dtype)
            src = jnp.concatenate([edge_index[0], loops])
            dst = jnp.concatenate([edge_index[1], loops])
            a_src = (h * att_src).sum(-1)
            a_dst = (h * att_dst).sum(-1)
            e = jax.nn.leaky_relu(a_src[src] + a_dst[dst], negative_slope=0.2)
            e_max = jax.ops.segment_max(e, dst, num_segments=M)
            ee = jnp.exp(e - e_max[dst])
            denom = jax.ops.segment_sum(ee, dst, num_segments=M)
            alpha = ee / (denom[dst] + 1e-16)
            msg = h[src] * alpha[:, :, None]
            agg = jax.ops.segment_sum(msg, dst, num_segments=M).reshape(M, HEADS * NUM_EXPERTS) + b_gat
            scores = _layernorm(agg, ln_gamma, ln_beta).reshape(M, HEADS, NUM_EXPERTS).mean(1)
            scores = scores.reshape(Bc, Nc, NUM_EXPERTS)
            topk_s, topk_i = jax.lax.top_k(scores, TOP_K)
            w = jax.nn.softmax(topk_s, axis=-1)
            out = jnp.zeros_like(x)
            for ei in range(NUM_EXPERTS):
                g = jnp.where(topk_i == ei, w, 0.0).sum(-1)
                hh = jax.nn.gelu(x @ W1[ei] + b1[ei], approximate=False)
                out = out + g[..., None] * (hh @ W2[ei] + b2[ei])
            return out
        key = jax.random.key(seed)
        ks = jax.random.split(key, 8)
        s = 0.05
        return {'x': jax.random.normal(ks[0], (B, N, D), jnp.float32), 'W_gat': jax.random.normal(ks[1], (D, HEADS * NUM_EXPERTS), jnp.float32) * s, 'att_src': jax.random.normal(ks[2], (HEADS, NUM_EXPERTS), jnp.float32) * s, 'att_dst': jax.random.normal(ks[3], (HEADS, NUM_EXPERTS), jnp.float32) * s, 'b_gat': jnp.zeros((HEADS * NUM_EXPERTS,), jnp.float32), 'ln_gamma': jnp.ones((HEADS * NUM_EXPERTS,), jnp.float32), 'ln_beta': jnp.zeros((HEADS * NUM_EXPERTS,), jnp.float32), 'W1': jax.random.normal(ks[4], (NUM_EXPERTS, D, 2 * D), jnp.float32) * s, 'b1': jnp.zeros((NUM_EXPERTS, 2 * D), jnp.float32), 'W2': jax.random.normal(ks[5], (NUM_EXPERTS, 2 * D, D), jnp.float32) * s, 'b2': jnp.zeros((NUM_EXPERTS, D), jnp.float32), 'edge_index': jax.random.randint(ks[6], (2, N_EDGES), 0, B * N, jnp.int32)}
    _L1_ffn_all = _L1_ffn_setup()
    _L1_ffn_in = {k: v for k, v in _L1_ffn_all.items() if k in ('W_gat', 'att_src', 'att_dst', 'b_gat', 'ln_gamma', 'ln_beta', 'W1', 'b1', 'W2', 'b2', 'edge_index')}
    del _L1_ffn_all
    return {'x': x, 'L0_conv_om_kernel': _L0_conv_in['om_kernel'], 'L0_conv_om_bias': _L0_conv_in['om_bias'], 'L0_conv_kernel': _L0_conv_in['kernel'], 'L0_conv_bias': _L0_conv_in['bias'], 'L1_attn_ln_gamma': _L1_attn_in['ln_gamma'], 'L1_attn_ln_beta': _L1_attn_in['ln_beta'], 'L1_attn_f_in_proj_w': _L1_attn_in['f_in_proj_w'], 'L1_attn_f_conv_w': _L1_attn_in['f_conv_w'], 'L1_attn_f_conv_b': _L1_attn_in['f_conv_b'], 'L1_attn_f_x_proj_w': _L1_attn_in['f_x_proj_w'], 'L1_attn_f_dt_proj_w': _L1_attn_in['f_dt_proj_w'], 'L1_attn_f_dt_proj_b': _L1_attn_in['f_dt_proj_b'], 'L1_attn_f_A_log': _L1_attn_in['f_A_log'], 'L1_attn_f_D': _L1_attn_in['f_D'], 'L1_attn_f_out_proj_w': _L1_attn_in['f_out_proj_w'], 'L1_attn_b_in_proj_w': _L1_attn_in['b_in_proj_w'], 'L1_attn_b_conv_w': _L1_attn_in['b_conv_w'], 'L1_attn_b_conv_b': _L1_attn_in['b_conv_b'], 'L1_attn_b_x_proj_w': _L1_attn_in['b_x_proj_w'], 'L1_attn_b_dt_proj_w': _L1_attn_in['b_dt_proj_w'], 'L1_attn_b_dt_proj_b': _L1_attn_in['b_dt_proj_b'], 'L1_attn_b_A_log': _L1_attn_in['b_A_log'], 'L1_attn_b_D': _L1_attn_in['b_D'], 'L1_attn_b_out_proj_w': _L1_attn_in['b_out_proj_w'], 'L1_ffn_W_gat': _L1_ffn_in['W_gat'], 'L1_ffn_att_src': _L1_ffn_in['att_src'], 'L1_ffn_att_dst': _L1_ffn_in['att_dst'], 'L1_ffn_b_gat': _L1_ffn_in['b_gat'], 'L1_ffn_ln_gamma': _L1_ffn_in['ln_gamma'], 'L1_ffn_ln_beta': _L1_ffn_in['ln_beta'], 'L1_ffn_W1': _L1_ffn_in['W1'], 'L1_ffn_b1': _L1_ffn_in['b1'], 'L1_ffn_W2': _L1_ffn_in['W2'], 'L1_ffn_b2': _L1_ffn_in['b2'], 'L1_ffn_edge_index': _L1_ffn_in['edge_index']}

def reference(x, L0_conv_om_kernel, L0_conv_om_bias, L0_conv_kernel, L0_conv_bias, L1_attn_ln_gamma, L1_attn_ln_beta, L1_attn_f_in_proj_w, L1_attn_f_conv_w, L1_attn_f_conv_b, L1_attn_f_x_proj_w, L1_attn_f_dt_proj_w, L1_attn_f_dt_proj_b, L1_attn_f_A_log, L1_attn_f_D, L1_attn_f_out_proj_w, L1_attn_b_in_proj_w, L1_attn_b_conv_w, L1_attn_b_conv_b, L1_attn_b_x_proj_w, L1_attn_b_dt_proj_w, L1_attn_b_dt_proj_b, L1_attn_b_A_log, L1_attn_b_D, L1_attn_b_out_proj_w, L1_ffn_W_gat, L1_ffn_att_src, L1_ffn_att_dst, L1_ffn_b_gat, L1_ffn_ln_gamma, L1_ffn_ln_beta, L1_ffn_W1, L1_ffn_b1, L1_ffn_W2, L1_ffn_b2, L1_ffn_edge_index):
    import jax
    import jax.numpy as jnp

    def _L0_conv_ref(inputs, om_kernel, om_bias, kernel, bias):
        import jax, jax.numpy as jnp
        import numpy as np
        from jax import lax
        K = 3
        PAD = 1
        STRIDE = 1
        DIL = 1
        OFFSET_SIZE = 2 * K * K

        def _dcnv2(x, om_kernel, om_bias, kernel, bias):
            B, H, W, C = x.shape
            om = lax.conv_general_dilated(x, om_kernel, window_strides=(STRIDE, STRIDE), padding=((PAD, PAD), (PAD, PAD)), rhs_dilation=(DIL, DIL), dimension_numbers=('NHWC', 'HWIO', 'NHWC')) + om_bias
            OH, OW = (om.shape[1], om.shape[2])
            KK = K * K
            offset = om[..., :OFFSET_SIZE].reshape(B, OH, OW, KK, 2)
            mask = jax.nn.sigmoid(om[..., OFFSET_SIZE:]) * 2.0
            kk = jnp.arange(KK)
            ky = (kk // K).astype(jnp.float32)
            kx = (kk % K).astype(jnp.float32)
            base_y = jnp.arange(OH, dtype=jnp.float32)[:, None] * STRIDE - PAD + ky[None, :] * DIL
            base_x = jnp.arange(OW, dtype=jnp.float32)[:, None] * STRIDE - PAD + kx[None, :] * DIL
            py = base_y[None, :, None, :] + offset[..., 0]
            px = base_x[None, None, :, :] + offset[..., 1]
            y0 = jnp.floor(py)
            x0 = jnp.floor(px)
            wy1 = py - y0
            wy0 = 1.0 - wy1
            wx1 = px - x0
            wx0 = 1.0 - wx1
            bi = jnp.arange(B)[:, None, None, None]

            def gather(yi, xi):
                valid = (yi >= 0) & (yi <= H - 1) & (xi >= 0) & (xi <= W - 1)
                yc = jnp.clip(yi, 0, H - 1).astype(jnp.int32)
                xc = jnp.clip(xi, 0, W - 1).astype(jnp.int32)
                v = x[bi, yc, xc]
                return v * valid[..., None].astype(x.dtype)
            y1 = y0 + 1.0
            x1 = x0 + 1.0
            cols = gather(y0, x0) * (wy0 * wx0)[..., None] + gather(y0, x1) * (wy0 * wx1)[..., None] + gather(y1, x0) * (wy1 * wx0)[..., None] + gather(y1, x1) * (wy1 * wx1)[..., None]
            cols = cols * mask[..., None]
            out = cols.reshape(B, OH, OW, KK * C) @ kernel
            return out + bias
        return _dcnv2(inputs, om_kernel, om_bias, kernel, bias)

    def _L1_attn_ref(x, ln_gamma, ln_beta, f_in_proj_w, f_conv_w, f_conv_b, f_x_proj_w, f_dt_proj_w, f_dt_proj_b, f_A_log, f_D, f_out_proj_w, b_in_proj_w, b_conv_w, b_conv_b, b_x_proj_w, b_dt_proj_w, b_dt_proj_b, b_A_log, b_D, b_out_proj_w):
        import jax, jax.numpy as jnp
        import numpy as np
        D_MODEL = 64
        D_STATE = 16
        D_CONV = 4
        D_INNER = 128
        DT_RANK = 16
        BN = 32
        M = 16
        PARAM_NAMES = ['in_proj_w', 'conv_w', 'conv_b', 'x_proj_w', 'dt_proj_w', 'dt_proj_b', 'A_log', 'D', 'out_proj_w']

        def _mamba(x, in_proj_w, conv_w, conv_b, x_proj_w, dt_proj_w, dt_proj_b, A_log, Dvec, out_proj_w):
            xz = x @ in_proj_w.T
            xs, z = jnp.split(xz, 2, axis=-1)
            xs_pad = jnp.pad(xs, ((0, 0), (D_CONV - 1, 0), (0, 0)))
            kern = jnp.transpose(conv_w, (2, 1, 0))
            xs = jax.lax.conv_general_dilated(xs_pad, kern, (1,), 'VALID', dimension_numbers=('NWC', 'WIO', 'NWC'), feature_group_count=D_INNER) + conv_b
            xs = jax.nn.silu(xs)
            dbc = xs @ x_proj_w.T
            dt = jax.nn.softplus(dbc[..., :DT_RANK] @ dt_proj_w.T + dt_proj_b)
            Bm = dbc[..., DT_RANK:DT_RANK + D_STATE]
            Cm = dbc[..., DT_RANK + D_STATE:]
            A = -jnp.exp(A_log)
            dA = jnp.exp(dt[..., None] * A)
            dBu = dt[..., None] * Bm[:, :, None, :] * xs[..., None]

            def combine(c1, c2):
                a1, b1 = c1
                a2, b2 = c2
                return (a1 * a2, a2 * b1 + b2)
            _, hs = jax.lax.associative_scan(combine, (dA, dBu), axis=1)
            y = jnp.einsum('blds,bls->bld', hs, Cm) + xs * Dvec
            y = y * jax.nn.silu(z)
            return y @ out_proj_w.T

        def _core(x, ln_gamma, ln_beta, fp, bp):
            mu = x.mean(-1, keepdims=True)
            var = x.var(-1, keepdims=True)
            xn = (x - mu) / jnp.sqrt(var + 1e-05) * ln_gamma + ln_beta
            y_fwd = _mamba(xn, *fp)
            y_bwd = jnp.flip(_mamba(jnp.flip(xn, 1), *bp), 1)
            return y_fwd + y_bwd + x

        def _mamba_params(key):
            ks = jax.random.split(key, 5)
            s = 0.02
            return {'in_proj_w': jax.random.normal(ks[0], (2 * D_INNER, D_MODEL)) * s, 'conv_w': jax.random.normal(ks[1], (D_INNER, 1, D_CONV)) * s, 'conv_b': jnp.zeros((D_INNER,)), 'x_proj_w': jax.random.normal(ks[2], (DT_RANK + 2 * D_STATE, D_INNER)) * s, 'dt_proj_w': jax.random.normal(ks[3], (D_INNER, DT_RANK)) * s, 'dt_proj_b': jnp.full((D_INNER,), -4.6), 'A_log': jnp.log(jnp.tile(jnp.arange(1, D_STATE + 1, dtype=jnp.float32), (D_INNER, 1))), 'D': jnp.ones((D_INNER,)), 'out_proj_w': jax.random.normal(ks[4], (D_MODEL, D_INNER)) * s}
        fp = (f_in_proj_w, f_conv_w, f_conv_b, f_x_proj_w, f_dt_proj_w, f_dt_proj_b, f_A_log, f_D, f_out_proj_w)
        bp = (b_in_proj_w, b_conv_w, b_conv_b, b_x_proj_w, b_dt_proj_w, b_dt_proj_b, b_A_log, b_D, b_out_proj_w)
        return _core(x, ln_gamma, ln_beta, fp, bp)

    def _L1_ffn_ref(x, W_gat, att_src, att_dst, b_gat, ln_gamma, ln_beta, W1, b1, W2, b2, edge_index):
        import jax, jax.numpy as jnp
        import numpy as np
        B, N, D = (16, 1024, 64)
        NUM_EXPERTS, TOP_K, HEADS = (4, 2, 4)
        N_EDGES = 262144
        LN_EPS = 1e-05

        def _layernorm(x, g, b):
            mu = x.mean(-1, keepdims=True)
            var = ((x - mu) ** 2).mean(-1, keepdims=True)
            return (x - mu) * jax.lax.rsqrt(var + LN_EPS) * g + b

        def _forward(x, edge_index, W_gat, att_src, att_dst, b_gat, ln_gamma, ln_beta, W1, b1, W2, b2):
            Bc, Nc, Dc = x.shape
            M = Bc * Nc
            x_flat = x.reshape(M, Dc)
            h = (x_flat @ W_gat).reshape(M, HEADS, NUM_EXPERTS)
            loops = jnp.arange(M, dtype=edge_index.dtype)
            src = jnp.concatenate([edge_index[0], loops])
            dst = jnp.concatenate([edge_index[1], loops])
            a_src = (h * att_src).sum(-1)
            a_dst = (h * att_dst).sum(-1)
            e = jax.nn.leaky_relu(a_src[src] + a_dst[dst], negative_slope=0.2)
            e_max = jax.ops.segment_max(e, dst, num_segments=M)
            ee = jnp.exp(e - e_max[dst])
            denom = jax.ops.segment_sum(ee, dst, num_segments=M)
            alpha = ee / (denom[dst] + 1e-16)
            msg = h[src] * alpha[:, :, None]
            agg = jax.ops.segment_sum(msg, dst, num_segments=M).reshape(M, HEADS * NUM_EXPERTS) + b_gat
            scores = _layernorm(agg, ln_gamma, ln_beta).reshape(M, HEADS, NUM_EXPERTS).mean(1)
            scores = scores.reshape(Bc, Nc, NUM_EXPERTS)
            topk_s, topk_i = jax.lax.top_k(scores, TOP_K)
            w = jax.nn.softmax(topk_s, axis=-1)
            out = jnp.zeros_like(x)
            for ei in range(NUM_EXPERTS):
                g = jnp.where(topk_i == ei, w, 0.0).sum(-1)
                hh = jax.nn.gelu(x @ W1[ei] + b1[ei], approximate=False)
                out = out + g[..., None] * (hh @ W2[ei] + b2[ei])
            return out
        return _forward(x, edge_index, W_gat, att_src, att_dst, b_gat, ln_gamma, ln_beta, W1, b1, W2, b2)

    def _gn(v, G=32, eps=1e-05):
        B_, H_, W_, C_ = v.shape
        g = v.reshape(B_, H_, W_, G, C_ // G)
        m = jnp.mean(g, axis=(1, 2, 4), keepdims=True)
        s = jnp.var(g, axis=(1, 2, 4), keepdims=True)
        return ((g - m) / jnp.sqrt(s + eps)).reshape(v.shape)

    def _ln_c(v, eps=1e-06):
        m = jnp.mean(v, axis=-1, keepdims=True)
        s = jnp.var(v, axis=-1, keepdims=True)
        return (v - m) / jnp.sqrt(s + eps)

    def _ln_t(v, eps=1e-05):
        m = jnp.mean(v, axis=-1, keepdims=True)
        s = jnp.var(v, axis=-1, keepdims=True)
        return (v - m) / jnp.sqrt(s + eps)

    def _to_tokens(v):
        B_, H_, W_, C_ = v.shape
        return v.reshape(B_, H_ * W_, C_)

    def _from_tokens(t, like):
        return t.reshape(like.shape)
    x = x + _L0_conv_ref(_gn(x), L0_conv_om_kernel, L0_conv_om_bias, L0_conv_kernel, L0_conv_bias)
    t = _to_tokens(x)
    t = t + _L1_attn_ref(_ln_t(t), L1_attn_ln_gamma, L1_attn_ln_beta, L1_attn_f_in_proj_w, L1_attn_f_conv_w, L1_attn_f_conv_b, L1_attn_f_x_proj_w, L1_attn_f_dt_proj_w, L1_attn_f_dt_proj_b, L1_attn_f_A_log, L1_attn_f_D, L1_attn_f_out_proj_w, L1_attn_b_in_proj_w, L1_attn_b_conv_w, L1_attn_b_conv_b, L1_attn_b_x_proj_w, L1_attn_b_dt_proj_w, L1_attn_b_dt_proj_b, L1_attn_b_A_log, L1_attn_b_D, L1_attn_b_out_proj_w)
    t = t + _L1_ffn_ref(_ln_t(t), L1_ffn_W_gat, L1_ffn_att_src, L1_ffn_att_dst, L1_ffn_b_gat, L1_ffn_ln_gamma, L1_ffn_ln_beta, L1_ffn_W1, L1_ffn_b1, L1_ffn_W2, L1_ffn_b2, L1_ffn_edge_index)
    x = _from_tokens(t, x)
    return x

_drawn_inputs = setup_inputs


def setup_inputs(seed=0):
    import zlib

    import numpy as np

    out = dict(_drawn_inputs(seed))
    spreads = {'L0_conv_om_bias': (0.0, 0.1),
     'L1_attn_ln_gamma': (1.0, 0.6),
     'L1_attn_ln_beta': (0.0, 0.8),
     'L1_attn_f_conv_b': (0.0, 0.8),
     'L1_attn_f_dt_proj_b': (-4.599999904632568, 0.6),
     'L1_attn_f_D': (1.0, 0.6),
     'L1_attn_b_conv_b': (0.0, 0.8),
     'L1_attn_b_dt_proj_b': (-4.599999904632568, 0.6),
     'L1_attn_b_D': (1.0, 0.6),
     'L1_ffn_b_gat': (0.0, 2.0),
     'L1_ffn_ln_gamma': (1.0, 0.6),
     'L1_ffn_ln_beta': (0.0, 2.0),
     'L1_ffn_b1': (0.0, 0.692),
     'L1_ffn_b2': (0.0, 0.301)}
    factors = {'L0_conv_bias': 4.959,
     'L1_attn_f_in_proj_w': 8.0,
     'L1_attn_f_conv_w': 8.0,
     'L1_attn_f_x_proj_w': 8.0,
     'L1_attn_f_dt_proj_w': 8.0,
     'L1_attn_f_A_log': 8.0,
     'L1_attn_f_out_proj_w': 8.0,
     'L1_attn_b_in_proj_w': 8.0,
     'L1_attn_b_conv_w': 8.0,
     'L1_attn_b_x_proj_w': 8.0,
     'L1_attn_b_dt_proj_w': 8.0,
     'L1_attn_b_A_log': 8.0,
     'L1_attn_b_out_proj_w': 8.0,
     'L1_ffn_att_src': 200.0,
     'L1_ffn_att_dst': 200.0,
     'L1_ffn_W_gat': 10.337}
    for name, (base, spread) in spreads.items():
        noise = np.random.default_rng([zlib.crc32(name.encode()), seed]).standard_normal(out[name].shape)
        drawn = base * np.exp(spread * noise) if base else spread * noise
        out[name] = jnp.asarray(drawn.astype(out[name].dtype))
    for name, factor in factors.items():
        out[name] = (out[name] * factor).astype(out[name].dtype)
    return out
```

```python
from contextlib import ExitStack

import concourse.bass as bass
from concourse import mybir

P = 128
BATCH, HEIGHT, WIDTH, C = 8, 16, 16, 64
SEQ = HEIGHT * WIDTH
T = BATCH * SEQ
NT = T // P
K2 = 9
OM = 3 * K2
GROUPS = 32
DI, DS, DTR, TAPS = 128, 16, 16, 4
SEQP = SEQ + 2 * (TAPS - 1)
HALF = T // 2
EDGES = 262144
EPP = EDGES // P
LAST = T - 1
HI, LO = 32, 64
HCH = 296
CHUNKS = [(e, min(HCH, EPP - e)) for e in range(0, EPP, HCH)]
CAP = 56
W = 56
ROUNDS = CAP // 8
NPO = T // P
HEADS, EXP = 4, 4
HE = HEADS * EXP
ROW = HE + HEADS
HID = 2 * C
LW = 32
BIG = 1.0e30
LEFT_COLUMN = 8 + (P // LW) * 33
LEFT_ROUND = 2 + 8 * LEFT_COLUMN

F32 = mybir.dt.float32
BF16 = mybir.dt.bfloat16
I32 = mybir.dt.int32
ALU = mybir.AluOpType
ACT = mybir.ActivationFunctionType
AX = mybir.AxisListType.X


class Link:

    def __init__(self, eng, sem):
        self.eng, self.sem, self.n = eng, sem, 0

    def __call__(self, ins):
        self.go(ins)
        self.wait()

    def go(self, ins):
        self.n += 1
        ins.then_inc(self.sem, 1)

    def wait(self):
        self.eng.wait_ge(self.sem, self.n)


def program(nc, a, out):
    with ExitStack() as ctx:
        def sb(name, shape, dt=F32):
            return ctx.enter_context(nc.sbuf_tensor(name, shape, dt))

        def sem(name):
            return ctx.enter_context(nc.semaphore(name))

        ps = ctx.enter_context(nc.psum_tensor("ps", [P, 8, 512], F32))

        def banks(lo, n, parts=P):
            return ps[0:parts, lo:lo + n, :].rearrange("p b n -> p (b n)")

        class Arena:

            def __init__(self, name, words):
                self.mem, self.words, self.top = sb(name, [P, words]), words, 0

            def __call__(self, n, dt=F32, parts=P):
                lo, words = self.top, n if dt != BF16 else (n + 1) // 2
                self.top += words
                assert self.top <= self.words, self.top
                v = self.mem[0:parts, lo:lo + words]
                return v if dt == F32 else v.bitcast(dt)

        ident = sb("ident", [P, P])
        ones_f = sb("ones_f", [1, P])
        iota_pi = sb("iota_pi", [P, 1], I32)
        pi_tmp = sb("pi_tmp", [P, 2], I32)
        ph = sb("ph", [P, 1])
        pl = sb("pl", [P, 1])
        pf = sb("pf", [P, 1])
        iota_y = sb("iota_y", [P, 2, K2 * HEIGHT])
        iota_x = sb("iota_x", [P, K2, WIDTH])
        pairmat = sb("pairmat", [C, C])
        iota_n = sb("iota_n", [P, P], BF16)
        tri = sb("tri", [P, P], BF16)
        sel = sb("sel", [96, 32], BF16)
        iota_j = sb("iota_j", [P, NPO])
        tiebreak = sb("tiebreak", [P, EXP, EXP])
        w_om = sb("w_om", [C, K2, OM])
        b_om = sb("b_om", [1, OM])
        w_cv = sb("w_cv", [C, K2, C])
        b_cv = sb("b_cv", [1, C])
        in_w = [sb(f"in_w{d}", [C, 2 * DI]) for d in range(2)]
        w_tap = [sb(f"w_tap{d}", [C, TAPS, DI]) for d in range(2)]
        vec = [sb(f"vec{d}", [P, 3]) for d in range(2)]
        xp_w = [sb(f"xp_w{d}", [P, 96]) for d in range(2)]
        xd_w = [sb(f"xd_w{d}", [P, DTR]) for d in range(2)]
        dp_w = [sb(f"dp_w{d}", [DTR, DI]) for d in range(2)]
        neg_a = [sb(f"neg_a{d}", [P, DS]) for d in range(2)]
        diag_d = [sb(f"diag_d{d}", [P, P]) for d in range(2)]
        o_w = [sb(f"o_w{d}", [P, C]) for d in range(2)]
        gb = sb("gb", [C, 2])
        w_gat = sb("w_gat", [C, HE])
        att = sb("att", [P, 2, HE])
        rows16 = sb("rows16", [P, 3, HE])
        w1 = sb("w1", [C, EXP, HID])
        b1 = sb("b1", [HID, EXP])
        w2 = sb("w2", [HID, EXP, C])
        b2 = sb("b2", [1, EXP * C])
        x_tok = sb("x_tok", [P, NT, C])
        st6 = sb("st6", [C, BATCH, 6])
        mv = sb("mv", [C, BATCH, 2])
        ms = sb("ms", [C, BATCH, 2])
        gnm = sb("gnm", [C, BATCH, 2])
        gnv = sb("gnv", [C, 2, BATCH])
        om = sb("om", [P, NT, OM])
        msk = sb("msk", [P, NT, K2])
        lns = sb("lns", [P, 6, NT])
        keys = sb("keys", [P, EPP + CAP])
        comp = keys[:, EPP:EPP + CAP]
        hi_b = sb("hi_b", [P, EPP], BF16)
        lo_b = sb("lo_b", [P, EPP], BF16)
        key_i = sb("key_i", [P, CAP], I32)
        int_a = sb("int_a", [P, 3, CAP], I32)
        owner = sb("owner", [P, CAP])
        same = sb("same", [P, CAP])
        run = sb("run", [P, CAP])
        slot = sb("slot", [P, CAP])
        dig = sb("dig", [P, 2, CAP])
        base_b = sb("base_b", [P, P], BF16)
        ell = sb("ell", [P, 2, W])
        ell_i = sb("ell_i", [P, 3, W], I32)
        src_idx = sb("src_idx", [P, W], I32)
        jslot = sb("jslot", [P, 2, W])
        pen = sb("pen", [P, NPO, W])
        hist_s = sb("hist_s", [P, LO])
        cnt4 = sb("cnt4", [P, 4, NPO])
        cnt = sb("cnt", [P, NPO])
        nleft = sb("nleft", [P, 2])
        nleft_i = sb("nleft_i", [1, 2], I32)

        hrow = sb("hrow", [P, NPO, ROW])
        adst = sb("adst", [P, HEADS, NPO])
        atmp = sb("atmp", [P, NPO, HE])
        last = sb("last", [P, ROW])
        amax = sb("amax", [P, HEADS, NPO])
        mx = sb("mx", [P, HEADS, NPO])
        mcur = sb("mcur", [P, HEADS, NPO])
        den = sb("den", [P, HEADS, NPO])
        acc = sb("acc", [P, HEADS, EXP, NPO])
        g1 = sb("g1", [P, HEADS, NPO])
        g2 = sb("g2", [P, HEADS, NPO])
        g4 = sb("g4", [P, HEADS, EXP, NPO])
        agg = sb("agg", [P, NPO, HE])
        gs = sb("gs", [P, 6, NPO])
        sc = sb("sc", [P, NPO, EXP])
        gate = sb("gate", [P, NPO, EXP])
        pause = sb("pause", [P, 4])
        left_row = sb("left_row", [P, ROW + 1])
        left_idx = sb("left_idx", [P, 2], I32)
        m8 = sb("m8", [P, 8])

        ar = Arena("arena", 26800)
        one_hi = ar(HI * HCH, BF16).rearrange("p (v e) -> p v e", v=HI)
        one_lo = ar(LO * HCH, BF16).rearrange("p (v e) -> p v e", v=LO)
        s_buf = ar(K2 * SEQ).rearrange("p (k y x) -> p k y x", k=K2, x=WIDTH)
        s_rows = s_buf.rearrange("p k y x -> p k (y x)")
        s_t = [ar(2 * K2 * P).rearrange("p (n q) -> p n q", n=2 * K2) for _ in range(2)]
        xk = [ar(2 * K2 * C).rearrange("p (t n) -> p t n", t=2) for _ in range(2)]
        wy = ar(NT * K2 * HEIGHT).rearrange("p (t k y) -> p t k y", t=NT, k=K2)
        ar.top = 0
        src_i = ar(EPP, I32)
        dst_i = ar(EPP, I32)
        e_tmp = ar(EPP)
        e_tm2 = ar(EPP)
        e_int = ar(EPP, I32)
        cw_b = [ar(TAPS * DI, parts=C).rearrange("p (k c) -> p k c", k=TAPS) for _ in range(2)]
        ar.top = 0
        xnt = ar(BATCH * SEQP, parts=C).rearrange("p (b s) -> p b s", b=BATCH)
        x0_at = ar.top
        xs, zs, dtv, uu = ([ar(T)] for _ in range(4))
        bc3 = [ar(T, BF16) for _ in range(2)]
        loop_at = ar.top
        da = [ar(HALF) for _ in range(2)]
        hh = [ar(HALF) for _ in range(2)]
        gg = [ar(HALF) for _ in range(2)]
        x1_at = ar.top
        for x in (xs, zs, dtv, uu):
            x.append(ar(T))
        ar.top = loop_at
        dtr = ar(T, parts=DTR)
        r1 = ar(T, parts=64)
        sp_t = ar(T)
        ar.top = loop_at
        sp_c = ar(T)
        ar.top = x0_at
        lnd, lsq, un, xn = (ar(NT * C).rearrange("p (t c) -> p t c", t=NT) for _ in range(4))
        ar.top = x1_at
        look = ar(CAP * P, BF16).rearrange("p (c q) -> p c q", c=CAP)
        slot1 = ar(CAP * W, BF16).rearrange("p (c w) -> p c w", c=CAP)
        pay = ar(CAP * 2 * W, BF16).rearrange("p (c h w) -> p c h w", c=CAP, h=2)
        key_tmp = look.rearrange("p c q -> p (c q)")[:, 0:EPP + CAP]
        ar.top = 0
        vt = ar(T, parts=C)
        v_tok, d_tok = (ar(NT * C).rearrange("p (t c) -> p t c", t=NT) for _ in range(2))
        assert ar.top <= x0_at + T
        ar.top = x0_at + 2 * T
        a_e, b_e = (ar(HEADS * NPO * W).rearrange("p (h j w) -> p h j w", h=HEADS, j=NPO) for _ in range(2))
        hid = [ar(HID * 4) for _ in range(2)]
        eo = ar(NPO * EXP * C).rearrange("p (j e c) -> p j e c", j=NPO, e=EXP)
        assert ar.top <= x1_at
        left_p = b_e.rearrange("p h j w -> p (h j w)")[:, 0:EXP * NPO * LW].rearrange("p (x j w) -> p x j w", x=EXP, j=NPO)
        ar.top = x1_at
        left_w = ar(HEADS * NPO * LW).rearrange("p (h j w) -> p h j w", h=HEADS, j=NPO)
        assert ar.top <= x1_at + T
        ar.top = x1_at + 2 * T
        left_all = ar(P * (ROW + 1)).rearrange("p (e r) -> p e r", e=P)
        lk = ar(2 * P, I32).rearrange("p (a e) -> p a e", a=2)
        lkf = ar(2 * P).rearrange("p (a e) -> p a e", a=2)
        left_pen = ar(NPO * LW).rearrange("p (j w) -> p j w", j=NPO)
        cmp1, cmp2 = (ar(NPO * EXP * EXP).rearrange("p (j a b) -> p j a b", j=NPO, a=EXP) for _ in range(2))
        br = Arena("arena2", 9216)
        xpad = br(3 * BATCH * (HEIGHT + 2) * WIDTH, parts=C).rearrange("p (s b y x) -> p s b y x", s=3, b=BATCH, x=WIDTH)
        wx = br(NT * K2 * WIDTH).rearrange("p (t k x) -> p t k x", t=NT, k=K2)
        br.top = 0
        own1 = br(CAP * P, BF16).rearrange("p (c q) -> p c q", c=CAP)
        resb = br(NPO * C).rearrange("p (j c) -> p j c", j=NPO)
        nb = br(W * ROW).rearrange("p (w r) -> p w r", w=W)
        t2 = br(NPO * C).rearrange("p (j c) -> p j c", j=NPO)
        res_d = nc.dram_tensor("res_scratch", [T, C], F32).ap()
        tab_d = nc.dram_tensor("node_rows", [T, ROW], F32).ap()
        cnt_d = nc.dram_tensor("hist_scratch", [4, T], F32).ap()
        left_d = nc.dram_tensor("left_scratch", [1, P * (ROW + 1)], F32).ap()

        names = """x_in edge_in wconv_in gb_in wmamba_in cw_in wffn_in att_in pool_step const_ready dve_step act_step
            xt_ready stats_ready pair_ready var_ready std_ready xhat_ready om_ready off_ready abs_step
            hat_ready sig_ready wx_ready s_ready st_psum st_ready xk_psum xk_ready conv_out t1_ready
            onehot_ready onehot_used hist_ready hist_out hist_back
            ln_var ln_std res_ready res_out res_back xn_ready xnt_psum xnt_ready taps_ready
            xs_psum xs_ready z_psum z_ready dbc_psum hi_ready dtr_ready rest_ready mid_ready bc_ready dt_psum
            sp_lin sp_step sp_ln dt_ready dt_free nega_ready diag_ready
            own_ready base_psum pay_ready ell_psum idx_ready left_psum left_count left_known
            b_psum b_used c_psum c_used da_ready da_used g_ready g_used y_psum y_used da_zero yg_ready
            t2_psum t2_ready v_ready vt_psum vt_ready h_psum h_ready tab_out last_in nb_in e_in exp_ready
            hid_psum hid_ready hid_used eo_psum eo_read gate_ready
            left_step left_idx_ready left_row_in left_key left_out left_in left_e left_exp out_ready out_done""".split()
        s = {n: sem(n) for n in names}
        block = ctx.enter_context(nc.Block())
        PRE = ("f_", "b_")
        edge_v = a["edges"].rearrange("r (p e) -> r p e", p=P)

        @block.sync
        def _(sp):
            sp.dma_start(x_tok[:], a["x"].rearrange("(t p) c -> p t c", p=P)).then_inc(s["x_in"], 16)
            sp.dma_start(w_om[:], a["om_kernel"].rearrange("k c n -> c k n")).then_inc(s["wconv_in"], 16)
            sp.dma_start(b_om[:], a["om_bias"]).then_inc(s["wconv_in"], 16)
            sp.dma_start(w_cv[:], a["kernel"].rearrange("(k c) n -> c k n", c=C)).then_inc(s["wconv_in"], 16)
            sp.dma_start(b_cv[:], a["bias"]).then_inc(s["wconv_in"], 16)
            sp.dma_start(src_i, edge_v[0]).then_inc(s["edge_in"], 16)
            sp.dma_start(dst_i, edge_v[1]).then_inc(s["edge_in"], 16)
            for d, pre in enumerate(PRE):
                sp.dma_start(cw_b[d], a[pre + "conv_w"].to_broadcast([C, TAPS * DI])
                             .rearrange("p (k c) -> p k c", k=TAPS)).then_inc(s["cw_in"], 16)
                sp.dma_start(in_w[d][:], a[pre + "in_w"]).then_inc(s["cw_in"], 16)
            for d, pre in enumerate(PRE):
                sp.dma_start(vec[d][:], a[pre + "vec"]).then_inc(s["wmamba_in"], 16)
                sp.dma_start(xd_w[d][:], a[pre + "xp_w"][:, 0:DTR]).then_inc(s["wmamba_in"], 16)
                for r in range(3):
                    sp.dma_start(xp_w[d][:, 32 * r:32 * r + 32], a[pre + "xp_w"][:, DTR:DTR + 2 * DS]).then_inc(s["wmamba_in"], 16)
                sp.dma_start(dp_w[d][:], a[pre + "dp_w"]).then_inc(s["wmamba_in"], 16)
                sp.dma_start(neg_a[d][:], a[pre + "a_log"]).then_inc(s["wmamba_in"], 16)
                sp.dma_start(o_w[d][:], a[pre + "o_w"]).then_inc(s["wmamba_in"], 16)
            sp.dma_start(gb[:], a["ln_gb"]).then_inc(s["gb_in"], 16)
            sp.dma_start(w_gat[:], a["w_gat"]).then_inc(s["wffn_in"], 16)
            sp.dma_start(w1[:], a["w1"].rearrange("e c n -> c e n")).then_inc(s["wffn_in"], 16)
            sp.dma_start(b1[:], a["b1"]).then_inc(s["wffn_in"], 16)
            sp.dma_start(w2[:], a["w2"].rearrange("e h n -> h e n")).then_inc(s["wffn_in"], 16)
            sp.dma_start(b2[:], a["b2"]).then_inc(s["wffn_in"], 16)
            sp.dma_start(att[:].rearrange("p a n -> p (a n)"), a["att"].to_broadcast([P, 2 * HE])).then_inc(s["att_in"], 16)
            sp.dma_start(rows16[:].rearrange("p a n -> p (a n)"), a["rows16"].to_broadcast([P, 3 * HE])).then_inc(s["att_in"], 16)

            sp.wait_ge(s["hist_ready"], 1)
            sp.dma_start(cnt_d.rearrange("g (h l) -> (g h) l", l=LO), hist_s[:]).then_inc(s["hist_out"], 16)
            sp.wait_ge(s["hist_out"], 16)
            sp.dma_start(cnt4[:], cnt_d.rearrange("g (p j) -> p g j", p=P)).then_inc(s["hist_back"], 16)
            sp.wait_ge(s["res_ready"], 1)
            sp.dma_start(res_d.rearrange("(t p) c -> p t c", p=P), x_tok[:]).then_inc(s["res_out"], 16)
            sp.wait_ge(s["res_out"], 16)
            sp.wait_ge(s["t1_ready"], NT)
            sp.dma_start(resb, res_d.rearrange("(p j) c -> p j c", p=P)).then_inc(s["res_back"], 16)
            sp.wait_ge(s["h_ready"], 1)
            sp.dma_start(tab_d.rearrange("(p j) r -> p j r", p=P), hrow[:]).then_inc(s["tab_out"], 16)
            sp.wait_ge(s["tab_out"], 16)
            sp.dma_start(last[:], tab_d[LAST:T, :].to_broadcast([P, ROW])).then_inc(s["last_in"], 16)
            sp.wait_ge(s["out_ready"], 1)
            sp.dma_start(out.rearrange("(p j) c -> p j c", p=P), t2).then_inc(s["out_done"], 16)
            sp.wait_ge(s["out_done"], 16)

        @block.gpsimd
        def _(g):
            k = Link(g, s["pool_step"])
            k(g.memset(ident[:], 0.0))
            k(g.affine_select(out=ident[:], in_=ident[:], compare_op=ALU.not_equal, fill=1.0, base=0,
                              pattern=[[-1, P]], channel_multiplier=1))
            k(g.memset(ones_f[:], 1.0))
            k(g.memset(pairmat[:], 0.5))
            pv = pairmat[:].rearrange("p (g two) -> p g two", two=2)
            k(g.affine_select(out=pv, in_=pv, compare_op=ALU.is_ge, fill=0.0, base=0,
                              pattern=[[-2, GROUPS], [0, 2]], channel_multiplier=1))
            k(g.affine_select(out=pv, in_=pv, compare_op=ALU.is_ge, fill=0.0, base=1,
                              pattern=[[2, GROUPS], [0, 2]], channel_multiplier=-1))
            k(g.memset(xpad, 0.0))
            k(g.iota(iota_pi[:], pattern=[[0, 1]], base=0, channel_multiplier=1))
            for i2 in range(2):
                k(g.iota(iota_y[:, i2, :], pattern=[[1, 3], [0, 3], [-1, HEIGHT]], base=8 * i2 - 1, channel_multiplier=0,
                         allow_small_or_imprecise_dtypes=True))
            k(g.iota(iota_x[:], pattern=[[0, 3], [1, 3], [-1, WIDTH]], base=-1, channel_multiplier=0,
                     allow_small_or_imprecise_dtypes=True))
            k(g.iota(iota_n[:], pattern=[[1, P]], base=0, channel_multiplier=0, allow_small_or_imprecise_dtypes=True))
            k(g.iota(iota_j[:], pattern=[[1, NPO]], base=0, channel_multiplier=0, allow_small_or_imprecise_dtypes=True))
            k(g.memset(tri[:], 1.0))
            k(g.affine_select(out=tri[:], in_=tri[:], compare_op=ALU.is_gt, fill=0.0, base=0,
                              pattern=[[1, P]], channel_multiplier=-1))
            k(g.memset(sel[:], 0.0))
            for part in range(3):
                k(g.affine_select(out=sel[:], in_=sel[:], compare_op=ALU.not_equal, fill=1.0, base=-32 * part,
                                  pattern=[[-1, 32]], channel_multiplier=1))
            k(g.memset(tiebreak[:], 1.0))
            g.affine_select(out=tiebreak[:], in_=tiebreak[:], compare_op=ALU.is_gt, fill=0.0, base=0,
                            pattern=[[1, EXP], [-1, EXP]], channel_multiplier=0).then_inc(s["const_ready"], 1)

            g.wait_ge(s["tab_out"], 16)
            g.wait_ge(s["idx_ready"], 1)
            for w in range(W):
                g.indirect_dma_start(out=nb[:, w, :], out_offset=None, in_=tab_d,
                                     in_offset=bass.IndirectOffsetOnAxis(ap=src_idx[:, w:w + 1], axis=0)).then_inc(s["nb_in"], 16)
            g.wait_ge(s["left_known"], 1)
            rounds = g.value_load(nleft_i[0:1, 0:1], min_val=0, max_val=EPP)
            with g.If(rounds > 0):
                with g.Fori(0, rounds) as r:
                    with g.Fori(0, 8) as c:
                        n = r * 8 + c
                        g.wait_ge(s["left_idx_ready"], n + 1)
                        g.tensor_tensor(pause[:, 0:1], pause[:, 2:3], pause[:, 2:3], ALU.add)
                        g.indirect_dma_start(out=left_row[:, 0:ROW], out_offset=None, in_=tab_d,
                                             in_offset=bass.IndirectOffsetOnAxis(ap=left_idx[:, 0:1], axis=0)).then_inc(s["left_row_in"], 16)
                        g.wait_ge(s["left_row_in"], n * 16 + 16)
                        g.tensor_tensor(pause[:, 0:1], pause[:, 2:3], pause[:, 2:3], ALU.add)
                        g.dma_start(left_d.rearrange("o (p r) -> (o p) r", p=P), left_row[:]).then_inc(s["left_out"], 16)
                        g.wait_ge(s["left_out"], n * 16 + 16)
                        g.tensor_tensor(pause[:, 0:1], pause[:, 2:3], pause[:, 2:3], ALU.add)
                        g.dma_start(left_all.rearrange("p e r -> p (e r)"), left_d.to_broadcast([P, P * (ROW + 1)])).then_inc(s["left_in"], 16)
                        g.wait_ge(s["left_in"], n * 16 + 16)

        @block.tensor
        def _(pe):
            pe.wait_ge(s["const_ready"], 1)
            pe.wait_ge(s["x_in"], 16)
            for i in range(NT):
                m = pe.transpose(ps[0:C, i // 4, (i % 4) * P:(i % 4) * P + P], x_tok[:, i, :], ident[:])
            m.then_inc(s["xt_ready"], 1)
            pe.wait_ge(s["stats_ready"], 1)
            pe.matmul(ps[0:C, 4, 0:2 * BATCH], pairmat[:], ms[:].rearrange("p b s -> p (b s)"), start=True, stop=True).then_inc(s["pair_ready"], 1)
            pe.wait_ge(s["wconv_in"], 64)
            pe.wait_ge(s["xhat_ready"], BATCH)
            for i in range(NT):
                b, r0 = i // 2, (i % 2) * 8
                o = ps[:, 5, OM * i:OM * i + OM]
                for t in range(K2):
                    ky, kx = t // 3, t % 3
                    pe.matmul(o, xpad[:, kx, b, r0 + ky:r0 + ky + 8, :].rearrange("p y x -> p (y x)"), w_om[:, t, :], start=(t == 0), stop=False)
                m = pe.matmul(o, ones_f[:], b_om[:], start=False, stop=True)
            m.then_inc(s["om_ready"], 1)

            def xk_part(b):
                for tau in range(2):
                    for hf in range(2):
                        n = 4 * b + 2 * tau + hf
                        if n >= 1:
                            pe.wait_ge(s["xk_ready"], n)
                        pe.matmul(ps[:, 7, 0:288], xpad[:, 1, b, 1 + 8 * tau:9 + 8 * tau, :].rearrange("p y x -> p (y x)"),
                                  w_cv[:].rearrange("p k n -> p (k n)")[:, 288 * hf:288 * hf + 288], start=True, stop=True).then_inc(s["xk_psum"], 1)

            def conv_tail(i):
                b = i // 2
                pe.wait_ge(s["st_ready"], 3 * i + 3)
                pe.wait_ge(s["xk_ready"], 4 * b + 4)
                if i >= 2:
                    pe.wait_ge(s["t1_ready"], i - 1)
                o = ps[:, 5 + i % 2, 0:C]
                pe.matmul(o, ones_f[:], b_cv[:], start=True, stop=False)
                for t in range(K2):
                    for tau in range(2):
                        m = pe.matmul(o, s_t[i % 2][:, 2 * t + tau, :], xk[b % 2][:, tau, C * t:C * t + C],
                                      start=False, stop=(t == K2 - 1 and tau == 1))
                m.then_inc(s["conv_out"], 1)

            def hist_chunk(ch):
                pe.wait_ge(s["onehot_ready"], ch + 1)
                for e in range(0, CHUNKS[ch][1], 4):
                    for q in range(4):
                        m = pe.matmul(ps[32 * q:32 * q + 32, 4, 0:LO], one_hi[:, :, e + q], one_lo[:, :, e + q],
                                      start=(ch == 0 and e == 0), stop=(ch == len(CHUNKS) - 1 and e == CHUNKS[ch][1] - 4),
                                      tile_position=(0, 32 * q))
                m.then_inc(s["onehot_used"], 1)

            for i in range(NT):
                if i % 2 == 0:
                    xk_part(i // 2)
                pe.wait_ge(s["s_ready"], i + 1)
                for q in range(3):
                    n = 3 * i + q
                    if n >= 2:
                        pe.wait_ge(s["st_ready"], n - 1)
                    for v in range(6):
                        t = 6 * q + v
                        m = pe.transpose(ps[:, 2 * (n % 2) + v // 4, (v % 4) * P:(v % 4) * P + P],
                                         s_rows[:, t // 2, (t % 2) * P:(t % 2) * P + P], ident[:])
                    m.then_inc(s["st_psum"], 1)
                if i:
                    conv_tail(i - 1)
                if i % 2 and i // 2 < len(CHUNKS):
                    hist_chunk(i // 2)
            conv_tail(NT - 1)

            pe.wait_ge(s["xn_ready"], 1)
            for i in range(NT):
                m = pe.transpose(ps[0:C, i // 4, (i % 4) * P:(i % 4) * P + P], xn[:, i, :], ident[:])
            m.then_inc(s["xnt_psum"], 1)
            pe.wait_ge(s["own_ready"], 1)
            for c in range(CAP):
                m = pe.matmul(ps[:, 5, 0:P], tri[:], own1[:, c, :], start=(c == 0), stop=(c == CAP - 1))
            m.then_inc(s["base_psum"], 1)
            pe.wait_ge(s["pay_ready"], 1)
            for c in range(CAP):
                m = pe.matmul(ps[:, 6, 0:2 * W], own1[:, c, :], pay[:, c, :, :].rearrange("p h w -> p (h w)"),
                              start=(c == 0), stop=(c == CAP - 1))
            m.then_inc(s["ell_psum"], 1)
            pe.wait_ge(s["left_count"], 1)
            pe.transpose(ps[0:1, 7, 0:P], nleft[:, 0:1], ident[:]).then_inc(s["left_psum"], 1)

            pe.wait_ge(s["xnt_ready"], 1)
            pe.wait_ge(s["taps_ready"], 2)
            pe.wait_ge(s["left_known"], 1)
            for d in range(2):
                if d:
                    pe.wait_ge(s["left_known"], 1)
                    pe.wait_ge(s["hi_ready"], d)
                    pe.wait_ge(s["rest_ready"], d)
                for q in range(4):
                    for t in range(TAPS):
                        shift = t if d == 0 else 2 * (TAPS - 1) - t
                        m = pe.matmul(ps[:, q, :], w_tap[d][:, t, :], xnt[:, 2 * q:2 * q + 2, shift:shift + SEQ],
                                      start=(t == 0), stop=(t == TAPS - 1))
                m.then_inc(s["xs_psum"], 1)
                if d:
                    pe.wait_ge(s["sp_lin"], 2 * d)
                else:
                    pe.wait_ge(s["idx_ready"], 1)
                for q in range(4):
                    m = pe.matmul(ps[:, 4 + q, :], in_w[d][:, DI:2 * DI], xnt[:, 2 * q:2 * q + 2, TAPS - 1:TAPS - 1 + SEQ],
                                  start=True, stop=True)
                m.then_inc(s["z_psum"], 1)
                pe.wait_ge(s["xs_ready"], d + 1)
                for q in range(4):
                    m = pe.matmul(ps[0:96, q, :], xp_w[d][:], xs[d][:, 512 * q:512 * q + 512], start=True, stop=True)
                pe.wait_ge(s["z_ready"], d + 1)
                for q in range(4):
                    m = pe.matmul(ps[0:DTR, 4 + q, :], xd_w[d][:], xs[d][:, 512 * q:512 * q + 512], start=True, stop=True)
                m.then_inc(s["dbc_psum"], 1)
                pe.wait_ge(s["dtr_ready"], d + 1)
                for q in range(4):
                    m = pe.matmul(ps[:, 4 + q, :], dp_w[d][:], dtr[:, 512 * q:512 * q + 512], start=True, stop=True)
                m.then_inc(s["dt_psum"], 1)

            pe.wait_ge(s["sp_lin"], 4)
            pe.wait_ge(s["rest_ready"], 2)
            pe.wait_ge(s["diag_ready"], 2)
            for d in range(2):
                pe.wait_ge(s["bc_ready"], d + 1)
                for hf in range(2):
                    blk, c0 = 2 * d + hf, hf * HALF
                    if blk:
                        pe.wait_ge(s["yg_ready"], blk)
                    for q in range(2):
                        pe.matmul(ps[:, 4 + q, :], diag_d[d][:], xs[d][:, c0 + 512 * q:c0 + 512 * q + 512], start=True, stop=True)
                    with pe.Fori(0, DS // 2) as it:
                        for e in range(2):
                            n = it * 2 + (16 * blk + e)
                            pe.wait_ge(s["b_used"], n + 1)
                            for q in range(2):
                                m = pe.matmul(ps[:, q, :], sel[:, bass.ds(it * 2 + e, 1)].to_broadcast([96, P]),
                                              bc3[d][0:96, c0 + 512 * q:c0 + 512 * q + 512], start=True, stop=True)
                            m.then_inc(s["b_psum"], 1)
                            pe.wait_ge(s["g_ready"], n + 1)
                            for q in range(2):
                                m = pe.matmul(ps[:, 2 + q, :], sel[:, bass.ds(it * 2 + (DS + e), 1)].to_broadcast([96, P]),
                                              bc3[d][0:96, c0 + 512 * q:c0 + 512 * q + 512], start=True, stop=True)
                            m.then_inc(s["c_psum"], 1)
                            if e:
                                pe.wait_ge(s["g_ready"], n + 1)
                                for q in range(2):
                                    m = pe.matmul(ps[:, 4 + q, :], ident[:], gg[0][:, 512 * q:512 * q + 512], start=False, stop=True, skip_group_check=True)
                                m.then_inc(s["g_used"], 1)
                        pe.wait_ge(s["g_ready"], it * 2 + (16 * blk + 3))
                        for q in range(2):
                            m = pe.matmul(ps[:, 4 + q, :], ident[:], gg[1][:, 512 * q:512 * q + 512], start=False, stop=True, skip_group_check=True)
                        m.then_inc(s["g_used"], 1)

            pe.wait_ge(s["yg_ready"], 4)
            for j in range(NPO):
                o = ps[:, 0 + j // 8, C * (j % 8):C * (j % 8) + C]
                for d in range(2):
                    m = pe.matmul(o, zs[d][:, j:T:NPO], o_w[d][:], start=(d == 0), stop=(d == 1))
            m.then_inc(s["t2_psum"], 1)
            pe.wait_ge(s["v_ready"], 1)
            for j in range(NPO):
                m = pe.transpose(ps[0:C, 4 + j // 4, (j % 4) * P:(j % 4) * P + P], v_tok[:, j, :], ident[:])
            m.then_inc(s["vt_psum"], 1)
            pe.wait_ge(s["vt_ready"], 1)
            pe.wait_ge(s["wffn_in"], 80)
            for j in range(NPO):
                m = pe.matmul(ps[:, 2, HE * j:HE * j + HE], vt[:, P * j:P * j + P], w_gat[:], start=True, stop=True)
            m.then_inc(s["h_psum"], 1)
            def expert_out(n):
                q, e = n // EXP, n % EXP
                if e == 0:
                    if q >= 2:
                        pe.wait_ge(s["eo_read"], q - 1)
                    if q == 1:
                        pe.wait_ge(s["vt_ready"], 1)
                    for bank in range(2):
                        pe.matmul(ps[:, 4 * (q % 2) + bank, :], ones_f[:], b2[:].unsqueeze(1).to_broadcast([1, 2, EXP * C]), start=True, stop=True)
                pe.wait_ge(s["hid_ready"], n + 1)
                for jj in range(4):
                    o = 256 * (jj % 2) + C * e
                    m = pe.matmul(ps[:, 4 * (q % 2) + jj // 2, o:o + C], hid[n % 2][:, P * jj:P * jj + P], w2[:, e, :],
                                  start=False, stop=True, skip_group_check=True)
                m.then_inc(s["eo_psum"], 1)

            for n in range(4 * EXP):
                q, e = n // EXP, n % EXP
                if n >= 2:
                    pe.wait_ge(s["hid_ready"], n - 1)
                pe.matmul(ps[:, 6 + n % 2, :], w1[:, e, :], vt[:, 512 * q:512 * q + 512], start=True, stop=True).then_inc(s["hid_psum"], 1)
                if n:
                    expert_out(n - 1)
            expert_out(4 * EXP - 1)

        @block.scalar
        def _(act):
            f = act.activation
            k = Link(act, s["act_step"])
            act.wait_ge(s["var_ready"], 1)
            f(gnv[:, 1, :], gnv[:, 0, :], ACT.Sqrt).then_inc(s["std_ready"], 1)
            act.wait_ge(s["off_ready"], 3)
            f(wy, wy, ACT.Abs, bias=ph[:]).then_inc(s["abs_step"], 1)
            f(wx, wx, ACT.Abs, bias=pl[:]).then_inc(s["abs_step"], 1)
            act.wait_ge(s["abs_step"], 1)
            f(wy, wy, ACT.Relu, scale=-1.0, bias=1.0).then_inc(s["hat_ready"], 1)
            act.wait_ge(s["abs_step"], 2)
            f(wx, wx, ACT.Relu, scale=-1.0, bias=1.0).then_inc(s["hat_ready"], 1)
            f(msk[:], om[:, :, 2 * K2:OM], ACT.Sigmoid).then_inc(s["sig_ready"], 1)

            def xk_copy(b):
                for tau in range(2):
                    for hf in range(2):
                        n = 4 * b + 2 * tau + hf
                        act.wait_ge(s["xk_psum"], n + 1)
                        if b >= 2:
                            act.wait_ge(s["conv_out"], 2 * b - 2)
                        f(xk[b % 2][:, tau, 288 * hf:288 * hf + 288], ps[:, 7, 0:288], ACT.Copy).then_inc(s["xk_ready"], 1)

            for i in range(NT):
                if i % 2 == 0:
                    xk_copy(i // 2)
                if i >= 2:
                    act.wait_ge(s["conv_out"], i - 1)
                for q in range(3):
                    n = 3 * i + q
                    act.wait_ge(s["st_psum"], n + 1)
                    f(s_t[i % 2][:, 6 * q:6 * q + 6, :].rearrange("p n q -> p (n q)"), banks(2 * (n % 2), 2)[:, 0:6 * P], ACT.Copy).then_inc(s["st_ready"], 1)
            act.wait_ge(s["ln_var"], 1)
            f(lns[:, 4, :], lns[:, 3, :], ACT.Sqrt).then_inc(s["ln_std"], 1)
            act.wait_ge(s["ln_var"], 2)
            f(lns[:, 4, :], lns[:, 3, :], ACT.Sqrt).then_inc(s["ln_std"], 1)
            act.wait_ge(s["xnt_psum"], 1)
            act.wait_ge(s["gb_in"], 16)
            act.wait_ge(s["da_zero"], 1)
            f(xnt[:, :, TAPS - 1:TAPS - 1 + SEQ], banks(0, 4, C).rearrange("p (b s) -> p b s", b=BATCH), ACT.Identity,
              scale=gb[:, 0:1], bias=gb[:, 1:2]).then_inc(s["xnt_ready"], 1)
            act.wait_ge(s["wmamba_in"], 2 * 8 * 16)
            for d in range(2):
                f(neg_a[d][:], neg_a[d][:], ACT.Exp).then_inc(s["nega_ready"], 1)
            for d in range(2):
                act.wait_ge(s["xs_psum"], d + 1)
                f(xs[d], banks(0, 4), ACT.Silu, bias=vec[d][:, 0:1]).then_inc(s["xs_ready"], 1)
                act.wait_ge(s["z_psum"], d + 1)
                f(zs[d], banks(4, 4), ACT.Silu).then_inc(s["z_ready"], 1)
                act.wait_ge(s["dbc_psum"], d + 1)
                if d:
                    act.wait_ge(s["dt_ready"], d)
                f(dtr, banks(4, 4, DTR), ACT.Copy).then_inc(s["dtr_ready"], 1)
                f(bc3[d][0:96, :], banks(0, 4, 96), ACT.Copy).then_inc(s["hi_ready"], 1)
                act.wait_ge(s["dt_psum"], d + 1)
                f(dtv[d], banks(4, 4), ACT.Relu, bias=vec[d][:, 1:2]).then_inc(s["sp_step"], 1)
                f(sp_t, banks(4, 4), ACT.Abs, bias=vec[d][:, 1:2]).then_inc(s["sp_lin"], 2)
                act.wait_ge(s["sp_lin"], 2 * d + 2)
                f(sp_t, sp_t, ACT.Exp, scale=-1.0).then_inc(s["sp_step"], 1)
                act.wait_ge(s["sp_step"], 2 * d + 2)
                f(uu[d], sp_t, ACT.Ln, bias=1.0).then_inc(s["sp_ln"], 1)
                act.wait_ge(s["rest_ready"], d + 1)
                f(bc3[d][0:64, :], r1, ACT.Copy).then_inc(s["mid_ready"], 1)
            for d in range(2):
                act.wait_ge(s["dt_ready"], d + 1)
                act.wait_ge(s["da_zero"], 2 + d)
                lo = 1 - d
                for hf in range(2):
                    blk, c0 = 2 * d + hf, hf * HALF
                    src = dtv[d][:, c0:c0 + HALF].rearrange("p (b s) -> p b s", s=SEQ)[:, :, lo:lo + SEQ - 1]
                    with act.Fori(0, DS // 2) as it:
                        for e in range(2):
                            act.wait_ge(s["da_used"], it * 2 + (16 * blk + e + 1))
                            f(da[e].rearrange("p (b s) -> p b s", s=SEQ)[:, :, lo:lo + SEQ - 1], src, ACT.Exp,
                              scale=neg_a[d][:, bass.ds(it * 2 + e, 1)]).then_inc(s["da_ready"], 1)
            act.wait_ge(s["ln_var"], 3)
            f(lns[:, 4, :], lns[:, 3, :], ACT.Sqrt).then_inc(s["ln_std"], 1)
            act.wait_ge(s["vt_psum"], 1)
            f(vt, banks(4, 4, C), ACT.Copy).then_inc(s["vt_ready"], 1)
            for n in range(4 * EXP):
                q, e = n // EXP, n % EXP
                act.wait_ge(s["hid_psum"], n + 1)
                if n >= 2:
                    act.wait_ge(s["eo_psum"], n - 1)
                f(hid[n % 2], ps[:, 6 + n % 2, :], ACT.Gelu, bias=b1[:, e:e + 1]).then_inc(s["hid_ready"], 1)
                if e == 0 and q:
                    act.wait_ge(s["eo_psum"], 4 * q)
                    f(eo[:, 4 * q - 4:4 * q].rearrange("p j e c -> p (j e c)"), banks(4 * ((q - 1) % 2), 2), ACT.Copy).then_inc(s["eo_read"], 1)
            act.wait_ge(s["eo_psum"], 4 * EXP)
            f(eo[:, 12:16].rearrange("p j e c -> p (j e c)"), banks(4, 2), ACT.Copy).then_inc(s["eo_read"], 1)
            act.wait_ge(s["e_in"], 1)
            f(g1[:], g1[:], ACT.Exp).then_inc(s["exp_ready"], 1)
            f(g2[:], g2[:], ACT.Exp).then_inc(s["exp_ready"], 1)
            act.wait_ge(s["e_in"], 2)
            f(a_e, a_e, ACT.Exp).then_inc(s["exp_ready"], 1)
            rounds = act.value_load(nleft_i[0:1, 0:1], min_val=0, max_val=EPP)
            with act.If(rounds > 0):
                with act.Fori(0, rounds) as r:
                    with act.Fori(0, 8 * (P // LW)) as c:
                        n = r * (8 * (P // LW)) + c
                        act.wait_ge(s["left_e"], n + 1)
                        f(g1[:], g1[:], ACT.Exp).then_inc(s["left_exp"], 1)
                        f(left_w, left_w, ACT.Exp).then_inc(s["left_exp"], 1)
            act.wait_ge(s["ln_var"], 4)
            f(gs[:, 4, :], gs[:, 3, :], ACT.Sqrt).then_inc(s["ln_std"], 1)
            act.wait_ge(s["ln_var"], 5)
            f(gate[:], gate[:], ACT.Exp).then_inc(s["ln_std"], 1)

        @block.vector
        def _(v):
            k = Link(v, s["dve_step"])

            def bc(ap, axis, n):
                shape = list(ap.unsqueeze(axis).shape)
                shape[axis] = n
                return ap.unsqueeze(axis).to_broadcast(shape)

            tt, ts, stt = v.tensor_tensor, v.tensor_scalar, v.scalar_tensor_tensor

            v.sem_inc(s["b_used"], 1)
            v.sem_inc(s["g_ready"], 1)
            v.sem_inc(s["g_used"], 2)
            v.sem_inc(s["da_used"], 2)

            v.memset(pause[:], 0.0)
            v.wait_ge(s["const_ready"], 1)
            k(ts(pi_tmp[:, 0:1], iota_pi[:], 4, None, ALU.arith_shift_right))
            k(ts(pi_tmp[:, 1:2], iota_pi[:], 15, None, ALU.bitwise_and))
            k(v.tensor_copy(ph[:], pi_tmp[:, 0:1]))
            k(v.tensor_copy(pl[:], pi_tmp[:, 1:2]))
            k(v.tensor_copy(pf[:], iota_pi[:]))
            v.wait_ge(s["xt_ready"], 1)
            for b in range(BATCH):
                k.go(v.bn_stats(out=st6[:, b, :], in_=ps[0:C, b // 2, (b % 2) * SEQ:(b % 2) * SEQ + SEQ]))
            k.wait()
            for b in range(BATCH):
                k.go(v.bn_aggr(out=mv[:, b, :], in_=st6[:, b, :]))
            k.wait()
            k(v.tensor_copy(ms[:, :, 0], mv[:, :, 0]))
            k(tt(ms[:, :, 1], mv[:, :, 0], mv[:, :, 0], ALU.mult))
            tt(ms[:, :, 1], ms[:, :, 1], mv[:, :, 1], ALU.add).then_inc(s["stats_ready"], 1)
            v.wait_ge(s["pair_ready"], 1)
            k(v.tensor_copy(gnm[:].rearrange("p b s -> p (b s)"), ps[0:C, 4, 0:2 * BATCH]))
            k(tt(gnv[:, 0, :], gnm[:, :, 0], gnm[:, :, 0], ALU.mult))
            k(tt(gnv[:, 0, :], gnm[:, :, 1], gnv[:, 0, :], ALU.subtract))
            ts(gnv[:, 0, :], gnv[:, 0, :], 1e-5, None, ALU.add).then_inc(s["var_ready"], 1)
            v.wait_ge(s["std_ready"], 1)
            k(v.reciprocal(gnv[:, 1, :], gnv[:, 1, :]))
            for b in range(BATCH):
                image = ps[0:C, b // 2, (b % 2) * SEQ:(b % 2) * SEQ + SEQ].rearrange("p (y x) -> p y x", x=WIDTH)
                for kx in (0, 2, 1):
                    lo, hi = max(0, 1 - kx), min(WIDTH, WIDTH + 1 - kx)
                    m = ts(xpad[:, kx, b, 1:1 + HEIGHT, lo:hi], image[:, :, lo + kx - 1:hi + kx - 1],
                           gnm[:, b, 0:1], gnv[:, 1, b:b + 1], ALU.subtract, ALU.mult)
                    if kx != 1:
                        k.go(m)
                m.then_inc(s["xhat_ready"], 1)
            k.wait()
            v.wait_ge(s["cw_in"], 64)
            for d in range(2):
                tt(w_tap[d][:], bc(in_w[d][:, 0:DI], 1, TAPS), cw_b[d], ALU.mult).then_inc(s["taps_ready"], 1)
            v.wait_ge(s["wmamba_in"], 2 * 8 * 16)
            for d in range(2):
                ts(diag_d[d][:], ident[:], vec[d][:, 2:3], None, ALU.mult).then_inc(s["diag_ready"], 1)

            v.wait_ge(s["edge_in"], 32)
            k.go(v.tensor_copy(e_tmp, src_i))
            k.go(v.tensor_copy(e_tm2, dst_i))
            k(ts(e_int, dst_i, LO - 1, None, ALU.bitwise_and))
            k(stt(out=keys[:, 0:EPP], in0=e_tm2, scalar=float(T), in1=e_tmp, op0=ALU.mult, op1=ALU.add))
            k(ts(e_tmp, e_tmp, float(LAST), None, ALU.is_lt))
            k.go(stt(out=lo_b[:], in0=e_tmp, scalar=float(LO), in1=e_int, op0=ALU.mult, op1=ALU.add))
            k(stt(out=e_tm2, in0=e_tm2, scalar=float(T), in1=e_tmp, op0=ALU.is_lt, op1=ALU.mult))
            k(stt(out=keys[:, 0:EPP], in0=keys[:, 0:EPP], scalar=1.0, in1=e_tm2, op0=ALU.add, op1=ALU.mult))
            k(ts(e_int, dst_i, 6, None, ALU.arith_shift_right))
            k(v.tensor_copy(hi_b[:], e_int))

            v.wait_ge(s["om_ready"], 1)
            k(v.tensor_copy(om[:].rearrange("p t n -> p (t n)"), ps[:, 5, 0:NT * OM]))
            for i2 in range(2):
                tt(wy[:, i2:NT:2], bc(om[:, i2:NT:2, 0:2 * K2:2], 3, HEIGHT),
                   bc(iota_y[:, i2, :].rearrange("p (k y) -> p k y", k=K2), 1, BATCH), ALU.add).then_inc(s["off_ready"], 1)
            tt(wx, bc(om[:, :, 1:2 * K2:2], 3, WIDTH), bc(iota_x[:], 1, NT), ALU.add).then_inc(s["off_ready"], 1)
            v.wait_ge(s["sig_ready"], 1)
            k(ts(msk[:], msk[:], 2.0, None, ALU.mult))
            v.wait_ge(s["hat_ready"], 2)
            k(tt(wx, wx, bc(msk[:], 3, WIDTH), ALU.mult))

            def conv_sum(i):
                v.wait_ge(s["conv_out"], i + 1)
                tt(x_tok[:, i, :], x_tok[:, i, :], ps[:, 5 + i % 2, 0:C], ALU.add).then_inc(s["t1_ready"], 1)

            for i in range(NT):
                if i >= 1:
                    v.wait_ge(s["st_psum"], 3 * i)
                tt(s_buf, bc(wy[:, i], 3, WIDTH), bc(wx[:, i], 2, HEIGHT), ALU.mult).then_inc(s["s_ready"], 1)
                if i >= 2:
                    conv_sum(i - 2)
                if i % 2 and i // 2 < len(CHUNKS):
                    ch = i // 2
                    e0, en = CHUNKS[ch]
                    if ch:
                        v.wait_ge(s["onehot_used"], ch)
                    for d in range(HI):
                        k.go(ts(one_hi[:, d, 0:en], hi_b[:, e0:e0 + en], float(d), None, ALU.is_equal))
                    for d in range(LO):
                        m = ts(one_lo[:, d, 0:en], lo_b[:, e0:e0 + en], float(d), None, ALU.is_equal)
                        if d < LO - 1:
                            k.go(m)
                        else:
                            m.then_inc(s["onehot_ready"], 1)
            conv_sum(NT - 2)
            conv_sum(NT - 1)
            v.wait_ge(s["onehot_used"], len(CHUNKS))
            v.tensor_copy(hist_s[:], ps[:, 4, 0:LO]).then_inc(s["hist_ready"], 1)
            v.wait_ge(s["t1_ready"], NT)

            def norm(dst, src, diff, sq, st, n, width, out_sem):
                k(v.tensor_reduce(out=st[:, 0, :], in_=src, axis=AX, op=ALU.add))
                k(ts(st[:, 1, :], st[:, 0, :], 1.0 / width, None, ALU.mult))
                k(tt(diff, src, bc(st[:, 1, :], 2, width), ALU.subtract))
                k(tt(sq, diff, diff, ALU.mult))
                k(v.tensor_reduce(out=st[:, 2, :], in_=sq, axis=AX, op=ALU.add))
                ts(st[:, 3, :], st[:, 2, :], 1.0 / width, 1e-5, ALU.mult, ALU.add).then_inc(s["ln_var"], 1)
                v.wait_ge(s["ln_std"], n)
                k(v.reciprocal(st[:, 5, :], st[:, 4, :]))
                m = tt(dst, diff, bc(st[:, 5, :], 2, width), ALU.mult)
                if out_sem is None:
                    k(m)
                else:
                    m.then_inc(out_sem, 1)

            norm(un, x_tok[:], lnd, lsq, lns, 1, C, None)
            tt(x_tok[:], x_tok[:], un, ALU.add).then_inc(s["res_ready"], 1)
            norm(xn, un, lnd, lsq, lns, 2, C, s["xn_ready"])
            k(v.memset(xnt[:, :, 0:TAPS - 1], 0.0))
            v.memset(xnt[:, :, TAPS - 1 + SEQ:SEQP], 0.0).then_inc(s["da_zero"], 1)
            v.wait_ge(s["nega_ready"], 2)
            for d in range(2):
                k(ts(neg_a[d][:], neg_a[d][:], -1.0, None, ALU.mult))

            for r in range(ROUNDS):
                k(v.max(out=comp[:, 8 * r:8 * r + 8], in_=keys[:, 0:EPP]))
                k(v.match_replace(out=keys[:, 0:EPP], in_to_replace=comp[:, 8 * r:8 * r + 8], in_values=keys[:, 0:EPP], imm_value=0.0))
            k(ts(key_i[:], comp, -1.0, None, ALU.add))
            k(ts(int_a[:, 0, :], key_i[:], 15, None, ALU.arith_shift_right))
            k(v.tensor_copy(owner[:], int_a[:, 0, :]))
            tt(own1, bc(iota_n[:], 1, CAP), bc(owner[:], 2, P), ALU.is_equal).then_inc(s["own_ready"], 1)
            k(ts(int_a[:, 0, :], key_i[:], 4, 127, ALU.arith_shift_right, ALU.bitwise_and))
            k(ts(dig[:, 0, :], int_a[:, 0, :], 1.0, None, ALU.add))
            k(ts(int_a[:, 1, :], key_i[:], 11, 15, ALU.arith_shift_right, ALU.bitwise_and))
            k(ts(int_a[:, 2, :], key_i[:], 15, None, ALU.bitwise_and))
            k(stt(out=dig[:, 1, :], in0=int_a[:, 2, :], scalar=16.0, in1=int_a[:, 1, :], op0=ALU.mult, op1=ALU.add))
            k(v.memset(same[:, 0:1], 0.0))
            k(tt(same[:, 1:CAP], owner[:, 1:CAP], owner[:, 0:CAP - 1], ALU.is_equal))
            k(v.tensor_tensor_scan(run[:], same[:], same[:], 0.0, ALU.mult, ALU.add))
            v.wait_ge(s["base_psum"], 1)
            k(ts(base_b[:], ps[:, 5, 0:P], float(P), None, ALU.min))
            k(tt(look, own1, bc(base_b[:], 1, CAP), ALU.mult))
            k(v.tensor_reduce(out=slot[:], in_=look, axis=AX, op=ALU.add))
            k(tt(slot[:], slot[:], run[:], ALU.add))
            k(tt(slot1, bc(iota_n[:, 0:W], 1, CAP), bc(slot[:], 2, W), ALU.is_equal))
            k(tt(pay[:, :, 0, :], slot1, bc(dig[:, 0, :], 2, W), ALU.mult))
            tt(pay[:, :, 1, :], slot1, bc(dig[:, 1, :], 2, W), ALU.mult).then_inc(s["pay_ready"], 1)
            k(stt(out=comp, in0=slot[:], scalar=float(W) - 0.5, in1=comp, op0=ALU.is_gt, op1=ALU.mult))
            ts(key_tmp, keys[:], 0.5, 0.0, ALU.is_gt, ALU.add, accum_out=nleft[:, 0:1]).then_inc(s["left_count"], 1)
            v.wait_ge(s["left_psum"], 1)
            k(v.reduce_max(nleft[0:1, 1:2], ps[0:1, 7, 0:P], AX))
            k(ts(nleft_i[0:1, 1:2], nleft[0:1, 1:2], 7.0, None, ALU.add))
            ts(nleft_i[0:1, 0:1], nleft_i[0:1, 1:2], 3, None, ALU.arith_shift_right).then_inc(s["left_known"], 1)
            v.wait_ge(s["ell_psum"], 1)
            k(v.tensor_copy(ell[:].rearrange("p h w -> p (h w)"), ps[:, 6, 0:2 * W]))
            k(v.tensor_copy(ell_i[:, 0, :], ell[:, 1, :]))
            k(ts(ell_i[:, 1, :], ell_i[:, 0, :], 4, None, ALU.arith_shift_right))
            k(ts(ell_i[:, 2, :], ell_i[:, 0, :], 15, None, ALU.bitwise_and))
            k(ts(jslot[:, 1, :], ell[:, 0, :], 1.0, 0.0, ALU.subtract, ALU.max))
            k(ts(jslot[:, 0, :], ell[:, 0, :], 0.5, -100.0, ALU.is_lt, ALU.mult))
            k(tt(jslot[:, 0, :], jslot[:, 0, :], ell_i[:, 2, :], ALU.add))
            stt(out=src_idx[:], in0=jslot[:, 1, :], scalar=16.0, in1=ell_i[:, 1, :], op0=ALU.mult, op1=ALU.add).then_inc(s["idx_ready"], 1)
            k(tt(pen[:], bc(jslot[:, 0, :], 1, NPO), bc(iota_j[:], 2, W), ALU.is_equal))
            k(ts(pen[:], pen[:], 1.0, BIG, ALU.subtract, ALU.mult))

            for d in range(2):
                v.wait_ge(s["hi_ready"], d + 1)
                tt(r1, banks(0, 4, 64), bc3[d][0:64, :], ALU.subtract).then_inc(s["rest_ready"], 1)
                v.wait_ge(s["sp_ln"], d + 1)
                k(ts(sp_c, sp_t, 1.0, 1.0, ALU.add, ALU.subtract))
                k(tt(sp_c, sp_t, sp_c, ALU.subtract))
                k(tt(sp_c, sp_c, uu[d], ALU.add))
                tt(dtv[d], dtv[d], sp_c, ALU.add).then_inc(s["dt_ready"], 1)
                v.wait_ge(s["dt_ready"], d + 1)
                k(tt(uu[d], dtv[d], xs[d], ALU.mult))
                v.wait_ge(s["mid_ready"], d + 1)
                tt(bc3[d][0:32, :], r1[0:32, :], bc3[d][0:32, :], ALU.subtract).then_inc(s["bc_ready"], 1)
                v.wait_ge(s["bc_ready"], d + 1)

            for d in range(2):
                first = 0 if d == 0 else SEQ - 1
                for e in range(2):
                    m = v.memset(da[e].rearrange("p (b s) -> p b s", s=SEQ)[:, :, first:first + 1], 0.0)
                    if e:
                        m.then_inc(s["da_zero"], 1)
                    else:
                        k(m)
                for hf in range(2):
                    blk, c0 = 2 * d + hf, hf * HALF
                    with v.Fori(0, DS // 2) as it:
                        for e in range(2):
                            n = it * 2 + (16 * blk + e)
                            v.wait_ge(s["b_psum"], n + 1)
                            tt(hh[e], uu[d][:, c0:c0 + HALF], banks(0, 2), ALU.mult).then_inc(s["b_used"], 1)
                            v.wait_ge(s["da_ready"], n + 1)
                            v.wait_ge(s["b_used"], n + 2)
                            o, x0, x1 = hh[e], da[e], hh[e]
                            if d:
                                o, x0, x1 = o[:, ::-1], x0[:, ::-1], x1[:, ::-1]
                            v.tensor_tensor_scan(o, x0, x1, 0.0, ALU.mult, ALU.add).then_inc(s["da_used"], 1)
                            v.wait_ge(s["c_psum"], n + 1)
                            v.wait_ge(s["g_used"], n + 1)
                            v.wait_ge(s["da_used"], n + 3)
                            tt(gg[e], hh[e], banks(2, 2), ALU.mult).then_inc(s["g_ready"], 1)
                    v.wait_ge(s["g_used"], 16 * blk + 18)
                    tt(zs[d][:, c0:c0 + HALF], zs[d][:, c0:c0 + HALF], banks(4, 2), ALU.mult).then_inc(s["yg_ready"], 1)

            v.wait_ge(s["t2_psum"], 1)
            v.wait_ge(s["res_back"], 16)
            k(tt(t2.rearrange("p j c -> p (j c)"), resb.rearrange("p j c -> p (j c)"), banks(0, 2), ALU.add))
            norm(v_tok, t2, d_tok, v_tok, lns, 3, C, s["v_ready"])
            v.wait_ge(s["att_in"], 32)
            v.wait_ge(s["h_psum"], 1)
            k(v.tensor_copy(hrow[:, :, 0:HE], ps[:, 2, 0:NPO * HE].rearrange("p (j n) -> p j n", j=NPO)))
            for r in (1, 0):
                k(tt(atmp[:], hrow[:, :, 0:HE], bc(att[:, r, :], 1, NPO), ALU.mult))
                to = adst[:].rearrange("p h j -> p j h") if r else hrow[:, :, HE:ROW]
                m = v.tensor_reduce(out=to, in_=atmp[:].rearrange("p j (h x) -> p j h x", h=HEADS), axis=AX, op=ALU.add)
                if r:
                    k(m)
                else:
                    m.then_inc(s["h_ready"], 1)

            def lrelu(dst, src):
                return stt(out=dst, in0=src, scalar=0.2, in1=src, op0=ALU.mult, op1=ALU.max)

            v.wait_ge(s["hist_back"], 16)
            v.wait_ge(s["last_in"], 16)
            k(v.tensor_reduce(out=cnt[:], in_=cnt4[:].rearrange("p g j -> p j g"), axis=AX, op=ALU.add))
            k(ts(gs[:, 0, :], cnt[:], 0.5, 1.0, ALU.is_gt, ALU.subtract))
            k(ts(gs[:, 0, :], gs[:, 0, :], BIG, None, ALU.mult))
            k(tt(g2[:], bc(gs[:, 0, :], 1, HEADS), bc(last[:, HE:ROW], 2, NPO), ALU.add))
            aself = hrow[:, :, HE:ROW].rearrange("p j h -> p h j")
            v.wait_ge(s["h_ready"], 1)
            k(tt(amax[:], aself, g2[:], ALU.max))
            v.wait_ge(s["nb_in"], 16 * W)
            for h in range(HEADS):
                k(tt(a_e[:, h], pen[:], bc(nb[:, :, HE + h], 1, NPO), ALU.add))
            k(v.tensor_reduce(out=mx[:], in_=a_e, axis=AX, op=ALU.max))
            k(tt(amax[:], amax[:], mx[:], ALU.max))
            k(tt(mx[:], amax[:], adst[:], ALU.add))
            k(lrelu(mcur[:], mx[:]))
            for t, x in ((g1, aself), (g2, g2[:])):
                k(tt(t[:], x, adst[:], ALU.add))
                k(lrelu(t[:], t[:]))
                m = tt(t[:], t[:], mcur[:], ALU.subtract)
                if t is g1:
                    k(m)
                else:
                    m.then_inc(s["e_in"], 1)

            def left_edges(n, c, at):
                done = [0]

                def step(ins):
                    done[0] += 1
                    ins.then_inc(s["left_step"], 1)
                    v.wait_ge(s["left_step"], at + done[0])

                step(v.tensor_copy(left_row[:, ROW:ROW + 1], m8[:, bass.ds(c, 1)]))
                step(ts(left_idx[:, 1:2], left_row[:, ROW:ROW + 1], -1.0, None, ALU.add))
                ts(left_idx[:, 0:1], left_idx[:, 1:2], LAST, None, ALU.bitwise_and).then_inc(s["left_idx_ready"], 1)
                v.wait_ge(s["left_in"], n * 16 + 16)
                step(ts(lk[:, 0, :], left_all[:, :, ROW], -1.0, None, ALU.add))
                step(ts(lk[:, 1, :], lk[:, 0, :], 15, None, ALU.arith_shift_right))
                step(ts(lkf[:, 0, :], lk[:, 1, :], pf[:], None, ALU.is_equal))
                step(ts(lk[:, 1, :], lk[:, 0, :], 11, 15, ALU.arith_shift_right, ALU.bitwise_and))
                step(stt(out=lkf[:, 1, :], in0=lk[:, 1, :], scalar=1.0, in1=lkf[:, 0, :], op0=ALU.add, op1=ALU.mult))
                step(ts(lkf[:, 1, :], lkf[:, 1, :], -1.0, None, ALU.add))
                for q in range(P // LW):
                    e0 = q * LW
                    step(tt(left_pen, bc(lkf[:, 1, e0:e0 + LW], 1, NPO), bc(iota_j[:], 2, LW), ALU.is_equal))
                    step(ts(left_pen, left_pen, 1.0, BIG, ALU.subtract, ALU.mult))
                    for h in range(HEADS):
                        step(tt(left_w[:, h], left_pen, bc(left_all[:, e0:e0 + LW, HE + h], 1, NPO), ALU.add))
                    step(v.tensor_reduce(out=mx[:], in_=left_w, axis=AX, op=ALU.max))
                    step(tt(amax[:], amax[:], mx[:], ALU.max))
                    step(tt(mx[:], amax[:], adst[:], ALU.add))
                    step(lrelu(mx[:], mx[:]))
                    step(tt(g1[:], mcur[:], mx[:], ALU.subtract))
                    step(v.tensor_copy(mcur[:], mx[:]))
                    step(tt(flat(left_w), flat(left_w), bc(ad2, 2, LW), ALU.add))
                    step(lrelu(flat(left_w), flat(left_w)))
                    tt(flat(left_w), flat(left_w), bc(mc2, 2, LW), ALU.subtract).then_inc(s["left_e"], 1)
                    v.wait_ge(s["left_exp"], n * (2 * (P // LW)) + (2 * q + 2))
                    step(tt(den[:], den[:], g1[:], ALU.mult))
                    step(v.tensor_reduce(out=mx[:], in_=left_w, axis=AX, op=ALU.add))
                    step(tt(den[:], den[:], mx[:], ALU.add))
                    for h in range(HEADS):
                        step(tt(left_p, bc(left_w[:, h], 1, EXP),
                                bc(left_all[:, e0:e0 + LW, EXP * h:EXP * h + EXP].rearrange("p w x -> p x w"), 2, NPO), ALU.mult))
                        step(v.tensor_reduce(out=g4[:, h], in_=left_p, axis=AX, op=ALU.add))
                        step(tt(acc[:, h], acc[:, h], bc(g1[:, h], 1, EXP), ALU.mult))
                        step(tt(acc[:, h], acc[:, h], g4[:, h], ALU.add))
                assert done[0] == LEFT_COLUMN, done[0]

            def flat(x):
                return x.rearrange("p h j w -> p (h j) w")

            ad2, mc2 = adst[:].rearrange("p h j -> p (h j)"), mcur[:].rearrange("p h j -> p (h j)")
            k(tt(flat(a_e), flat(a_e), bc(ad2, 2, W), ALU.add))
            k(lrelu(flat(b_e), flat(a_e)))
            tt(flat(a_e), flat(b_e), bc(mc2, 2, W), ALU.subtract).then_inc(s["e_in"], 1)
            v.wait_ge(s["exp_ready"], 3)
            k(tt(g2[:], g2[:], bc(cnt[:], 1, HEADS), ALU.mult))
            k(v.tensor_reduce(out=den[:], in_=a_e, axis=AX, op=ALU.add))
            k(tt(den[:], den[:], g1[:], ALU.add))
            k(tt(den[:], den[:], g2[:], ALU.add))
            for h in range(HEADS):
                o = b_e[:].rearrange("p x j w -> p x j w")
                k(tt(o, bc(a_e[:, h], 1, EXP), bc(nb[:, :, EXP * h:EXP * h + EXP].rearrange("p w x -> p x w"), 2, NPO), ALU.mult))
                k(v.tensor_reduce(out=acc[:, h], in_=o, axis=AX, op=ALU.add))
            hself = hrow[:, :, 0:HE].rearrange("p j (h x) -> p h x j", h=HEADS)
            for h in range(HEADS):
                k(tt(g4[:, h], bc(g1[:, h], 1, EXP), hself[:, h], ALU.mult))
                k(tt(acc[:, h], acc[:, h], g4[:, h], ALU.add))
                k(tt(g4[:, h], bc(g2[:, h], 1, EXP), bc(last[:, EXP * h:EXP * h + EXP], 2, NPO), ALU.mult))
                k(tt(acc[:, h], acc[:, h], g4[:, h], ALU.add))

            rounds = v.value_load(nleft_i[0:1, 0:1], min_val=0, max_val=EPP)
            with v.If(rounds > 0):
                with v.Fori(0, rounds) as r:
                    ls = s["left_step"]
                    v.max(out=m8[:], in_=keys[:]).then_inc(ls, 1)
                    v.wait_ge(ls, r * LEFT_ROUND + 1)
                    v.memset(pause[:, 1:2], 0.0)
                    v.match_replace(out=keys[:], in_to_replace=m8[:], in_values=keys[:], imm_value=0.0).then_inc(ls, 1)
                    v.wait_ge(ls, r * LEFT_ROUND + 2)
                    v.memset(pause[:, 1:2], 0.0)
                    with v.Fori(0, 8) as c:
                        at = r * LEFT_ROUND + c * LEFT_COLUMN + 2
                        left_edges(r * 8 + c, c, at)
            k(ts(den[:], den[:], 1e-16, None, ALU.add))
            k(v.reciprocal(den[:], den[:]))
            aggv = agg[:].rearrange("p j (h x) -> p h x j", h=HEADS)
            for h in range(HEADS):
                k(tt(aggv[:, h], acc[:, h], bc(den[:, h], 1, EXP), ALU.mult))
            k(tt(agg[:], agg[:], bc(rows16[:, 0, :], 1, NPO), ALU.add))
            norm(agg[:], agg[:], agg[:], atmp[:], gs[:], 4, HE, None)
            k(tt(agg[:], agg[:], bc(rows16[:, 1, :], 1, NPO), ALU.mult))
            k(tt(agg[:], agg[:], bc(rows16[:, 2, :], 1, NPO), ALU.add))
            k(v.tensor_reduce(out=sc[:], in_=agg[:].rearrange("p j (h x) -> p j x h", h=HEADS), axis=AX, op=ALU.add))
            k(ts(sc[:], sc[:], 1.0 / HEADS, None, ALU.mult))
            k(tt(cmp1, bc(sc[:], 2, EXP), bc(sc[:], 3, EXP), ALU.is_gt))
            k(tt(cmp2, bc(sc[:], 2, EXP), bc(sc[:], 3, EXP), ALU.is_equal))
            k(tt(cmp2.rearrange("p j a b -> p j (a b)"), cmp2.rearrange("p j a b -> p j (a b)"),
                 bc(tiebreak[:].rearrange("p a b -> p (a b)"), 1, NPO), ALU.mult))
            k(tt(cmp1, cmp1, cmp2, ALU.add))
            k(v.tensor_reduce(out=atmp[:, :, 0:EXP], in_=cmp1, axis=AX, op=ALU.add))
            k(v.tensor_reduce(out=gs[:, 0, :], in_=sc[:], axis=AX, op=ALU.max))
            tt(gate[:], sc[:], bc(gs[:, 0, :], 2, EXP), ALU.subtract).then_inc(s["ln_var"], 1)
            v.wait_ge(s["ln_std"], 5)
            k(stt(out=gate[:], in0=atmp[:, :, 0:EXP], scalar=1.5, in1=gate[:], op0=ALU.is_lt, op1=ALU.mult))
            k(v.tensor_reduce(out=gs[:, 1, :], in_=gate[:], axis=AX, op=ALU.add))
            k(v.reciprocal(gs[:, 1, :], gs[:, 1, :]))
            k(tt(gate[:], gate[:], bc(gs[:, 1, :], 2, EXP), ALU.mult))
            v.wait_ge(s["eo_read"], 4)
            ev = eo.rearrange("p j e c -> p (j e) c")
            k(tt(ev, ev, bc(gate[:].rearrange("p j e -> p (j e)"), 2, C), ALU.mult))
            k(v.tensor_reduce(out=d_tok, in_=eo.rearrange("p j e c -> p j c e"), axis=AX, op=ALU.add))
            tt(t2, t2, d_tok, ALU.add).then_inc(s["out_ready"], 1)


INS = ["x", "om_kernel", "om_bias", "kernel", "bias", "edges", "ln_gb", "w_gat", "att", "rows16", "w1", "b1", "w2", "b2"] + [
    p + n for p in ("f_", "b_") for n in ("in_w", "conv_w", "vec", "xp_w", "dp_w", "a_log", "o_w")]


def laid_out(x, **w):
    import numpy as np

    def c(v):
        return np.ascontiguousarray(v)

    r = {
        "x": c(x).reshape(T, C), "om_kernel": c(w["L0_conv_om_kernel"]).reshape(K2, C, OM),
        "om_bias": c(w["L0_conv_om_bias"]).reshape(1, OM), "kernel": c(w["L0_conv_kernel"]),
        "bias": c(w["L0_conv_bias"]).reshape(1, C), "edges": c(w["L1_ffn_edge_index"]),
        "ln_gb": c(np.stack([w["L1_attn_ln_gamma"], w["L1_attn_ln_beta"]], 1)),
        "w_gat": c(w["L1_ffn_W_gat"]),
        "att": c(np.stack([w["L1_ffn_att_src"], w["L1_ffn_att_dst"]])).reshape(1, 2 * HE),
        "rows16": c(np.stack([w["L1_ffn_b_gat"], w["L1_ffn_ln_gamma"], w["L1_ffn_ln_beta"]])).reshape(1, 3 * HE),
        "w1": c(w["L1_ffn_W1"]), "b1": c(np.asarray(w["L1_ffn_b1"]).T), "w2": c(w["L1_ffn_W2"]),
        "b2": c(w["L1_ffn_b2"]).reshape(1, EXP * C),
    }
    for p in ("f_", "b_"):
        def m(n):
            return np.asarray(w["L1_attn_" + p + n])
        r[p + "in_w"] = c(m("in_proj_w").T)
        r[p + "conv_w"] = c(m("conv_w")[:, 0, :].T).reshape(1, TAPS * DI)
        r[p + "vec"] = c(np.stack([m("conv_b"), m("dt_proj_b"), m("D")], 1))
        r[p + "xp_w"] = c(m("x_proj_w").T)
        r[p + "dp_w"] = c(m("dt_proj_w").T)
        r[p + "a_log"] = c(m("A_log"))
        r[p + "o_w"] = c(m("out_proj_w").T)
    return r


def kernel(**inputs):
    import numpy as np
    import concourse.bacc as bacc
    from concourse.bass_utils import run_bass_kernel_spmd

    nc = bacc.Bacc("TRN2", target_bir_lowering=False, num_devices=1)
    arrays = laid_out(**{n: np.asarray(v) for n, v in inputs.items()})
    a = {n: nc.dram_tensor("dram_" + n, arrays[n].shape, mybir.dt.from_np(arrays[n].dtype), kind="ExternalInput").ap() for n in INS}
    out = nc.dram_tensor("out", [T, C], F32, kind="ExternalOutput").ap()
    program(nc, a, out)
    r = run_bass_kernel_spmd(nc, [{"dram_" + n: arrays[n] for n in INS}], core_ids=[0])
    return r.results[0]["out"].reshape(BATCH, HEIGHT, WIDTH, C)
```

```python
from contextlib import ExitStack

import concourse.bass as bass
from concourse import mybir

P = 128
BATCH, HEIGHT, WIDTH, C = 8, 16, 16, 64
SEQ = HEIGHT * WIDTH
T = BATCH * SEQ
NT = T // P
K2 = 9
OM = 3 * K2
GROUPS = 32
DI, DS, DTR, TAPS = 128, 16, 16, 4
SEQP = SEQ + 2 * (TAPS - 1)
HALF = T // 2
EDGES = 262144
EPP = EDGES // P
LAST = T - 1
HI, LO = 32, 64
HCH = 296
CHUNKS = [(e, min(HCH, EPP - e)) for e in range(0, EPP, HCH)]
CAP = 56
W = 56
ROUNDS = CAP // 8
OMQ = 4
TPQ = NT // OMQ
POOL_TAPS = 4
NPO = T // P
HEADS, EXP = 4, 4
HE = HEADS * EXP
ROW = HE + HEADS
HID = 2 * C
LW = 32
BIG = 1.0e30
LEFT_COLUMN = 8 + (P // LW) * 33
LEFT_ROUND = 4 + 8 * LEFT_COLUMN

F32 = mybir.dt.float32
BF16 = mybir.dt.bfloat16
I32 = mybir.dt.int32
ALU = mybir.AluOpType
ACT = mybir.ActivationFunctionType
AX = mybir.AxisListType.X


class Link:

    def __init__(self, eng, sem):
        self.eng, self.sem, self.n = eng, sem, 0

    def __call__(self, ins):
        self.go(ins)
        self.wait()

    def go(self, ins):
        self.n += 1
        ins.then_inc(self.sem, 1)

    def wait(self):
        self.eng.wait_ge(self.sem, self.n)


def program(nc, a, out):
    with ExitStack() as ctx:
        def sb(name, shape, dt=F32):
            return ctx.enter_context(nc.sbuf_tensor(name, shape, dt))

        def sem(name):
            return ctx.enter_context(nc.semaphore(name))

        ps = ctx.enter_context(nc.psum_tensor("ps", [P, 8, 512], F32))

        def banks(lo, n, parts=P):
            return ps[0:parts, lo:lo + n, :].rearrange("p b n -> p (b n)")

        class Arena:

            def __init__(self, name, words):
                self.mem, self.words, self.top = sb(name, [P, words]), words, 0

            def __call__(self, n, dt=F32, parts=P):
                lo, words = self.top, n if dt != BF16 else (n + 1) // 2
                self.top += words
                assert self.top <= self.words, self.top
                v = self.mem[0:parts, lo:lo + words]
                return v if dt == F32 else v.bitcast(dt)

        ident = sb("ident", [P, P])
        ones_f = sb("ones_f", [1, P])
        iota_pi = sb("iota_pi", [P, 1], I32)
        pi_tmp = sb("pi_tmp", [P, 2], I32)
        ph = sb("ph", [P, 1])
        pl = sb("pl", [P, 1])
        pf = sb("pf", [P, 1])
        iota_y = sb("iota_y", [P, 2, K2 * HEIGHT])
        iota_x = sb("iota_x", [P, K2, WIDTH])
        pairmat = sb("pairmat", [P, P])
        iota_n = sb("iota_n", [P, P], BF16)
        tri = sb("tri", [P, P], BF16)
        sel = sb("sel", [96, 32], BF16)
        iota_j = sb("iota_j", [P, NPO])
        tiebreak = sb("tiebreak", [P, EXP, EXP])
        w_om2 = sb("w_om2", [P, 3, OM])
        w_om1 = sb("w_om1", [C, 3, OM])
        b_om = sb("b_om", [OM, 1])
        w_cv = sb("w_cv", [C, K2, C])
        b_cv = sb("b_cv", [1, C])
        in_w = [sb(f"in_w{d}", [P, 2 * DI]) for d in range(2)]
        w_tap = [sb(f"w_tap{d}", [P, TAPS // 2, DI]) for d in range(2)]
        vec = [sb(f"vec{d}", [P, 3]) for d in range(2)]
        xp_w = [sb(f"xp_w{d}", [P, 96]) for d in range(2)]
        xd_w = [sb(f"xd_w{d}", [DTR, DI]) for d in range(2)]
        dt_w = [sb(f"dt_w{d}", [P, DI]) for d in range(2)]
        dp_w = [sb(f"dp_w{d}", [DTR, DI]) for d in range(2)]
        neg_a = [sb(f"neg_a{d}", [P, DS]) for d in range(2)]
        diag_d = [sb(f"diag_d{d}", [P, P]) for d in range(2)]
        o_w = [sb(f"o_w{d}", [P, C]) for d in range(2)]
        gb = sb("gb", [P, 2])
        w_gat = sb("w_gat", [C, HE])
        att = sb("att", [P, 2, HE])
        rows16 = sb("rows16", [P, 3, HE])
        w1 = sb("w1", [C, EXP, HID])
        b1 = sb("b1", [HID, EXP])
        w2 = sb("w2", [HID, EXP, C])
        b2 = sb("b2", [1, EXP * C])
        x_tok = sb("x_tok", [P, NT, C])
        st6 = sb("st6", [P, BATCH, 6])
        mv = sb("mv", [P, BATCH, 2])
        ms = sb("ms", [P, BATCH, 2])
        gnm = sb("gnm", [P, BATCH, 2])
        gnv = sb("gnv", [P, 3, BATCH])
        om = sb("om", [P, NT, OM])
        msk = sb("msk", [P, NT, K2])
        lns = sb("lns", [P, 6, NT])
        keys = sb("keys", [P, EPP + CAP])
        comp = keys[:, EPP:EPP + CAP]
        hi_b = sb("hi_b", [P, EPP], BF16)
        lo_b = sb("lo_b", [P, EPP], BF16)
        key_i = sb("key_i", [P, CAP], I32)
        int_a = sb("int_a", [P, 3, CAP], I32)
        owner = sb("owner", [P, CAP])
        owner_b = sb("owner_b", [P, CAP], BF16)
        same = sb("same", [P, CAP])
        run = sb("run", [P, CAP])
        slot = sb("slot", [P, CAP])
        dig = sb("dig", [P, 2, CAP])
        base_b = sb("base_b", [P, P], BF16)
        ell = sb("ell", [P, 2, W])
        ell_i = sb("ell_i", [P, 3, W], I32)
        src_idx = sb("src_idx", [P, W], I32)
        jslot = sb("jslot", [P, 2, W])
        pen = sb("pen", [P, NPO, W])
        hist_s = sb("hist_s", [P, LO])
        cnt4 = sb("cnt4", [P, 4, NPO])
        cnt = sb("cnt", [P, NPO])
        nleft = sb("nleft", [P, 2])
        nleft_i = sb("nleft_i", [1, 2], I32)

        hrow = sb("hrow", [P, NPO, ROW])
        adst = sb("adst", [P, HEADS, NPO])
        atmp = sb("atmp", [P, NPO, HE])
        last = sb("last", [P, ROW])
        amax = sb("amax", [P, HEADS, NPO])
        mx = sb("mx", [P, HEADS, NPO])
        mcur = sb("mcur", [P, HEADS, NPO])
        den = sb("den", [P, HEADS, NPO])
        acc = sb("acc", [P, HEADS, EXP, NPO])
        g1 = sb("g1", [P, HEADS, NPO])
        g2 = sb("g2", [P, HEADS, NPO])
        g4 = sb("g4", [P, HEADS, EXP, NPO])
        agg = sb("agg", [P, NPO, HE])
        gs = sb("gs", [P, 6, NPO])
        sc = sb("sc", [P, NPO, EXP])
        gate = sb("gate", [P, NPO, EXP])
        pause = sb("pause", [P, 4])
        left_row = sb("left_row", [P, ROW + 1])
        left_idx = sb("left_idx", [P, 2], I32)
        m8 = sb("m8", [P, 8])

        ar = Arena("arena", 26800)
        one_hi = ar(HI * HCH, BF16).rearrange("p (v e) -> p v e", v=HI)
        one_lo = ar(LO * HCH, BF16).rearrange("p (v e) -> p v e", v=LO)
        s_buf = [ar(K2 * SEQ).rearrange("p (k y x) -> p k y x", k=K2, x=WIDTH)]
        s_t = [ar(2 * K2 * P).rearrange("p (n q) -> p n q", n=2 * K2) for _ in range(2)]
        xk = [ar(2 * K2 * C).rearrange("p (t n) -> p t n", t=2) for _ in range(2)]
        wy = ar(NT * K2 * HEIGHT).rearrange("p (t k y) -> p t k y", t=NT, k=K2)
        ar.top = 0
        src_i = ar(EPP, I32)
        dst_i = ar(EPP, I32)
        e_tmp = ar(EPP)
        e_tm2 = ar(EPP)
        e_int = ar(EPP, I32)
        cw_b = [ar(TAPS * DI).rearrange("p (k c) -> p k c", k=TAPS) for _ in range(2)]
        x_dup = ar(NT * 2 * C).rearrange("p (t r c) -> p t r c", t=NT, r=2)
        om_t = s_t[1].rearrange("p n q -> p (n q)")[0:OM, 0:T]
        ar.top = 0
        xnt = ar(BATCH * SEQP).rearrange("p (b s) -> p b s", b=BATCH)
        x0_at = ar.top
        xs, zs, dtv, uu = ([ar(T)] for _ in range(4))
        bc3 = [ar(T, BF16) for _ in range(2)]
        loop_at = ar.top
        da = [ar(HALF) for _ in range(2)]
        hh = [ar(HALF) for _ in range(2)]
        gg = [ar(HALF) for _ in range(2)]
        x1_at = ar.top
        for x in (xs, zs, dtv, uu):
            x.append(ar(T))
        ar.top = loop_at
        r1 = ar(T, parts=64)
        sp_t = ar(T)
        sp_c = ar(T)
        ar.top = x0_at
        lnd, lsq, un = (ar(NT * C).rearrange("p (t c) -> p t c", t=NT) for _ in range(3))
        xn = ar(NT * 2 * C).rearrange("p (t r c) -> p t r c", t=NT, r=2)
        ar.top = x1_at
        look = ar(CAP * P, BF16).rearrange("p (c q) -> p c q", c=CAP)
        slot1 = ar(CAP * W, BF16).rearrange("p (c w) -> p c w", c=CAP)
        pay = ar(CAP * 2 * W, BF16).rearrange("p (c h w) -> p c h w", c=CAP, h=2)
        key_tmp = look.rearrange("p c q -> p (c q)")[:, 0:EPP + CAP]
        ar.top = 0
        vt = ar(T, parts=C)
        v_tok, d_tok = (ar(NT * C).rearrange("p (t c) -> p t c", t=NT) for _ in range(2))
        assert ar.top <= x0_at + T
        ar.top = x0_at + 2 * T
        a_e, b_e = (ar(HEADS * NPO * W).rearrange("p (h j w) -> p h j w", h=HEADS, j=NPO) for _ in range(2))
        hid = [ar(HID * 4) for _ in range(2)]
        eo = ar(NPO * EXP * C).rearrange("p (j e c) -> p j e c", j=NPO, e=EXP)
        assert ar.top <= x1_at
        left_p = b_e.rearrange("p h j w -> p (h j w)")[:, 0:EXP * NPO * LW].rearrange("p (x j w) -> p x j w", x=EXP, j=NPO)
        ar.top = x1_at
        left_w = ar(HEADS * NPO * LW).rearrange("p (h j w) -> p h j w", h=HEADS, j=NPO)
        assert ar.top <= x1_at + T
        ar.top = x1_at + 2 * T
        left_all = ar(P * (ROW + 1)).rearrange("p (e r) -> p e r", e=P)
        lk = ar(2 * P, I32).rearrange("p (a e) -> p a e", a=2)
        lkf = ar(2 * P).rearrange("p (a e) -> p a e", a=2)
        left_pen = ar(NPO * LW).rearrange("p (j w) -> p j w", j=NPO)
        cmp1, cmp2 = (ar(NPO * EXP * EXP).rearrange("p (j a b) -> p j a b", j=NPO, a=EXP) for _ in range(2))
        br = Arena("arena2", 10528)
        xpad = br(BATCH * (HEIGHT + 2) * (WIDTH + 2)).rearrange("p (b y x) -> p b y x", b=BATCH, x=WIDTH + 2)
        xc = br(T, parts=C).rearrange("p (b q) -> p b q", b=BATCH)
        wx = br(NT * K2 * WIDTH).rearrange("p (t k x) -> p t k x", t=NT, k=K2)
        s2_at = br.top
        s_buf.append(br(K2 * SEQ).rearrange("p (k y x) -> p k y x", k=K2, x=WIDTH))
        s_rows = [b.rearrange("p k y x -> p k (y x)") for b in s_buf]
        br.top = s2_at
        own1 = br(CAP * P, BF16).rearrange("p (c q) -> p c q", c=CAP)
        br.top = 0
        cs = [br(HALF) for _ in range(2)]
        resb = br(NPO * C).rearrange("p (j c) -> p j c", j=NPO)
        nb = br(W * ROW).rearrange("p (w r) -> p w r", w=W)
        t2 = br(NPO * C).rearrange("p (j c) -> p j c", j=NPO)
        res_d = nc.dram_tensor("res_scratch", [T, C], F32).ap()
        tab_d = nc.dram_tensor("node_rows", [T, ROW], F32).ap()
        cnt_d = nc.dram_tensor("hist_scratch", [4, T], F32).ap()
        left_d = nc.dram_tensor("left_scratch", [1, P * (ROW + 1)], F32).ap()

        names = """x_in edge_in wconv_in gb_in wmamba_in cw_in wffn_in att_in pool_step xdup_in ident_ready const_ready dve_step act_step
            xt_ready stats_ready pair_ready var_ready std_ready gn_ready xhat_ready xhat2_ready xc_ready
            omt_psum omt_ready om_ready om_read off_ready abs_step wx_ready
            hat_ready s_ready s2_ready st_psum st_ready xk_psum xk_ready conv_out t1_ready
            onehot_ready onehot_used hist_ready hist_out hist_back
            ln_var ln_std res_ready res_out res_back xn_ready xnt_psum xnt_ready taps_ready
            xs_psum xs_ready z_psum z_ready dbc_psum hi_ready rest_ready mid_ready bc_ready dt_psum
            sp_lin dtw_psum dtw_ready sp_step sp_ln dt_ready dt_free nega_ready diag_ready
            own_ready base_psum base_read pay_ready ell_psum idx_ready left_psum left_count left_known
            b_psum b_used c_psum c_used da_ready scan_ready c_ready g_ready g_used da_zero yg_ready
            t2_psum t2_ready v_ready vt_psum vt_ready h_psum h_ready tab_out last_in nb_in e_in exp_ready
            hid_psum hid_ready hid_used eo_psum eo_read gate_ready
            left_step pause_step left_idx_ready left_row_in left_key left_out left_in left_e left_exp out_ready out_done""".split()
        s = {n: sem(n) for n in names}
        block = ctx.enter_context(nc.Block())
        PRE = ("f_", "b_")
        edge_v = a["edges"].rearrange("r (p e) -> r p e", p=P)

        @block.sync
        def _(sp):
            x_tiles = a["x"].rearrange("(t p) c -> p t c", p=P)
            for r in range(2):
                sp.dma_start(x_dup[:, :, r, :], x_tiles).then_inc(s["xdup_in"], 16)
            om_k = a["om_kernel"].rearrange("(y x) c n -> x c y n", x=3)
            for r in range(2):
                sp.dma_start(w_om2[C * r:C * r + C], om_k[r]).then_inc(s["wconv_in"], 16)
            sp.dma_start(w_om1[:], om_k[2]).then_inc(s["wconv_in"], 16)
            sp.dma_start(b_om[:], a["om_bias"]).then_inc(s["wconv_in"], 16)
            sp.dma_start(w_cv[:], a["kernel"].rearrange("(k c) n -> c k n", c=C)).then_inc(s["wconv_in"], 16)
            sp.dma_start(b_cv[:], a["bias"]).then_inc(s["wconv_in"], 16)
            sp.dma_start(src_i, edge_v[0]).then_inc(s["edge_in"], 16)
            sp.dma_start(dst_i, edge_v[1]).then_inc(s["edge_in"], 16)
            sp.dma_start(x_tok[:], x_tiles).then_inc(s["x_in"], 16)
            for d, pre in enumerate(PRE):
                sp.dma_start(cw_b[d], a[pre + "conv_w"].to_broadcast([P, TAPS * DI])
                             .rearrange("p (k c) -> p k c", k=TAPS)).then_inc(s["cw_in"], 16)
                for r in range(2):
                    sp.dma_start(in_w[d][C * r:C * r + C, :], a[pre + "in_w"]).then_inc(s["cw_in"], 16)
            for d, pre in enumerate(PRE):
                sp.dma_start(vec[d][:], a[pre + "vec"]).then_inc(s["wmamba_in"], 16)
                sp.dma_start(xd_w[d][:], a[pre + "xd_w"]).then_inc(s["wmamba_in"], 16)
                for r in range(3):
                    sp.dma_start(xp_w[d][:, 32 * r:32 * r + 32], a[pre + "xp_w"][:, DTR:DTR + 2 * DS]).then_inc(s["wmamba_in"], 16)
                sp.dma_start(dp_w[d][:], a[pre + "dp_w"]).then_inc(s["wmamba_in"], 16)
                sp.dma_start(neg_a[d][:], a[pre + "a_log"]).then_inc(s["wmamba_in"], 16)
                sp.dma_start(o_w[d][:], a[pre + "o_w"]).then_inc(s["wmamba_in"], 16)
            for r in range(2):
                sp.dma_start(gb[C * r:C * r + C, :], a["ln_gb"]).then_inc(s["gb_in"], 16)
            sp.dma_start(w_gat[:], a["w_gat"]).then_inc(s["wffn_in"], 16)
            sp.dma_start(w1[:], a["w1"].rearrange("e c n -> c e n")).then_inc(s["wffn_in"], 16)
            sp.dma_start(b1[:], a["b1"]).then_inc(s["wffn_in"], 16)
            sp.dma_start(w2[:], a["w2"].rearrange("e h n -> h e n")).then_inc(s["wffn_in"], 16)
            sp.dma_start(b2[:], a["b2"]).then_inc(s["wffn_in"], 16)
            sp.dma_start(att[:].rearrange("p a n -> p (a n)"), a["att"].to_broadcast([P, 2 * HE])).then_inc(s["att_in"], 16)
            sp.dma_start(rows16[:].rearrange("p a n -> p (a n)"), a["rows16"].to_broadcast([P, 3 * HE])).then_inc(s["att_in"], 16)

            sp.wait_ge(s["hist_ready"], 1)
            sp.dma_start(cnt_d.rearrange("g (h l) -> (g h) l", l=LO), hist_s[:]).then_inc(s["hist_out"], 16)
            sp.wait_ge(s["hist_out"], 16)
            sp.dma_start(cnt4[:], cnt_d.rearrange("g (p j) -> p g j", p=P)).then_inc(s["hist_back"], 16)
            sp.wait_ge(s["res_ready"], 1)
            sp.dma_start(res_d.rearrange("(t p) c -> p t c", p=P), x_tok[:]).then_inc(s["res_out"], 16)
            sp.wait_ge(s["res_out"], 16)
            sp.wait_ge(s["t1_ready"], NT)
            sp.dma_start(resb, res_d.rearrange("(p j) c -> p j c", p=P)).then_inc(s["res_back"], 16)
            sp.wait_ge(s["h_ready"], 1)
            sp.dma_start(tab_d.rearrange("(p j) r -> p j r", p=P), hrow[:]).then_inc(s["tab_out"], 16)
            sp.wait_ge(s["tab_out"], 16)
            sp.dma_start(last[:], tab_d[LAST:T, :].to_broadcast([P, ROW])).then_inc(s["last_in"], 16)
            sp.wait_ge(s["out_ready"], 1)
            sp.dma_start(out.rearrange("(p j) c -> p j c", p=P), t2).then_inc(s["out_done"], 16)
            sp.wait_ge(s["out_done"], 16)

        @block.gpsimd
        def _(g):
            k = Link(g, s["pool_step"])
            k(g.memset(ident[:], 0.0))
            k(g.affine_select(out=ident[:], in_=ident[:], compare_op=ALU.not_equal, fill=1.0, base=0,
                              pattern=[[-1, P]], channel_multiplier=1))
            g.sem_inc(s["ident_ready"], 1)
            k(g.memset(ones_f[:], 1.0))
            k(g.memset(pairmat[:], 0.5))
            pv = pairmat[:].rearrange("p (g two) -> p g two", two=2)
            k(g.affine_select(out=pv, in_=pv, compare_op=ALU.is_ge, fill=0.0, base=0,
                              pattern=[[-2, P // 2], [0, 2]], channel_multiplier=1))
            k(g.affine_select(out=pv, in_=pv, compare_op=ALU.is_ge, fill=0.0, base=1,
                              pattern=[[2, P // 2], [0, 2]], channel_multiplier=-1))
            k(g.memset(xpad, 0.0))
            k(g.iota(iota_pi[:], pattern=[[0, 1]], base=0, channel_multiplier=1))
            for i2 in range(2):
                k(g.iota(iota_y[:, i2, :], pattern=[[1, 3], [0, 3], [-1, HEIGHT]], base=8 * i2 - 1, channel_multiplier=0,
                         allow_small_or_imprecise_dtypes=True))
            k(g.iota(iota_x[:], pattern=[[0, 3], [1, 3], [-1, WIDTH]], base=-1, channel_multiplier=0,
                     allow_small_or_imprecise_dtypes=True))
            k(g.iota(iota_n[:], pattern=[[1, P]], base=0, channel_multiplier=0, allow_small_or_imprecise_dtypes=True))
            k(g.iota(iota_j[:], pattern=[[1, NPO]], base=0, channel_multiplier=0, allow_small_or_imprecise_dtypes=True))
            k(g.memset(tri[:], 1.0))
            k(g.affine_select(out=tri[:], in_=tri[:], compare_op=ALU.is_gt, fill=0.0, base=0,
                              pattern=[[1, P]], channel_multiplier=-1))
            k(g.memset(sel[:], 0.0))
            for part in range(3):
                k(g.affine_select(out=sel[:], in_=sel[:], compare_op=ALU.not_equal, fill=1.0, base=-32 * part,
                                  pattern=[[-1, 32]], channel_multiplier=1))
            k(g.memset(tiebreak[:], 1.0))
            g.affine_select(out=tiebreak[:], in_=tiebreak[:], compare_op=ALU.is_gt, fill=0.0, base=0,
                            pattern=[[1, EXP], [-1, EXP]], channel_multiplier=0).then_inc(s["const_ready"], 1)

            for i in range(NT):
                if i % TPQ == 0:
                    g.wait_ge(s["wx_ready"], i // TPQ + 1)
                if i >= 2:
                    g.wait_ge(s["st_psum"], 3 * i - 3)
                kk = slice(K2 - POOL_TAPS, K2)
                g.tensor_tensor(s_buf[i % 2][:, kk], wy[:, i, kk].unsqueeze(3).to_broadcast([P, POOL_TAPS, HEIGHT, WIDTH]),
                                wx[:, i, kk].unsqueeze(2).to_broadcast([P, POOL_TAPS, HEIGHT, WIDTH]), ALU.mult).then_inc(s["s2_ready"], 1)
            for blk in range(4):
                with g.Fori(0, DS // 2) as it:
                    for e in range(2):
                        n = it * 2 + (16 * blk + e)
                        g.wait_ge(s["scan_ready"], n + 3)
                        g.wait_ge(s["c_ready"], n + 2)
                        g.wait_ge(s["g_used"], n + 1)
                        g.tensor_tensor(gg[e], hh[e], cs[e], ALU.mult).then_inc(s["g_ready"], 1)

            g.wait_ge(s["tab_out"], 16)
            g.wait_ge(s["idx_ready"], 1)
            for w in range(W):
                g.indirect_dma_start(out=nb[:, w, :], out_offset=None, in_=tab_d,
                                     in_offset=bass.IndirectOffsetOnAxis(ap=src_idx[:, w:w + 1], axis=0)).then_inc(s["nb_in"], 16)
            g.sem_inc(s["pause_step"], 1)
            g.wait_ge(s["left_known"], 1)
            rounds = g.value_load(nleft_i[0:1, 0:1], min_val=0, max_val=EPP)
            with g.If(rounds > 0):
                with g.Fori(0, rounds) as r:
                    with g.Fori(0, 8) as c:
                        n = r * 8 + c
                        g.wait_ge(s["left_idx_ready"], n + 1)
                        g.wait_ge(s["pause_step"], n * 3 + 1)
                        g.tensor_tensor(pause[:, 0:1], pause[:, 2:3], pause[:, 2:3], ALU.add).then_inc(s["pause_step"], 1)
                        g.indirect_dma_start(out=left_row[:, 0:ROW], out_offset=None, in_=tab_d,
                                             in_offset=bass.IndirectOffsetOnAxis(ap=left_idx[:, 0:1], axis=0)).then_inc(s["left_row_in"], 16)
                        g.wait_ge(s["left_row_in"], n * 16 + 16)
                        g.wait_ge(s["pause_step"], n * 3 + 2)
                        g.tensor_tensor(pause[:, 0:1], pause[:, 2:3], pause[:, 2:3], ALU.add).then_inc(s["pause_step"], 1)
                        g.dma_start(left_d.rearrange("o (p r) -> (o p) r", p=P), left_row[:]).then_inc(s["left_out"], 16)
                        g.wait_ge(s["left_out"], n * 16 + 16)
                        g.wait_ge(s["pause_step"], n * 3 + 3)
                        g.tensor_tensor(pause[:, 0:1], pause[:, 2:3], pause[:, 2:3], ALU.add).then_inc(s["pause_step"], 1)
                        g.dma_start(left_all.rearrange("p e r -> p (e r)"), left_d.to_broadcast([P, P * (ROW + 1)])).then_inc(s["left_in"], 16)
                        g.wait_ge(s["left_in"], n * 16 + 16)

        @block.tensor
        def _(pe):
            pe.wait_ge(s["ident_ready"], 1)
            pe.wait_ge(s["xdup_in"], 32)
            for i in range(NT):
                m = pe.transpose(ps[:, i // 4, (i % 4) * P:(i % 4) * P + P], x_dup[:, i].rearrange("p r c -> p (r c)"), ident[:])
                if i % 4 == 3:
                    m.then_inc(s["xt_ready"], 1)
            pe.wait_ge(s["const_ready"], 1)
            pe.wait_ge(s["stats_ready"], 1)
            pe.matmul(ps[:, 4, 0:2 * BATCH], pairmat[:], ms[:].rearrange("p b s -> p (b s)"), start=True, stop=True).then_inc(s["pair_ready"], 1)
            pe.wait_ge(s["wconv_in"], 96)

            def om_chunk(q):
                pe.wait_ge(s["xhat_ready"], 2 * q + 2)
                pe.wait_ge(s["xhat2_ready"], 2 * q + 2)
                if q >= 2:
                    pe.wait_ge(s["omt_ready"], q - 1)
                o = ps[0:OM, (4, 7)[q % 2], :]
                for ky in range(3):
                    pe.matmul(o, w_om2[:, ky, :], xpad[:, 2 * q:2 * q + 2, ky:ky + HEIGHT, 0:WIDTH], start=(ky == 0), stop=False)
                for ky in range(3):
                    m = pe.matmul(o, w_om1[:, ky, :], xpad[0:C, 2 * q:2 * q + 2, ky:ky + HEIGHT, 2:2 + WIDTH], start=False, stop=(ky == 2))
                m.then_inc(s["omt_psum"], 1)

            def om_turn(q):
                pe.wait_ge(s["omt_ready"], q + 1)
                if q >= 2:
                    pe.wait_ge(s["om_read"], q - 1)
                for i in range(TPQ):
                    m = pe.transpose(ps[:, 5 + q % 2, OM * i:OM * i + OM], om_t[:, P * (TPQ * q + i):P * (TPQ * q + i) + P], ident[0:OM, 0:OM])
                m.then_inc(s["om_ready"], 1)

            def xk_part(n):
                b, tau, hf = n // 4, (n // 2) % 2, n % 2
                if n >= 1:
                    pe.wait_ge(s["xk_ready"], n)
                pe.matmul(ps[:, 7, 0:288], xc[:, b, P * tau:P * tau + P],
                          w_cv[:].rearrange("p k n -> p (k n)")[:, 288 * hf:288 * hf + 288], start=True, stop=True).then_inc(s["xk_psum"], 1)

            def conv_tail(i):
                b = i // 2
                pe.wait_ge(s["st_ready"], 3 * i + 3)
                pe.wait_ge(s["xk_ready"], 4 * b + 4)
                if i >= 2:
                    pe.wait_ge(s["t1_ready"], i - 1)
                else:
                    pe.wait_ge(s["om_read"], OMQ)
                o = ps[:, 5 + i % 2, 0:C]
                pe.matmul(o, ones_f[:], b_cv[:], start=True, stop=False)
                for t in range(K2):
                    for tau in range(2):
                        m = pe.matmul(o, s_t[i % 2][:, 2 * t + tau, :], xk[b % 2][:, tau, C * t:C * t + C],
                                      start=False, stop=(t == K2 - 1 and tau == 1))
                m.then_inc(s["conv_out"], 1)

            def hist_chunk(ch):
                pe.wait_ge(s["onehot_ready"], ch + 1)
                for e in range(0, CHUNKS[ch][1], 4):
                    for q in range(4):
                        m = pe.matmul(ps[32 * q:32 * q + 32, 4, 0:LO], one_hi[:, :, e + q], one_lo[:, :, e + q],
                                      start=(ch == 0 and e == 0), stop=(ch == len(CHUNKS) - 1 and e == CHUNKS[ch][1] - 4),
                                      tile_position=(0, 32 * q))
                m.then_inc(s["onehot_used"], 1)

            om_chunk(0)
            om_chunk(1)
            om_turn(0)
            om_chunk(2)
            om_turn(1)
            om_chunk(3)
            om_turn(2)
            om_turn(3)
            pe.wait_ge(s["xc_ready"], 1)
            for n in range(4):
                xk_part(n)
            for i in range(NT):
                pe.wait_ge(s["s_ready"], i + 1)
                pe.wait_ge(s["s2_ready"], i + 1)
                for q in range(3):
                    n = 3 * i + q
                    if n >= 2:
                        pe.wait_ge(s["st_ready"], n - 1)
                    for v in range(6):
                        t = 6 * q + v
                        m = pe.transpose(ps[:, 2 * (n % 2) + v // 4, (v % 4) * P:(v % 4) * P + P],
                                         s_rows[i % 2][:, t // 2, (t % 2) * P:(t % 2) * P + P], ident[:])
                    m.then_inc(s["st_psum"], 1)
                if i < NT - 2:
                    xk_part(4 + 2 * i)
                if i:
                    conv_tail(i - 1)
                if i < NT - 2:
                    xk_part(5 + 2 * i)
                if i % 2 == 0 and 1 <= i // 2 <= len(CHUNKS):
                    hist_chunk(i // 2 - 1)
            conv_tail(NT - 1)

            pe.wait_ge(s["xn_ready"], 1)
            for i in range(NT):
                m = pe.transpose(ps[:, i // 4, (i % 4) * P:(i % 4) * P + P], xn[:, i, :, :].rearrange("p r c -> p (r c)"), ident[:])
            m.then_inc(s["xnt_psum"], 1)
            pe.wait_ge(s["own_ready"], 1)
            for c in range(CAP):
                m = pe.matmul(ps[:, 5, 0:P], tri[:], own1[:, c, :], start=(c == 0), stop=(c == CAP - 1))
            m.then_inc(s["base_psum"], 1)
            pe.wait_ge(s["xnt_ready"], 2)
            pe.wait_ge(s["taps_ready"], 4)
            pe.wait_ge(s["wmamba_in"], 2 * 8 * 16)
            for d in range(2):
                pe.matmul(ps[:, 7, DI * d:DI * d + DI], xd_w[d][:], dp_w[d][:], start=True, stop=True).then_inc(s["dtw_psum"], 1)

            def project_x(d):
                for hf in range(2):
                    if d:
                        pe.wait_ge(s["rest_ready"], hf + 1)
                    for q in (2 * hf, 2 * hf + 1):
                        for j in range(TAPS // 2):
                            shift = 2 * j if d == 0 else TAPS + 1 - 2 * j
                            m = pe.matmul(ps[:, q, :], w_tap[d][:, j, :], xnt[:, 2 * q:2 * q + 2, shift:shift + SEQ],
                                          start=(j == 0), stop=(j == TAPS // 2 - 1))
                    m.then_inc(s["xs_psum"], 1)

            def project_z(d):
                for hf in range(2):
                    if d:
                        pe.wait_ge(s["sp_lin"], hf + 1)
                    for q in (2 * hf, 2 * hf + 1):
                        m = pe.matmul(ps[:, 4 + q, :], in_w[d][0:C, DI:2 * DI], xnt[0:C, 2 * q:2 * q + 2, TAPS - 1:TAPS - 1 + SEQ],
                                      start=True, stop=True)
                    m.then_inc(s["z_psum"], 1)

            def project_bc_dt(d):
                for hf in range(2):
                    pe.wait_ge(s["xs_ready"], 2 * d + hf + 1)
                    for q in (2 * hf, 2 * hf + 1):
                        m = pe.matmul(ps[0:96, q, :], xp_w[d][:], xs[d][:, 512 * q:512 * q + 512], start=True, stop=True)
                    m.then_inc(s["dbc_psum"], 1)
                for hf in range(2):
                    pe.wait_ge(s["z_ready"], 2 * d + hf + 1)
                    for q in (2 * hf, 2 * hf + 1):
                        m = pe.matmul(ps[:, 4 + q, :], dt_w[d][:], xs[d][:, 512 * q:512 * q + 512], start=True, stop=True)
                    m.then_inc(s["dt_psum"], 1)

            project_x(0)
            pe.wait_ge(s["base_read"], 1)
            pe.wait_ge(s["dtw_ready"], 2)
            project_z(0)
            project_bc_dt(0)
            pe.wait_ge(s["rest_ready"], 1)
            pe.wait_ge(s["pay_ready"], 1)
            for c in range(CAP):
                m = pe.matmul(ps[:, 0, 0:2 * W], own1[:, c, :], pay[:, c, :, :].rearrange("p h w -> p (h w)"),
                              start=(c == 0), stop=(c == CAP - 1))
            m.then_inc(s["ell_psum"], 1)
            pe.wait_ge(s["left_count"], 1)
            pe.transpose(ps[0:1, 1, 0:P], nleft[:, 0:1], ident[:]).then_inc(s["left_psum"], 1)
            project_z(1)
            pe.wait_ge(s["idx_ready"], 1)
            pe.wait_ge(s["left_known"], 1)
            project_x(1)
            project_bc_dt(1)

            def rows(d, hf, i0, n, e):
                pe.wait_ge(s["b_used"], n + 1)
                for q in range(2):
                    m = pe.matmul(ps[:, 6 * e + q, :], sel[:, i0].to_broadcast([96, P]),
                                  bc3[d][0:96, hf * HALF + 512 * q:hf * HALF + 512 * q + 512], start=True, stop=True)
                m.then_inc(s["b_psum"], 1)

            def rows_c(d, hf, i0, n):
                pe.wait_ge(s["c_ready"], n + 1)
                for q in range(2):
                    m = pe.matmul(ps[:, 2 + q, :], sel[:, i0].to_broadcast([96, P]),
                                  bc3[d][0:96, hf * HALF + 512 * q:hf * HALF + 512 * q + 512], start=True, stop=True)
                m.then_inc(s["c_psum"], 1)

            def add_state(n, e):
                pe.wait_ge(s["g_ready"], n + 3)
                for q in range(2):
                    m = pe.matmul(ps[:, 4 + q, :], ident[:], gg[e][:, 512 * q:512 * q + 512], start=False, stop=True, skip_group_check=True)
                m.then_inc(s["g_used"], 1)

            def first_rows(blk):
                d, hf = blk // 2, blk % 2
                for e in range(2):
                    rows(d, hf, slice(e, e + 1), 16 * blk + e, e)
                    rows_c(d, hf, slice(DS + e, DS + e + 1), 16 * blk + e)

            pe.wait_ge(s["sp_lin"], 4)
            pe.wait_ge(s["rest_ready"], 4)
            pe.wait_ge(s["diag_ready"], 2)
            pe.wait_ge(s["bc_ready"], 2)
            first_rows(0)
            for blk in range(4):
                d, hf = blk // 2, blk % 2
                if blk:
                    pe.wait_ge(s["yg_ready"], blk)
                for q in range(2):
                    c0 = hf * HALF + 512 * q
                    pe.matmul(ps[:, 4 + q, :], diag_d[d][:], xs[d][:, c0:c0 + 512], start=True, stop=True)
                with pe.Fori(0, DS // 2 - 1) as it:
                    for e in range(2):
                        n = it * 2 + (16 * blk + e)
                        rows(d, hf, bass.ds(it * 2 + (2 + e), 1), n + 2, e)
                        rows_c(d, hf, bass.ds(it * 2 + (DS + 2 + e), 1), n + 2)
                        add_state(n, e)
                if blk < 3:
                    first_rows(blk + 1)
                for e in range(2):
                    add_state(16 * blk + DS - 2 + e, e)

            pe.wait_ge(s["yg_ready"], 4)
            for j in range(NPO):
                o = ps[:, 0 + j // 8, C * (j % 8):C * (j % 8) + C]
                for d in range(2):
                    m = pe.matmul(o, zs[d][:, j:T:NPO], o_w[d][:], start=(d == 0), stop=(d == 1))
            m.then_inc(s["t2_psum"], 1)
            pe.wait_ge(s["v_ready"], 1)
            for j in range(NPO):
                m = pe.transpose(ps[0:C, 4 + j // 4, (j % 4) * P:(j % 4) * P + P], v_tok[:, j, :], ident[:])
            m.then_inc(s["vt_psum"], 1)
            pe.wait_ge(s["vt_ready"], 1)
            pe.wait_ge(s["wffn_in"], 80)
            for j in range(NPO):
                m = pe.matmul(ps[:, 2, HE * j:HE * j + HE], vt[:, P * j:P * j + P], w_gat[:], start=True, stop=True)
            m.then_inc(s["h_psum"], 1)
            def expert_out(n):
                q, e = n // EXP, n % EXP
                if e == 0:
                    if q >= 2:
                        pe.wait_ge(s["eo_read"], q - 1)
                    if q == 1:
                        pe.wait_ge(s["vt_ready"], 1)
                    for bank in range(2):
                        pe.matmul(ps[:, 4 * (q % 2) + bank, :], ones_f[:], b2[:].unsqueeze(1).to_broadcast([1, 2, EXP * C]), start=True, stop=True)
                pe.wait_ge(s["hid_ready"], n + 1)
                for jj in range(4):
                    o = 256 * (jj % 2) + C * e
                    m = pe.matmul(ps[:, 4 * (q % 2) + jj // 2, o:o + C], hid[n % 2][:, P * jj:P * jj + P], w2[:, e, :],
                                  start=False, stop=True, skip_group_check=True)
                m.then_inc(s["eo_psum"], 1)

            for n in range(4 * EXP):
                q, e = n // EXP, n % EXP
                if n >= 2:
                    pe.wait_ge(s["hid_ready"], n - 1)
                pe.matmul(ps[:, 6 + n % 2, :], w1[:, e, :], vt[:, 512 * q:512 * q + 512], start=True, stop=True).then_inc(s["hid_psum"], 1)
                if n:
                    expert_out(n - 1)
            expert_out(4 * EXP - 1)

        @block.scalar
        def _(act):
            f = act.activation
            k = Link(act, s["act_step"])
            act.wait_ge(s["var_ready"], 1)
            f(gnv[:, 1, :], gnv[:, 0, :], ACT.Sqrt).then_inc(s["std_ready"], 1)
            act.wait_ge(s["const_ready"], 1)
            act.wait_ge(s["gn_ready"], 1)
            for b in range(BATCH):
                f(xpad[C:P, b, 1:1 + HEIGHT, 0:WIDTH], ps[C:P, b // 2, (b % 2) * SEQ:(b % 2) * SEQ + SEQ].rearrange("p (y x) -> p y x", x=WIDTH),
                  ACT.Identity, scale=gnv[C:P, 1, b:b + 1], bias=gnv[C:P, 2, b:b + 1]).then_inc(s["xhat2_ready"], 1)
            act.wait_ge(s["xhat_ready"], BATCH)
            f(xc.rearrange("p b (y x) -> p b y x", x=WIDTH), xpad[0:C, :, 1:1 + HEIGHT, 1:1 + WIDTH], ACT.Copy).then_inc(s["xc_ready"], 1)

            def om_copy(q):
                act.wait_ge(s["omt_psum"], q + 1)
                f(om_t[:, 512 * q:512 * q + 512], ps[0:OM, (4, 7)[q % 2], :], ACT.Identity, bias=b_om[:]).then_inc(s["omt_ready"], 1)

            def hats(q):
                ii = slice(TPQ * q, TPQ * q + TPQ)
                act.wait_ge(s["off_ready"], q + 1)
                f(wx[:, ii], wx[:, ii], ACT.Abs, bias=pl[:]).then_inc(s["abs_step"], 1)
                f(wy[:, ii], wy[:, ii], ACT.Abs, bias=ph[:]).then_inc(s["abs_step"], 1)
                act.wait_ge(s["abs_step"], 2 * q + 1)
                f(wx[:, ii], wx[:, ii], ACT.Relu, scale=-1.0, bias=1.0)
                act.wait_ge(s["abs_step"], 2 * q + 2)
                f(wy[:, ii], wy[:, ii], ACT.Relu, scale=-1.0, bias=1.0)
                f(msk[:, ii], om[:, ii, 2 * K2:OM], ACT.Sigmoid).then_inc(s["hat_ready"], 1)

            om_copy(0)
            om_copy(1)
            hats(0)
            om_copy(2)
            om_copy(3)
            for q in range(1, OMQ):
                hats(q)

            def xk_copy(n):
                        b, tau, hf = n // 4, (n // 2) % 2, n % 2
                        act.wait_ge(s["xk_psum"], n + 1)
                        if b >= 2:
                            act.wait_ge(s["conv_out"], 2 * b - 2)
                        f(xk[b % 2][:, tau, 288 * hf:288 * hf + 288], ps[:, 7, 0:288], ACT.Copy).then_inc(s["xk_ready"], 1)

            for n in range(4):
                xk_copy(n)
            for i in range(NT):
                if i >= 2:
                    act.wait_ge(s["conv_out"], i - 1)
                for q in range(3):
                    n = 3 * i + q
                    act.wait_ge(s["st_psum"], n + 1)
                    f(s_t[i % 2][:, 6 * q:6 * q + 6, :].rearrange("p n q -> p (n q)"), banks(2 * (n % 2), 2)[:, 0:6 * P], ACT.Copy).then_inc(s["st_ready"], 1)
                if i < NT - 2:
                    xk_copy(4 + 2 * i)
                    xk_copy(5 + 2 * i)
            act.wait_ge(s["ln_var"], 1)
            f(lns[:, 4, :], lns[:, 3, :], ACT.Sqrt).then_inc(s["ln_std"], 1)
            act.wait_ge(s["ln_var"], 2)
            f(lns[:, 4, :], lns[:, 3, :], ACT.Sqrt).then_inc(s["ln_std"], 1)
            act.wait_ge(s["xnt_psum"], 1)
            act.wait_ge(s["gb_in"], 32)
            act.wait_ge(s["da_zero"], 1)
            for r in range(2):
                rr = slice(C * r, C * r + C)
                f(xnt[rr, :, TAPS - 1 - r:TAPS - 1 - r + SEQ], ps[rr, 0:4, :].rearrange("p b n -> p (b n)").rearrange("p (b s) -> p b s", b=BATCH),
                  ACT.Identity, scale=gb[rr, 0:1], bias=gb[rr, 1:2]).then_inc(s["xnt_ready"], 1)
            act.wait_ge(s["wmamba_in"], 2 * 8 * 16)
            for d in range(2):
                f(neg_a[d][:], neg_a[d][:], ACT.Exp).then_inc(s["nega_ready"], 1)
            for d in range(2):
                act.wait_ge(s["dtw_psum"], 2)
                f(dt_w[d][:], ps[:, 7, DI * d:DI * d + DI], ACT.Copy).then_inc(s["dtw_ready"], 1)
            for d in range(2):
                cols = [slice(HALF * hf, HALF * hf + HALF) for hf in range(2)]
                for part in ((0, 1) if d == 0 else (1, 0)):
                    for hf in range(2):
                        if part == 0:
                            act.wait_ge(s["xs_psum"], 2 * d + hf + 1)
                            f(xs[d][:, cols[hf]], banks(2 * hf, 2), ACT.Silu, bias=vec[d][:, 0:1]).then_inc(s["xs_ready"], 1)
                        else:
                            act.wait_ge(s["z_psum"], 2 * d + hf + 1)
                            f(zs[d][:, cols[hf]], banks(4 + 2 * hf, 2), ACT.Silu).then_inc(s["z_ready"], 1)
                for hf in range(2):
                    act.wait_ge(s["dbc_psum"], 2 * d + hf + 1)
                    f(bc3[d][0:96, cols[hf]], banks(2 * hf, 2, 96), ACT.Copy).then_inc(s["hi_ready"], 1)
                if d:
                    act.wait_ge(s["dt_ready"], d)
                for hf in range(2):
                    act.wait_ge(s["dt_psum"], 2 * d + hf + 1)
                    f(dtv[d][:, cols[hf]], banks(4 + 2 * hf, 2), ACT.Relu, bias=vec[d][:, 1:2]).then_inc(s["sp_step"], 1)
                    f(sp_t[:, cols[hf]], banks(4 + 2 * hf, 2), ACT.Abs, bias=vec[d][:, 1:2]).then_inc(s["sp_lin"], 1)
                act.wait_ge(s["sp_lin"], 2 * d + 2)
                f(sp_t, sp_t, ACT.Exp, scale=-1.0).then_inc(s["sp_step"], 1)
                act.wait_ge(s["sp_step"], 3 * d + 3)
                f(uu[d], sp_t, ACT.Ln, bias=1.0).then_inc(s["sp_ln"], 1)
                act.wait_ge(s["rest_ready"], 2 * d + 2)
                f(bc3[d][0:64, :], r1, ACT.Copy).then_inc(s["mid_ready"], 1)
            for d in range(2):
                act.wait_ge(s["dt_ready"], d + 1)
                act.wait_ge(s["da_zero"], 2 + d)
                lo = 1 - d
                for hf in range(2):
                    blk, c0 = 2 * d + hf, hf * HALF
                    src = dtv[d][:, c0:c0 + HALF].rearrange("p (b s) -> p b s", s=SEQ)[:, :, lo:lo + SEQ - 1]
                    with act.Fori(0, DS // 2) as it:
                        for e in range(2):
                            n = it * 2 + (16 * blk + e)
                            act.wait_ge(s["scan_ready"], n + 1)
                            f(da[e].rearrange("p (b s) -> p b s", s=SEQ)[:, :, lo:lo + SEQ - 1], src, ACT.Exp,
                              scale=neg_a[d][:, bass.ds(it * 2 + e, 1)]).then_inc(s["da_ready"], 1)
                            act.wait_ge(s["c_psum"], n + 1)
                            act.wait_ge(s["g_ready"], n + 1)
                            f(cs[e], banks(2, 2), ACT.Copy).then_inc(s["c_ready"], 1)
            act.wait_ge(s["ln_var"], 3)
            f(lns[:, 4, :], lns[:, 3, :], ACT.Sqrt).then_inc(s["ln_std"], 1)
            act.wait_ge(s["vt_psum"], 1)
            f(vt, banks(4, 4, C), ACT.Copy).then_inc(s["vt_ready"], 1)
            for n in range(4 * EXP):
                q, e = n // EXP, n % EXP
                act.wait_ge(s["hid_psum"], n + 1)
                if n >= 2:
                    act.wait_ge(s["eo_psum"], n - 1)
                f(hid[n % 2], ps[:, 6 + n % 2, :], ACT.Gelu, bias=b1[:, e:e + 1]).then_inc(s["hid_ready"], 1)
                if e == 0 and q:
                    act.wait_ge(s["eo_psum"], 4 * q)
                    f(eo[:, 4 * q - 4:4 * q].rearrange("p j e c -> p (j e c)"), banks(4 * ((q - 1) % 2), 2), ACT.Copy).then_inc(s["eo_read"], 1)
            act.wait_ge(s["eo_psum"], 4 * EXP)
            f(eo[:, 12:16].rearrange("p j e c -> p (j e c)"), banks(4, 2), ACT.Copy).then_inc(s["eo_read"], 1)
            act.wait_ge(s["e_in"], 1)
            f(g1[:], g1[:], ACT.Exp).then_inc(s["exp_ready"], 1)
            f(g2[:], g2[:], ACT.Exp).then_inc(s["exp_ready"], 1)
            act.wait_ge(s["e_in"], 2)
            f(a_e, a_e, ACT.Exp).then_inc(s["exp_ready"], 1)
            rounds = act.value_load(nleft_i[0:1, 0:1], min_val=0, max_val=EPP)
            with act.If(rounds > 0):
                with act.Fori(0, rounds) as r:
                    with act.Fori(0, 8 * (P // LW)) as c:
                        n = r * (8 * (P // LW)) + c
                        act.wait_ge(s["left_e"], n + 1)
                        f(g1[:], g1[:], ACT.Exp).then_inc(s["left_exp"], 1)
                        f(left_w, left_w, ACT.Exp).then_inc(s["left_exp"], 1)
            act.wait_ge(s["ln_var"], 4)
            f(gs[:, 4, :], gs[:, 3, :], ACT.Sqrt).then_inc(s["ln_std"], 1)
            act.wait_ge(s["ln_var"], 5)
            f(gate[:], gate[:], ACT.Exp).then_inc(s["ln_std"], 1)

        @block.vector
        def _(v):
            k = Link(v, s["dve_step"])

            def bc(ap, axis, n):
                shape = list(ap.unsqueeze(axis).shape)
                shape[axis] = n
                return ap.unsqueeze(axis).to_broadcast(shape)

            tt, ts, stt = v.tensor_tensor, v.tensor_scalar, v.scalar_tensor_tensor

            v.sem_inc(s["b_used"], 2)
            v.sem_inc(s["c_ready"], 1)
            v.sem_inc(s["g_ready"], 2)
            v.sem_inc(s["g_used"], 2)
            v.sem_inc(s["scan_ready"], 2)

            v.memset(pause[:], 0.0)
            for b in range(BATCH):
                if b % 2 == 0:
                    v.wait_ge(s["xt_ready"], b // 2 + 1)
                k.go(v.bn_stats(out=st6[:, b, :], in_=ps[:, b // 2, (b % 2) * SEQ:(b % 2) * SEQ + SEQ]))
            k.wait()
            for b in range(BATCH):
                k.go(v.bn_aggr(out=mv[:, b, :], in_=st6[:, b, :]))
            k.wait()
            k(v.tensor_copy(ms[:, :, 0], mv[:, :, 0]))
            k(tt(ms[:, :, 1], mv[:, :, 0], mv[:, :, 0], ALU.mult))
            tt(ms[:, :, 1], ms[:, :, 1], mv[:, :, 1], ALU.add).then_inc(s["stats_ready"], 1)
            v.wait_ge(s["pair_ready"], 1)
            k(v.tensor_copy(gnm[:].rearrange("p b s -> p (b s)"), ps[:, 4, 0:2 * BATCH]))
            k(tt(gnv[:, 0, :], gnm[:, :, 0], gnm[:, :, 0], ALU.mult))
            k(tt(gnv[:, 0, :], gnm[:, :, 1], gnv[:, 0, :], ALU.subtract))
            ts(gnv[:, 0, :], gnv[:, 0, :], 1e-5, None, ALU.add).then_inc(s["var_ready"], 1)
            v.wait_ge(s["std_ready"], 1)
            k(v.reciprocal(gnv[:, 1, :], gnv[:, 1, :]))
            stt(out=gnv[:, 2, :], in0=gnm[:, :, 0], scalar=-1.0, in1=gnv[:, 1, :], op0=ALU.mult, op1=ALU.mult).then_inc(s["gn_ready"], 1)
            v.wait_ge(s["const_ready"], 1)
            for b in range(BATCH):
                ts(xpad[0:C, b, 1:1 + HEIGHT, 1:1 + WIDTH], ps[0:C, b // 2, (b % 2) * SEQ:(b % 2) * SEQ + SEQ].rearrange("p (y x) -> p y x", x=WIDTH),
                   gnm[0:C, b, 0:1], gnv[0:C, 1, b:b + 1], ALU.subtract, ALU.mult).then_inc(s["xhat_ready"], 1)
            k(ts(pi_tmp[:, 0:1], iota_pi[:], 4, None, ALU.arith_shift_right))
            k(ts(pi_tmp[:, 1:2], iota_pi[:], 15, None, ALU.bitwise_and))
            k(v.tensor_copy(ph[:], pi_tmp[:, 0:1]))
            k(v.tensor_copy(pl[:], pi_tmp[:, 1:2]))
            k(v.tensor_copy(pf[:], iota_pi[:]))
            v.wait_ge(s["cw_in"], 96)
            for d in range(2):
                for r in range(2):
                    rr, tap = slice(C * r, C * r + C), (r if d == 0 else 1 - r)
                    tt(w_tap[d][rr], bc(in_w[d][rr, 0:DI], 1, TAPS // 2), cw_b[d][rr, tap:TAPS:2, :], ALU.mult).then_inc(s["taps_ready"], 1)
            v.wait_ge(s["wmamba_in"], 2 * 8 * 16)
            for d in range(2):
                ts(diag_d[d][:], ident[:], vec[d][:, 2:3], None, ALU.mult).then_inc(s["diag_ready"], 1)

            v.wait_ge(s["edge_in"], 32)
            k.go(v.tensor_copy(e_tmp, src_i))
            k.go(v.tensor_copy(e_tm2, dst_i))
            k(ts(e_int, dst_i, LO - 1, None, ALU.bitwise_and))
            k(stt(out=keys[:, 0:EPP], in0=e_tm2, scalar=float(T), in1=e_tmp, op0=ALU.mult, op1=ALU.add))

            def offsets(q):
                ii = slice(TPQ * q, TPQ * q + TPQ)
                v.wait_ge(s["om_ready"], q + 1)
                k(v.tensor_copy(om[:, ii].rearrange("p t n -> p (t n)"), ps[:, 5 + q % 2, 0:TPQ * OM]))
                v.sem_inc(s["om_read"], 1)
                for i2 in range(2):
                    jj = slice(TPQ * q + i2, TPQ * q + TPQ, 2)
                    k.go(tt(wy[:, jj], bc(om[:, jj, 0:2 * K2:2], 3, HEIGHT),
                            bc(iota_y[:, i2, :].rearrange("p (k y) -> p k y", k=K2), 1, TPQ // 2), ALU.add))
                tt(wx[:, ii], bc(om[:, ii, 1:2 * K2:2], 3, WIDTH), bc(iota_x[:], 1, TPQ), ALU.add).then_inc(s["off_ready"], 1)

            def masks(q):
                ii = slice(TPQ * q, TPQ * q + TPQ)
                v.wait_ge(s["hat_ready"], q + 1)
                k(ts(msk[:, ii], msk[:, ii], 2.0, None, ALU.mult))
                tt(wx[:, ii], wx[:, ii], bc(msk[:, ii], 3, WIDTH), ALU.mult).then_inc(s["wx_ready"], 1)

            k(ts(e_tmp, e_tmp, float(LAST), None, ALU.is_lt))
            k.go(stt(out=lo_b[:], in0=e_tmp, scalar=float(LO), in1=e_int, op0=ALU.mult, op1=ALU.add))
            k(stt(out=e_tm2, in0=e_tm2, scalar=float(T), in1=e_tmp, op0=ALU.is_lt, op1=ALU.mult))
            k(stt(out=keys[:, 0:EPP], in0=keys[:, 0:EPP], scalar=1.0, in1=e_tm2, op0=ALU.add, op1=ALU.mult))
            k(ts(e_int, dst_i, 6, None, ALU.arith_shift_right))
            k.go(v.tensor_copy(hi_b[:], e_int))
            offsets(0)

            def conv_sum(i):
                v.wait_ge(s["conv_out"], i + 1)
                tt(x_tok[:, i, :], x_tok[:, i, :], ps[:, 5 + i % 2, 0:C], ALU.add).then_inc(s["t1_ready"], 1)

            def onehots(ch, part):
                e0, en = CHUNKS[ch]
                if ch and part == 0:
                    v.wait_ge(s["onehot_used"], ch)
                for x in range(part * (HI + LO) // 2, (part + 1) * (HI + LO) // 2):
                    if x < HI:
                        m = ts(one_hi[:, x, 0:en], hi_b[:, e0:e0 + en], float(x), None, ALU.is_equal)
                    else:
                        m = ts(one_lo[:, x - HI, 0:en], lo_b[:, e0:e0 + en], float(x - HI), None, ALU.is_equal)
                    if x < HI + LO - 1:
                        k.go(m)
                    else:
                        m.then_inc(s["onehot_ready"], 1)

            def extract(r):
                k(v.max(out=comp[:, 8 * r:8 * r + 8], in_=keys[:, 0:EPP]))
                k.go(v.match_replace(out=keys[:, 0:EPP], in_to_replace=comp[:, 8 * r:8 * r + 8], in_values=keys[:, 0:EPP], imm_value=0.0))

            for i in range(NT):
                if i % TPQ == 0:
                    masks(i // TPQ)
                    v.wait_ge(s["wx_ready"], i // TPQ + 1)
                if i >= 2:
                    v.wait_ge(s["st_psum"], 3 * i - 3)
                kk = slice(0, K2 - POOL_TAPS)
                tt(s_buf[i % 2][:, kk], bc(wy[:, i, kk], 3, WIDTH), bc(wx[:, i, kk], 2, HEIGHT), ALU.mult).then_inc(s["s_ready"], 1)
                if i == 0:
                    for q in range(1, OMQ):
                        offsets(q)
                if i >= 3:
                    conv_sum(i - 3)
                if i % 2 and 1 <= i // 2 <= ROUNDS:
                    k.wait()
                    extract(i // 2 - 1)
                if 1 <= i <= 2 * len(CHUNKS):
                    onehots((i - 1) // 2, (i - 1) % 2)
            k.wait()
            k(ts(key_i[:], comp, -1.0, None, ALU.add))
            k(ts(int_a[:, 0, :], key_i[:], 15, None, ALU.arith_shift_right))
            k(v.tensor_copy(owner[:], int_a[:, 0, :]))
            k(v.tensor_copy(owner_b[:], owner[:]))
            k(ts(int_a[:, 0, :], key_i[:], 4, 127, ALU.arith_shift_right, ALU.bitwise_and))
            k(ts(dig[:, 0, :], int_a[:, 0, :], 1.0, None, ALU.add))
            k(ts(int_a[:, 1, :], key_i[:], 11, 15, ALU.arith_shift_right, ALU.bitwise_and))
            k(ts(int_a[:, 2, :], key_i[:], 15, None, ALU.bitwise_and))
            k(stt(out=dig[:, 1, :], in0=int_a[:, 2, :], scalar=16.0, in1=int_a[:, 1, :], op0=ALU.mult, op1=ALU.add))
            k(v.memset(same[:, 0:1], 0.0))
            k(tt(same[:, 1:CAP], owner[:, 1:CAP], owner[:, 0:CAP - 1], ALU.is_equal))
            k(v.tensor_tensor_scan(run[:], same[:], same[:], 0.0, ALU.mult, ALU.add))
            for i in range(NT - 3, NT):
                conv_sum(i)
            v.wait_ge(s["onehot_used"], len(CHUNKS))
            v.tensor_copy(hist_s[:], ps[:, 4, 0:LO]).then_inc(s["hist_ready"], 1)
            v.wait_ge(s["t1_ready"], NT)

            def norm(dst, src, diff, sq, st, n, width, out_sem):
                k(v.tensor_reduce(out=st[:, 0, :], in_=src, axis=AX, op=ALU.add))
                k(ts(st[:, 1, :], st[:, 0, :], 1.0 / width, None, ALU.mult))
                k(tt(diff, src, bc(st[:, 1, :], 2, width), ALU.subtract))
                k(tt(sq, diff, diff, ALU.mult))
                k(v.tensor_reduce(out=st[:, 2, :], in_=sq, axis=AX, op=ALU.add))
                ts(st[:, 3, :], st[:, 2, :], 1.0 / width, 1e-5, ALU.mult, ALU.add).then_inc(s["ln_var"], 1)
                v.wait_ge(s["ln_std"], n)
                k(v.reciprocal(st[:, 5, :], st[:, 4, :]))
                m = tt(dst, diff, bc(st[:, 5, :], 2, width), ALU.mult)
                if out_sem is None:
                    k(m)
                else:
                    m.then_inc(out_sem, 1)

            norm(un, x_tok[:], lnd, lsq, lns, 1, C, None)
            tt(x_tok[:], x_tok[:], un, ALU.add).then_inc(s["res_ready"], 1)
            norm(xn[:, :, 0, :], un, lnd, lsq, lns, 2, C, None)
            v.tensor_copy(xn[:, :, 1, :], xn[:, :, 0, :]).then_inc(s["xn_ready"], 1)
            for r in range(2):
                rr = slice(C * r, C * r + C)
                k(v.memset(xnt[rr, :, 0:TAPS - 1 - r], 0.0))
                m = v.memset(xnt[rr, :, TAPS - 1 - r + SEQ:SEQP], 0.0)
                if r:
                    m.then_inc(s["da_zero"], 1)
                else:
                    k(m)
            v.wait_ge(s["nega_ready"], 2)
            for d in range(2):
                k(ts(neg_a[d][:], neg_a[d][:], -1.0, None, ALU.mult))

            tt(own1, bc(iota_n[:], 1, CAP), bc(owner_b[:], 2, P), ALU.is_equal).then_inc(s["own_ready"], 1)
            v.wait_ge(s["base_psum"], 1)
            k(ts(base_b[:], ps[:, 5, 0:P], float(P), None, ALU.min))
            v.sem_inc(s["base_read"], 1)
            k(tt(look, own1, bc(base_b[:], 1, CAP), ALU.mult))
            k(v.tensor_reduce(out=slot[:], in_=look, axis=AX, op=ALU.add))
            k(tt(slot[:], slot[:], run[:], ALU.add))
            k(tt(slot1, bc(iota_n[:, 0:W], 1, CAP), bc(slot[:], 2, W), ALU.is_equal))
            k(tt(pay[:, :, 0, :], slot1, bc(dig[:, 0, :], 2, W), ALU.mult))
            tt(pay[:, :, 1, :], slot1, bc(dig[:, 1, :], 2, W), ALU.mult).then_inc(s["pay_ready"], 1)
            k(stt(out=comp, in0=slot[:], scalar=float(W) - 0.5, in1=comp, op0=ALU.is_gt, op1=ALU.mult))
            ts(key_tmp, keys[:], 0.5, 0.0, ALU.is_gt, ALU.add, accum_out=nleft[:, 0:1]).then_inc(s["left_count"], 1)
            for d in range(2):
                if d:
                    v.wait_ge(s["left_psum"], 1)
                    k(v.reduce_max(nleft[0:1, 1:2], ps[0:1, 1, 0:P], AX))
                    k(ts(nleft_i[0:1, 1:2], nleft[0:1, 1:2], 7.0, None, ALU.add))
                    ts(nleft_i[0:1, 0:1], nleft_i[0:1, 1:2], 3, None, ALU.arith_shift_right).then_inc(s["left_known"], 1)
                    v.wait_ge(s["ell_psum"], 1)
                    k(v.tensor_copy(ell[:].rearrange("p h w -> p (h w)"), ps[:, 0, 0:2 * W]))
                    k(v.tensor_copy(ell_i[:, 0, :], ell[:, 1, :]))
                    k(ts(ell_i[:, 1, :], ell_i[:, 0, :], 4, None, ALU.arith_shift_right))
                    k(ts(ell_i[:, 2, :], ell_i[:, 0, :], 15, None, ALU.bitwise_and))
                    k(ts(jslot[:, 1, :], ell[:, 0, :], 1.0, 0.0, ALU.subtract, ALU.max))
                    k(ts(jslot[:, 0, :], ell[:, 0, :], 0.5, -100.0, ALU.is_lt, ALU.mult))
                    k(tt(jslot[:, 0, :], jslot[:, 0, :], ell_i[:, 2, :], ALU.add))
                    stt(out=src_idx[:], in0=jslot[:, 1, :], scalar=16.0, in1=ell_i[:, 1, :], op0=ALU.mult, op1=ALU.add).then_inc(s["idx_ready"], 1)
                    k(tt(pen[:], bc(jslot[:, 0, :], 1, NPO), bc(iota_j[:], 2, W), ALU.is_equal))
                    k(ts(pen[:], pen[:], 1.0, BIG, ALU.subtract, ALU.mult))
                for hf in range(2):
                    cols = slice(HALF * hf, HALF * hf + HALF)
                    v.wait_ge(s["hi_ready"], 2 * d + hf + 1)
                    tt(r1[:, cols], banks(2 * hf, 2, 64), bc3[d][0:64, cols], ALU.subtract).then_inc(s["rest_ready"], 1)
                v.wait_ge(s["sp_ln"], d + 1)
                k(ts(sp_c, sp_t, 1.0, 1.0, ALU.add, ALU.subtract))
                k(tt(sp_c, sp_t, sp_c, ALU.subtract))
                k(tt(sp_c, sp_c, uu[d], ALU.add))
                tt(dtv[d], dtv[d], sp_c, ALU.add).then_inc(s["dt_ready"], 1)
                v.wait_ge(s["dt_ready"], d + 1)
                k(tt(uu[d], dtv[d], xs[d], ALU.mult))
                v.wait_ge(s["mid_ready"], d + 1)
                tt(bc3[d][0:32, :], r1[0:32, :], bc3[d][0:32, :], ALU.subtract).then_inc(s["bc_ready"], 1)
                v.wait_ge(s["bc_ready"], d + 1)

            def no_decay(d):
                first = 0 if d == 0 else SEQ - 1
                k(v.memset(da[0].rearrange("p (b s) -> p b s", s=SEQ)[:, :, first:first + 1], 0.0))
                v.memset(da[1].rearrange("p (b s) -> p b s", s=SEQ)[:, :, first:first + 1], 0.0).then_inc(s["da_zero"], 1)

            def scan_state(blk, n, e):
                d, c0 = blk // 2, (blk % 2) * HALF
                v.wait_ge(s["b_psum"], n + 1)
                v.wait_ge(s["g_ready"], n + 1)
                tt(hh[e], uu[d][:, c0:c0 + HALF], banks(6 * e, 2), ALU.mult).then_inc(s["b_used"], 1)
                v.wait_ge(s["da_ready"], n + 1)
                v.wait_ge(s["b_used"], n + 3)
                o, x0, x1 = hh[e], da[e], hh[e]
                if d:
                    o, x0, x1 = o[:, ::-1], x0[:, ::-1], x1[:, ::-1]
                v.tensor_tensor_scan(o, x0, x1, 0.0, ALU.mult, ALU.add).then_inc(s["scan_ready"], 1)

            def gated(blk):
                d, c0 = blk // 2, (blk % 2) * HALF
                v.wait_ge(s["g_used"], 16 * blk + 18)
                tt(zs[d][:, c0:c0 + HALF], zs[d][:, c0:c0 + HALF], banks(4, 2), ALU.mult).then_inc(s["yg_ready"], 1)

            no_decay(0)
            for blk in range(4):
                if blk == 2:
                    v.wait_ge(s["scan_ready"], 34)
                    no_decay(1)
                for e in range(2):
                    scan_state(blk, 16 * blk + e, e)
                if blk:
                    gated(blk - 1)
                with v.Fori(0, DS // 2 - 1) as it:
                    for e in range(2):
                        scan_state(blk, it * 2 + (16 * blk + 2 + e), e)
            gated(3)

            v.wait_ge(s["t2_psum"], 1)
            v.wait_ge(s["res_back"], 16)
            k(tt(t2.rearrange("p j c -> p (j c)"), resb.rearrange("p j c -> p (j c)"), banks(0, 2), ALU.add))
            norm(v_tok, t2, d_tok, v_tok, lns, 3, C, s["v_ready"])
            v.wait_ge(s["att_in"], 32)
            v.wait_ge(s["h_psum"], 1)
            k(v.tensor_copy(hrow[:, :, 0:HE], ps[:, 2, 0:NPO * HE].rearrange("p (j n) -> p j n", j=NPO)))
            for r in (1, 0):
                k(tt(atmp[:], hrow[:, :, 0:HE], bc(att[:, r, :], 1, NPO), ALU.mult))
                to = adst[:].rearrange("p h j -> p j h") if r else hrow[:, :, HE:ROW]
                m = v.tensor_reduce(out=to, in_=atmp[:].rearrange("p j (h x) -> p j h x", h=HEADS), axis=AX, op=ALU.add)
                if r:
                    k(m)
                else:
                    m.then_inc(s["h_ready"], 1)

            def lrelu(dst, src):
                return stt(out=dst, in0=src, scalar=0.2, in1=src, op0=ALU.mult, op1=ALU.max)

            v.wait_ge(s["hist_back"], 16)
            v.wait_ge(s["last_in"], 16)
            k(v.tensor_reduce(out=cnt[:], in_=cnt4[:].rearrange("p g j -> p j g"), axis=AX, op=ALU.add))
            k(ts(gs[:, 0, :], cnt[:], 0.5, 1.0, ALU.is_gt, ALU.subtract))
            k(ts(gs[:, 0, :], gs[:, 0, :], BIG, None, ALU.mult))
            k(tt(g2[:], bc(gs[:, 0, :], 1, HEADS), bc(last[:, HE:ROW], 2, NPO), ALU.add))
            aself = hrow[:, :, HE:ROW].rearrange("p j h -> p h j")
            v.wait_ge(s["h_ready"], 1)
            k(tt(amax[:], aself, g2[:], ALU.max))
            v.wait_ge(s["nb_in"], 16 * W)
            for h in range(HEADS):
                k(tt(a_e[:, h], pen[:], bc(nb[:, :, HE + h], 1, NPO), ALU.add))
            k(v.tensor_reduce(out=mx[:], in_=a_e, axis=AX, op=ALU.max))
            k(tt(amax[:], amax[:], mx[:], ALU.max))
            k(tt(mx[:], amax[:], adst[:], ALU.add))
            k(lrelu(mcur[:], mx[:]))
            for t, x in ((g1, aself), (g2, g2[:])):
                k(tt(t[:], x, adst[:], ALU.add))
                k(lrelu(t[:], t[:]))
                m = tt(t[:], t[:], mcur[:], ALU.subtract)
                if t is g1:
                    k(m)
                else:
                    m.then_inc(s["e_in"], 1)

            def left_edges(n, c, at):
                done = [0]

                def step(ins):
                    done[0] += 1
                    ins.then_inc(s["left_step"], 1)
                    v.wait_ge(s["left_step"], at + done[0])

                step(v.tensor_copy(left_row[:, ROW:ROW + 1], m8[:, bass.ds(c, 1)]))
                step(ts(left_idx[:, 1:2], left_row[:, ROW:ROW + 1], -1.0, None, ALU.add))
                ts(left_idx[:, 0:1], left_idx[:, 1:2], LAST, None, ALU.bitwise_and).then_inc(s["left_idx_ready"], 1)
                v.wait_ge(s["left_in"], n * 16 + 16)
                step(ts(lk[:, 0, :], left_all[:, :, ROW], -1.0, None, ALU.add))
                step(ts(lk[:, 1, :], lk[:, 0, :], 15, None, ALU.arith_shift_right))
                step(ts(lkf[:, 0, :], lk[:, 1, :], pf[:], None, ALU.is_equal))
                step(ts(lk[:, 1, :], lk[:, 0, :], 11, 15, ALU.arith_shift_right, ALU.bitwise_and))
                step(stt(out=lkf[:, 1, :], in0=lk[:, 1, :], scalar=1.0, in1=lkf[:, 0, :], op0=ALU.add, op1=ALU.mult))
                step(ts(lkf[:, 1, :], lkf[:, 1, :], -1.0, None, ALU.add))
                for q in range(P // LW):
                    e0 = q * LW
                    step(tt(left_pen, bc(lkf[:, 1, e0:e0 + LW], 1, NPO), bc(iota_j[:], 2, LW), ALU.is_equal))
                    step(ts(left_pen, left_pen, 1.0, BIG, ALU.subtract, ALU.mult))
                    for h in range(HEADS):
                        step(tt(left_w[:, h], left_pen, bc(left_all[:, e0:e0 + LW, HE + h], 1, NPO), ALU.add))
                    step(v.tensor_reduce(out=mx[:], in_=left_w, axis=AX, op=ALU.max))
                    step(tt(amax[:], amax[:], mx[:], ALU.max))
                    step(tt(mx[:], amax[:], adst[:], ALU.add))
                    step(lrelu(mx[:], mx[:]))
                    step(tt(g1[:], mcur[:], mx[:], ALU.subtract))
                    step(v.tensor_copy(mcur[:], mx[:]))
                    step(tt(flat(left_w), flat(left_w), bc(ad2, 2, LW), ALU.add))
                    step(lrelu(flat(left_w), flat(left_w)))
                    tt(flat(left_w), flat(left_w), bc(mc2, 2, LW), ALU.subtract).then_inc(s["left_e"], 1)
                    v.wait_ge(s["left_exp"], n * (2 * (P // LW)) + (2 * q + 2))
                    step(tt(den[:], den[:], g1[:], ALU.mult))
                    step(v.tensor_reduce(out=mx[:], in_=left_w, axis=AX, op=ALU.add))
                    step(tt(den[:], den[:], mx[:], ALU.add))
                    for h in range(HEADS):
                        step(tt(left_p, bc(left_w[:, h], 1, EXP),
                                bc(left_all[:, e0:e0 + LW, EXP * h:EXP * h + EXP].rearrange("p w x -> p x w"), 2, NPO), ALU.mult))
                        step(v.tensor_reduce(out=g4[:, h], in_=left_p, axis=AX, op=ALU.add))
                        step(tt(acc[:, h], acc[:, h], bc(g1[:, h], 1, EXP), ALU.mult))
                        step(tt(acc[:, h], acc[:, h], g4[:, h], ALU.add))
                assert done[0] == LEFT_COLUMN, done[0]

            def flat(x):
                return x.rearrange("p h j w -> p (h j) w")

            ad2, mc2 = adst[:].rearrange("p h j -> p (h j)"), mcur[:].rearrange("p h j -> p (h j)")
            k(tt(flat(a_e), flat(a_e), bc(ad2, 2, W), ALU.add))
            k(lrelu(flat(b_e), flat(a_e)))
            tt(flat(a_e), flat(b_e), bc(mc2, 2, W), ALU.subtract).then_inc(s["e_in"], 1)
            v.wait_ge(s["exp_ready"], 3)
            k(tt(g2[:], g2[:], bc(cnt[:], 1, HEADS), ALU.mult))
            k(v.tensor_reduce(out=den[:], in_=a_e, axis=AX, op=ALU.add))
            k(tt(den[:], den[:], g1[:], ALU.add))
            k(tt(den[:], den[:], g2[:], ALU.add))
            for h in range(HEADS):
                o = b_e[:].rearrange("p x j w -> p x j w")
                k(tt(o, bc(a_e[:, h], 1, EXP), bc(nb[:, :, EXP * h:EXP * h + EXP].rearrange("p w x -> p x w"), 2, NPO), ALU.mult))
                k(v.tensor_reduce(out=acc[:, h], in_=o, axis=AX, op=ALU.add))
            hself = hrow[:, :, 0:HE].rearrange("p j (h x) -> p h x j", h=HEADS)
            for h in range(HEADS):
                k(tt(g4[:, h], bc(g1[:, h], 1, EXP), hself[:, h], ALU.mult))
                k(tt(acc[:, h], acc[:, h], g4[:, h], ALU.add))
                k(tt(g4[:, h], bc(g2[:, h], 1, EXP), bc(last[:, EXP * h:EXP * h + EXP], 2, NPO), ALU.mult))
                k(tt(acc[:, h], acc[:, h], g4[:, h], ALU.add))

            rounds = v.value_load(nleft_i[0:1, 0:1], min_val=0, max_val=EPP)
            with v.If(rounds > 0):
                with v.Fori(0, rounds) as r:
                    ls = s["left_step"]
                    v.max(out=m8[:], in_=keys[:]).then_inc(ls, 1)
                    v.wait_ge(ls, r * LEFT_ROUND + 1)
                    v.memset(pause[:, 1:2], 0.0).then_inc(ls, 1)
                    v.match_replace(out=keys[:], in_to_replace=m8[:], in_values=keys[:], imm_value=0.0).then_inc(ls, 1)
                    v.wait_ge(ls, r * LEFT_ROUND + 3)
                    v.memset(pause[:, 1:2], 0.0).then_inc(ls, 1)
                    with v.Fori(0, 8) as c:
                        at = r * LEFT_ROUND + c * LEFT_COLUMN + 4
                        left_edges(r * 8 + c, c, at)
            k(ts(den[:], den[:], 1e-16, None, ALU.add))
            k(v.reciprocal(den[:], den[:]))
            aggv = agg[:].rearrange("p j (h x) -> p h x j", h=HEADS)
            for h in range(HEADS):
                k(tt(aggv[:, h], acc[:, h], bc(den[:, h], 1, EXP), ALU.mult))
            k(tt(agg[:], agg[:], bc(rows16[:, 0, :], 1, NPO), ALU.add))
            norm(agg[:], agg[:], agg[:], atmp[:], gs[:], 4, HE, None)
            k(tt(agg[:], agg[:], bc(rows16[:, 1, :], 1, NPO), ALU.mult))
            k(tt(agg[:], agg[:], bc(rows16[:, 2, :], 1, NPO), ALU.add))
            k(v.tensor_reduce(out=sc[:], in_=agg[:].rearrange("p j (h x) -> p j x h", h=HEADS), axis=AX, op=ALU.add))
            k(ts(sc[:], sc[:], 1.0 / HEADS, None, ALU.mult))
            k(tt(cmp1, bc(sc[:], 2, EXP), bc(sc[:], 3, EXP), ALU.is_gt))
            k(tt(cmp2, bc(sc[:], 2, EXP), bc(sc[:], 3, EXP), ALU.is_equal))
            k(tt(cmp2.rearrange("p j a b -> p j (a b)"), cmp2.rearrange("p j a b -> p j (a b)"),
                 bc(tiebreak[:].rearrange("p a b -> p (a b)"), 1, NPO), ALU.mult))
            k(tt(cmp1, cmp1, cmp2, ALU.add))
            k(v.tensor_reduce(out=atmp[:, :, 0:EXP], in_=cmp1, axis=AX, op=ALU.add))
            k(v.tensor_reduce(out=gs[:, 0, :], in_=sc[:], axis=AX, op=ALU.max))
            tt(gate[:], sc[:], bc(gs[:, 0, :], 2, EXP), ALU.subtract).then_inc(s["ln_var"], 1)
            v.wait_ge(s["ln_std"], 5)
            k(stt(out=gate[:], in0=atmp[:, :, 0:EXP], scalar=1.5, in1=gate[:], op0=ALU.is_lt, op1=ALU.mult))
            k(v.tensor_reduce(out=gs[:, 1, :], in_=gate[:], axis=AX, op=ALU.add))
            k(v.reciprocal(gs[:, 1, :], gs[:, 1, :]))
            k(tt(gate[:], gate[:], bc(gs[:, 1, :], 2, EXP), ALU.mult))
            v.wait_ge(s["eo_read"], 4)
            ev = eo.rearrange("p j e c -> p (j e) c")
            k(tt(ev, ev, bc(gate[:].rearrange("p j e -> p (j e)"), 2, C), ALU.mult))
            k(v.tensor_reduce(out=d_tok, in_=eo.rearrange("p j e c -> p j c e"), axis=AX, op=ALU.add))
            tt(t2, t2, d_tok, ALU.add).then_inc(s["out_ready"], 1)


INS = ["x", "om_kernel", "om_bias", "kernel", "bias", "edges", "ln_gb", "w_gat", "att", "rows16", "w1", "b1", "w2", "b2"] + [
    p + n for p in ("f_", "b_") for n in ("in_w", "conv_w", "vec", "xp_w", "xd_w", "dp_w", "a_log", "o_w")]


def laid_out(x, **w):
    import numpy as np

    def c(v):
        return np.ascontiguousarray(v)

    r = {
        "x": c(x).reshape(T, C), "om_kernel": c(w["L0_conv_om_kernel"]).reshape(K2, C, OM),
        "om_bias": c(w["L0_conv_om_bias"]).reshape(OM, 1), "kernel": c(w["L0_conv_kernel"]),
        "bias": c(w["L0_conv_bias"]).reshape(1, C), "edges": c(w["L1_ffn_edge_index"]),
        "ln_gb": c(np.stack([w["L1_attn_ln_gamma"], w["L1_attn_ln_beta"]], 1)),
        "w_gat": c(w["L1_ffn_W_gat"]),
        "att": c(np.stack([w["L1_ffn_att_src"], w["L1_ffn_att_dst"]])).reshape(1, 2 * HE),
        "rows16": c(np.stack([w["L1_ffn_b_gat"], w["L1_ffn_ln_gamma"], w["L1_ffn_ln_beta"]])).reshape(1, 3 * HE),
        "w1": c(w["L1_ffn_W1"]), "b1": c(np.asarray(w["L1_ffn_b1"]).T), "w2": c(w["L1_ffn_W2"]),
        "b2": c(w["L1_ffn_b2"]).reshape(1, EXP * C),
    }
    for p in ("f_", "b_"):
        def m(n):
            return np.asarray(w["L1_attn_" + p + n])
        r[p + "in_w"] = c(m("in_proj_w").T)
        r[p + "conv_w"] = c(m("conv_w")[:, 0, :].T).reshape(1, TAPS * DI)
        r[p + "vec"] = c(np.stack([m("conv_b"), m("dt_proj_b"), m("D")], 1))
        r[p + "xp_w"] = c(m("x_proj_w").T)
        r[p + "xd_w"] = c(m("x_proj_w")[0:DTR])
        r[p + "dp_w"] = c(m("dt_proj_w").T)
        r[p + "a_log"] = c(m("A_log"))
        r[p + "o_w"] = c(m("out_proj_w").T)
    return r


def kernel(**inputs):
    import numpy as np
    import concourse.bacc as bacc
    from concourse.bass_utils import run_bass_kernel_spmd

    nc = bacc.Bacc("TRN2", target_bir_lowering=False, num_devices=1)
    arrays = laid_out(**{n: np.asarray(v) for n, v in inputs.items()})
    a = {n: nc.dram_tensor("dram_" + n, arrays[n].shape, mybir.dt.from_np(arrays[n].dtype), kind="ExternalInput").ap() for n in INS}
    out = nc.dram_tensor("out", [T, C], F32, kind="ExternalOutput").ap()
    program(nc, a, out)
    r = run_bass_kernel_spmd(nc, [{"dram_" + n: arrays[n] for n in INS}], core_ids=[0])
    return r.results[0]["out"].reshape(BATCH, HEIGHT, WIDTH, C)
```

```python
from contextlib import ExitStack

import concourse.bass as bass
from concourse import mybir

P = 128
BATCH, HEIGHT, WIDTH, C = 8, 16, 16, 64
SEQ = HEIGHT * WIDTH
T = BATCH * SEQ
NT = T // P
K2 = 9
OM = 3 * K2
DI, DS, DTR, TAPS = 128, 16, 16, 4
SEQP = SEQ + 2 * (TAPS - 1)
HALF = T // 2
EDGES = 262144
EPP = EDGES // P
LAST = T - 1
HI, LO = 32, 64
HCH = 296
CHUNKS = [(e, min(HCH, EPP - e)) for e in range(0, EPP, HCH)]
CAP = 56
W = 56
ROUNDS = CAP // 8
OMQ = 4
TPQ = NT // OMQ
POOL_TAPS = 5
NPO = T // P
W_AT = (0, 10, 26, 44, W)
WCH = len(W_AT) - 1
WC_MAX = max(b - a for a, b in zip(W_AT, W_AT[1:]))
DVE_NODES = 11
HEADS, EXP = 4, 4
HE = HEADS * EXP
ROW = HE + HEADS
HID = 2 * C
LW = 32
BIG = 1.0e30
LEFT_COLUMN = 8 + (P // LW) * 33
LEFT_ROUND = 4 + 8 * LEFT_COLUMN

F32 = mybir.dt.float32
BF16 = mybir.dt.bfloat16
I32 = mybir.dt.int32
ALU = mybir.AluOpType
ACT = mybir.ActivationFunctionType
AX = mybir.AxisListType.X


class Link:

    def __init__(self, eng, sem):
        self.eng, self.sem, self.n = eng, sem, 0

    def __call__(self, ins):
        self.go(ins)
        self.wait()

    def go(self, ins):
        self.n += 1
        ins.then_inc(self.sem, 1)

    def wait(self):
        self.eng.wait_ge(self.sem, self.n)


def program(nc, a, out):
    with ExitStack() as ctx:
        def sb(name, shape, dt=F32):
            return ctx.enter_context(nc.sbuf_tensor(name, shape, dt))

        def sem(name):
            return ctx.enter_context(nc.semaphore(name))

        ps = ctx.enter_context(nc.psum_tensor("ps", [P, 8, 512], F32))

        def banks(lo, n, parts=P):
            return ps[0:parts, lo:lo + n, :].rearrange("p b n -> p (b n)")

        class Arena:

            def __init__(self, name, words):
                self.mem, self.words, self.top = sb(name, [P, words]), words, 0

            def __call__(self, n, dt=F32, parts=P):
                lo, words = self.top, n if dt != BF16 else (n + 1) // 2
                self.top += words
                assert self.top <= self.words, self.top
                v = self.mem[0:parts, lo:lo + words]
                return v if dt == F32 else v.bitcast(dt)

        ident = sb("ident", [P, P])
        ones_f = sb("ones_f", [1, P])
        iota_pi = sb("iota_pi", [P, 1], I32)
        pi_tmp = sb("pi_tmp", [P, 2], I32)
        ph = sb("ph", [P, 1])
        pl = sb("pl", [P, 1])
        pf = sb("pf", [P, 1])
        iota_y = sb("iota_y", [P, 2, K2 * HEIGHT])
        iota_x = sb("iota_x", [P, K2, WIDTH])
        pairmat = sb("pairmat", [P, P])
        iota_n = sb("iota_n", [P, P], BF16)
        tri = sb("tri", [P, P], BF16)
        sel = sb("sel", [96, 32], BF16)
        iota_j = sb("iota_j", [P, NPO])
        tiebreak = sb("tiebreak", [P, EXP, EXP])
        w_om2 = sb("w_om2", [P, 3, OM])
        w_om1 = sb("w_om1", [C, 3, OM])
        b_om = sb("b_om", [OM, 1])
        w_cv = sb("w_cv", [C, K2, C])
        b_cv = sb("b_cv", [1, C])
        in_w = [sb(f"in_w{d}", [P, 2 * DI]) for d in range(2)]
        w_tap = [sb(f"w_tap{d}", [P, TAPS // 2, DI]) for d in range(2)]
        vec = [sb(f"vec{d}", [P, 3]) for d in range(2)]
        xp_w = [sb(f"xp_w{d}", [P, 96]) for d in range(2)]
        xd_w = [sb(f"xd_w{d}", [DTR, DI]) for d in range(2)]
        dt_w = [sb(f"dt_w{d}", [P, DI]) for d in range(2)]
        dp_w = [sb(f"dp_w{d}", [DTR, DI]) for d in range(2)]
        neg_a = [sb(f"neg_a{d}", [P, DS]) for d in range(2)]
        diag_d = [sb(f"diag_d{d}", [P, P]) for d in range(2)]
        o_w = [sb(f"o_w{d}", [P, C]) for d in range(2)]
        gb = sb("gb", [P, 2])
        w_gat = sb("w_gat", [C, HE])
        att = sb("att", [P, 2, HE])
        rows16 = sb("rows16", [P, 3, HE])
        w1 = sb("w1", [C, EXP, HID])
        b1 = sb("b1", [HID, EXP])
        w2 = sb("w2", [HID, EXP, C])
        b2 = sb("b2", [1, EXP * C])
        ones_b = sb("ones_b", [1, P], BF16)
        x_tok = sb("x_tok", [P, NT, C])
        st6 = sb("st6", [P, BATCH, 6])
        mv = sb("mv", [P, BATCH, 2])
        ms = sb("ms", [P, BATCH, 2])
        gnm = sb("gnm", [P, BATCH, 2])
        gnv = sb("gnv", [P, 3, BATCH])
        om = sb("om", [P, NT, OM])
        msk = sb("msk", [P, NT, K2])
        lns = sb("lns", [P, 6, NT])
        keys = sb("keys", [P, EPP + CAP])
        comp = keys[:, EPP:EPP + CAP]
        hi_b = sb("hi_b", [P, EPP], BF16)
        lo_b = sb("lo_b", [P, EPP], BF16)
        key_i = sb("key_i", [P, CAP], I32)
        int_a = sb("int_a", [P, 3, CAP], I32)
        owner = sb("owner", [P, CAP])
        owner_b = sb("owner_b", [P, CAP], BF16)
        same = sb("same", [P, CAP])
        run = sb("run", [P, CAP])
        slot = sb("slot", [P, CAP])
        dig = sb("dig", [P, 2, CAP])
        base_b = sb("base_b", [P, P], BF16)
        ell = sb("ell", [P, 2, W])
        ell_i = sb("ell_i", [P, 3, W], I32)
        src_idx = sb("src_idx", [P, W], I32)
        jslot = sb("jslot", [P, 2, W])
        pen = sb("pen", [P, NPO, W])
        hist_s = sb("hist_s", [P, LO])
        cnt4 = sb("cnt4", [P, 4, NPO])
        cnt = sb("cnt", [P, NPO])
        nleft = sb("nleft", [P, 2])
        nleft_i = sb("nleft_i", [1, 2], I32)
        hrow = sb("hrow", [P, NPO, ROW])
        adst = sb("adst", [P, HEADS, NPO])
        atmp = sb("atmp", [P, NPO, HE])
        last = sb("last", [P, ROW])
        amax = sb("amax", [P, HEADS, NPO])
        mx = sb("mx", [P, HEADS, NPO])
        mcur = sb("mcur", [P, HEADS, NPO])
        den = sb("den", [P, HEADS, NPO])
        acc = sb("acc", [P, HEADS, EXP, NPO])
        g1 = sb("g1", [P, HEADS, NPO])
        g2 = sb("g2", [P, HEADS, NPO])
        g4 = sb("g4", [P, HEADS, EXP, NPO])
        agg = sb("agg", [P, NPO, HE])
        lnd, lsq, un = (x.rearrange("p (t c) -> p t c", t=TPQ) for x in (
            agg[:].rearrange("p j n -> p (j n)"), atmp[:].rearrange("p j n -> p (j n)"), acc[:].rearrange("p h x j -> p (h x j)")))
        gs = sb("gs", [P, 6, NPO])
        sc = sb("sc", [P, NPO, EXP])
        gate = sb("gate", [P, NPO, EXP])
        pause = sb("pause", [P, 4])
        left_row = sb("left_row", [P, ROW + 1])
        left_idx = sb("left_idx", [P, 2], I32)
        m8 = sb("m8", [P, 8])

        ar = Arena("arena", 26800)
        one_hi = ar(HI * HCH, BF16).rearrange("p (v e) -> p v e", v=HI)
        one_lo = ar(LO * HCH, BF16).rearrange("p (v e) -> p v e", v=LO)
        s_buf = [ar(K2 * SEQ).rearrange("p (k y x) -> p k y x", k=K2, x=WIDTH)]
        s_t = [ar(2 * K2 * P).rearrange("p (n q) -> p n q", n=2 * K2) for _ in range(2)]
        xk = [ar(2 * K2 * C).rearrange("p (t n) -> p t n", t=2) for _ in range(2)]
        wy = ar(NT * K2 * HEIGHT).rearrange("p (t k y) -> p t k y", t=NT, k=K2)
        ar.top = 0
        src_i = ar(EPP, I32)
        dst_i = ar(EPP, I32)
        e_tmp = ar(EPP)
        e_tm2 = ar(EPP)
        e_int = ar(EPP, I32)
        cw_b = [ar(TAPS * DI).rearrange("p (k c) -> p k c", k=TAPS) for _ in range(2)]
        x_dup = ar(NT * 2 * C).rearrange("p (t r c) -> p t r c", t=NT, r=2)
        om_t = s_t[1].rearrange("p n q -> p (n q)")[0:OM, 0:T]
        ar.top = 0
        xnt = ar(BATCH * SEQP).rearrange("p (b s) -> p b s", b=BATCH)
        x0_at = ar.top
        xs, zs, dtv, uu = ([ar(T)] for _ in range(4))
        bc3 = [ar(T, BF16) for _ in range(2)]
        loop_at = ar.top
        da = [ar(HALF) for _ in range(2)]
        hh = [ar(HALF) for _ in range(2)]
        gg = [ar(HALF) for _ in range(2)]
        x1_at = ar.top
        for x in (xs, zs, dtv, uu):
            x.append(ar(T))
        ar.top = loop_at
        sp_t = ar(T)
        sp_c = ar(T)
        r1 = ar(T, parts=64)
        ar.top = x0_at
        ar.top = x1_at
        look = ar(CAP * P, BF16).rearrange("p (c q) -> p c q", c=CAP)
        slot1 = ar(CAP * W, BF16).rearrange("p (c w) -> p c w", c=CAP)
        pay = ar(CAP * 2 * W, BF16).rearrange("p (c h w) -> p c h w", c=CAP, h=2)
        key_tmp = look.rearrange("p c q -> p (c q)")[:, 0:EPP + CAP]
        ar.top = 0
        vt = ar(T, parts=C)
        v_tok, d_tok = (ar(NT * C).rearrange("p (t c) -> p t c", t=NT) for _ in range(2))
        assert ar.top <= x0_at + T
        ar.top = x0_at + 2 * T
        a_e, b_e = (ar(HEADS * NPO * W).rearrange("p (h j w) -> p h j w", h=HEADS, j=NPO) for _ in range(2))
        hid = [ar(HID * 4) for _ in range(2)]
        eo = ar(NPO * EXP * C).rearrange("p (j e c) -> p j e c", j=NPO, e=EXP)
        assert ar.top <= x1_at
        diff_t = b_e.rearrange("p h j w -> p (h j w)")[0:C, 0:T]
        left_p = b_e.rearrange("p h j w -> p (h j w)")[:, 0:EXP * NPO * LW].rearrange("p (x j w) -> p x j w", x=EXP, j=NPO)
        ar.top = x1_at
        left_w = ar(HEADS * NPO * LW).rearrange("p (h j w) -> p h j w", h=HEADS, j=NPO)
        assert ar.top <= x1_at + T
        e_c = left_w.rearrange("p h j w -> p (h j w)")

        def chunk_products(wc):
            return prod[:, 0:HE * NPO * wc].rearrange("p (h x j w) -> p h x j w", h=HEADS, x=EXP, j=NPO)

        def chunk_weights(wc):
            return e_c[:, 0:HEADS * NPO * wc].rearrange("p (h j w) -> p h j w", h=HEADS, j=NPO)
        ar.top = x1_at + T
        prod = ar(HE * NPO * WC_MAX)
        ar.top = x1_at + 2 * T
        left_all = ar(P * (ROW + 1)).rearrange("p (e r) -> p e r", e=P)
        lk = ar(2 * P, I32).rearrange("p (a e) -> p a e", a=2)
        lkf = ar(2 * P).rearrange("p (a e) -> p a e", a=2)
        left_pen = ar(NPO * LW).rearrange("p (j w) -> p j w", j=NPO)
        cmp1, cmp2 = (ar(NPO * EXP * EXP).rearrange("p (j a b) -> p j a b", j=NPO, a=EXP) for _ in range(2))
        br = Arena("arena2", 10528)
        xpad = br(BATCH * (HEIGHT + 2) * (WIDTH + 2)).rearrange("p (b y x) -> p b y x", b=BATCH, x=WIDTH + 2)
        xc = br(T, parts=C).rearrange("p (b q) -> p b q", b=BATCH)
        wx = br(NT * K2 * WIDTH).rearrange("p (t k x) -> p t k x", t=NT, k=K2)
        xn2 = wx.rearrange("p t k x -> p (t k x)")[:, 0:NT * 2 * C].rearrange("p (t r c) -> p t r c", t=NT, r=2)
        s2_at = br.top
        s_buf.append(br(K2 * SEQ).rearrange("p (k y x) -> p k y x", k=K2, x=WIDTH))
        s_rows = [b.rearrange("p k y x -> p k (y x)") for b in s_buf]
        br.top = s2_at
        own1 = br(CAP * P, BF16).rearrange("p (c q) -> p c q", c=CAP)
        br.top = 0
        cs = [br(HALF) for _ in range(2)]
        br.top = 0
        b2_rest = br(EXP * C, parts=1)
        b2_part = br(3 * EXP * C, BF16, parts=1).rearrange("p (a n) -> p a n", a=3)
        br.top = 2 * HALF
        resb = br(NPO * C).rearrange("p (j c) -> p j c", j=NPO)
        nb = br(W * ROW).rearrange("p (w r) -> p w r", w=W)
        t2 = br(NPO * C).rearrange("p (j c) -> p j c", j=NPO)
        res_d = nc.dram_tensor("res_scratch", [T, C], F32).ap()
        tab_d = nc.dram_tensor("node_rows", [T, ROW], F32).ap()
        cnt_d = nc.dram_tensor("hist_scratch", [4, T], F32).ap()
        left_d = nc.dram_tensor("left_scratch", [1, P * (ROW + 1)], F32).ap()

        names = """x_in edge_in wconv_in gb_in wmamba_in cw_in wffn_in att_in pool_step xdup_in ident_ready const_ready dve_step act_step
            xt_ready stats_ready pair_ready var_ready std_ready gn_ready xhat_ready xhat2_ready xc_ready
            omt_psum omt_ready om_ready om_read off_ready abs_step wx_ready
            hat_ready s_ready s2_ready st_psum st_ready xk_psum xk_ready conv_out t1_ready
            onehot_ready onehot_used hist_ready hist_out hist_back
            ln_var ln_std res_ready res_out res_back xn_ready xn2_ready xnt_psum xnt_ready taps_ready
            xs_psum xs_ready z_psum z_ready dbc_psum hi_ready rest_ready mid_ready bc_ready dt_psum
            dtw_psum dtw_ready sp_relu sp_abs sp_exp sp_ln dt_ready uu_ready nega_ready diag_ready
            own_ready base_psum base_read pay_ready ell_psum idx_ready left_psum left_count left_known
            b_psum b_used c_psum da_ready scan_ready c_ready g_ready g_used da_zero yg_ready
            b2_ready t2_psum diff_ready dt2_psum dt2_ready v_ready vt_psum vt_ready h_psum h_ready tab_out last_in nb_in0 nb_in1 nb_in2 nb_in3 e_in exp_ready
            hid_psum hid_ready eo_psum eo_read gate_ready
            left_step pause_step left_idx_ready left_row_in left_out left_in left_e left_exp out_ready out2_ready out_done""".split()
        s = {n: sem(n) for n in names}
        block = ctx.enter_context(nc.Block())
        PRE = ("f_", "b_")
        edge_v = a["edges"].rearrange("r (p e) -> r p e", p=P)

        @block.sync
        def _(sp):
            x_tiles = a["x"].rearrange("(t p) c -> p t c", p=P)
            for r in range(2):
                sp.dma_start(x_dup[:, :, r, :], x_tiles).then_inc(s["xdup_in"], 16)
            om_k = a["om_kernel"].rearrange("(y x) c n -> x c y n", x=3)
            for r in range(2):
                sp.dma_start(w_om2[C * r:C * r + C], om_k[r]).then_inc(s["wconv_in"], 16)
            sp.dma_start(w_om1[:], om_k[2]).then_inc(s["wconv_in"], 16)
            sp.dma_start(b_om[:], a["om_bias"]).then_inc(s["wconv_in"], 16)
            sp.dma_start(w_cv[:], a["kernel"].rearrange("(k c) n -> c k n", c=C)).then_inc(s["wconv_in"], 16)
            sp.dma_start(b_cv[:], a["bias"]).then_inc(s["wconv_in"], 16)
            sp.dma_start(src_i, edge_v[0]).then_inc(s["edge_in"], 16)
            sp.dma_start(dst_i, edge_v[1]).then_inc(s["edge_in"], 16)
            sp.dma_start(x_tok[:], x_tiles).then_inc(s["x_in"], 16)
            for d, pre in enumerate(PRE):
                sp.dma_start(cw_b[d], a[pre + "conv_w"].to_broadcast([P, TAPS * DI])
                             .rearrange("p (k c) -> p k c", k=TAPS)).then_inc(s["cw_in"], 16)
                for r in range(2):
                    sp.dma_start(in_w[d][C * r:C * r + C, :], a[pre + "in_w"]).then_inc(s["cw_in"], 16)
            for d, pre in enumerate(PRE):
                sp.dma_start(vec[d][:], a[pre + "vec"]).then_inc(s["wmamba_in"], 16)
                sp.dma_start(xd_w[d][:], a[pre + "xd_w"]).then_inc(s["wmamba_in"], 16)
                for r in range(3):
                    sp.dma_start(xp_w[d][:, 32 * r:32 * r + 32], a[pre + "xp_w"][:, DTR:DTR + 2 * DS]).then_inc(s["wmamba_in"], 16)
                sp.dma_start(dp_w[d][:], a[pre + "dp_w"]).then_inc(s["wmamba_in"], 16)
                sp.dma_start(neg_a[d][:], a[pre + "a_log"]).then_inc(s["wmamba_in"], 16)
                sp.dma_start(o_w[d][:], a[pre + "o_w"]).then_inc(s["wmamba_in"], 16)
            for r in range(2):
                sp.dma_start(gb[C * r:C * r + C, :], a["ln_gb"]).then_inc(s["gb_in"], 16)
            sp.dma_start(w_gat[:], a["w_gat"]).then_inc(s["wffn_in"], 16)
            sp.dma_start(w1[:], a["w1"].rearrange("e c n -> c e n")).then_inc(s["wffn_in"], 16)
            sp.dma_start(b1[:], a["b1"]).then_inc(s["wffn_in"], 16)
            sp.dma_start(w2[:], a["w2"].rearrange("e h n -> h e n")).then_inc(s["wffn_in"], 16)
            sp.dma_start(b2[:], a["b2"]).then_inc(s["wffn_in"], 16)
            sp.dma_start(att[:].rearrange("p a n -> p (a n)"), a["att"].to_broadcast([P, 2 * HE])).then_inc(s["att_in"], 16)
            sp.dma_start(rows16[:].rearrange("p a n -> p (a n)"), a["rows16"].to_broadcast([P, 3 * HE])).then_inc(s["att_in"], 16)

            for g in range(NT // TPQ):
                sp.wait_ge(s["res_ready"], g + 1)
                sp.dma_start(res_d.rearrange("(t p) c -> p t c", p=P)[:, TPQ * g:TPQ * g + TPQ], x_tok[:, TPQ * g:TPQ * g + TPQ]).then_inc(s["res_out"], 16)
            sp.wait_ge(s["res_out"], 16 * (NT // TPQ))
            sp.wait_ge(s["xn_ready"], NT // TPQ)
            sp.dma_start(resb, res_d.rearrange("(p j) c -> p j c", p=P)).then_inc(s["res_back"], 16)
            sp.wait_ge(s["hist_ready"], 1)
            sp.dma_start(cnt_d.rearrange("g (h l) -> (g h) l", l=LO), hist_s[:]).then_inc(s["hist_out"], 16)
            sp.wait_ge(s["hist_out"], 16)
            sp.dma_start(cnt4[:], cnt_d.rearrange("g (p j) -> p g j", p=P)).then_inc(s["hist_back"], 16)
            sp.wait_ge(s["h_ready"], 1)
            sp.dma_start(tab_d.rearrange("(p j) r -> p j r", p=P), hrow[:]).then_inc(s["tab_out"], 16)
            sp.wait_ge(s["tab_out"], 16)
            sp.dma_start(last[:], tab_d[LAST:T, :].to_broadcast([P, ROW])).then_inc(s["last_in"], 16)
            out_v = out.rearrange("(p j) c -> p j c", p=P)
            sp.wait_ge(s["out2_ready"], 1)
            sp.dma_start(out_v[:, DVE_NODES:NPO], t2[:, DVE_NODES:NPO]).then_inc(s["out_done"], 16)
            sp.wait_ge(s["out_ready"], 1)
            sp.dma_start(out_v[:, 0:DVE_NODES], t2[:, 0:DVE_NODES]).then_inc(s["out_done"], 16)
            sp.wait_ge(s["out_done"], 32)

        @block.gpsimd
        def _(g):
            k = Link(g, s["pool_step"])
            k(g.memset(ident[:], 0.0))
            k(g.affine_select(out=ident[:], in_=ident[:], compare_op=ALU.not_equal, fill=1.0, base=0,
                              pattern=[[-1, P]], channel_multiplier=1))
            g.sem_inc(s["ident_ready"], 1)
            k(g.memset(ones_f[:], 1.0))
            k(g.memset(ones_b[:], 1.0))
            k(g.memset(pairmat[:], 0.5))
            pv = pairmat[:].rearrange("p (g two) -> p g two", two=2)
            k(g.affine_select(out=pv, in_=pv, compare_op=ALU.is_ge, fill=0.0, base=0,
                              pattern=[[-2, P // 2], [0, 2]], channel_multiplier=1))
            k(g.affine_select(out=pv, in_=pv, compare_op=ALU.is_ge, fill=0.0, base=1,
                              pattern=[[2, P // 2], [0, 2]], channel_multiplier=-1))
            k(g.memset(xpad, 0.0))
            k(g.iota(iota_pi[:], pattern=[[0, 1]], base=0, channel_multiplier=1))
            for i2 in range(2):
                k(g.iota(iota_y[:, i2, :], pattern=[[1, 3], [0, 3], [-1, HEIGHT]], base=8 * i2 - 1, channel_multiplier=0,
                         allow_small_or_imprecise_dtypes=True))
            k(g.iota(iota_x[:], pattern=[[0, 3], [1, 3], [-1, WIDTH]], base=-1, channel_multiplier=0,
                     allow_small_or_imprecise_dtypes=True))
            k(g.iota(iota_n[:], pattern=[[1, P]], base=0, channel_multiplier=0, allow_small_or_imprecise_dtypes=True))
            k(g.iota(iota_j[:], pattern=[[1, NPO]], base=0, channel_multiplier=0, allow_small_or_imprecise_dtypes=True))
            k(g.memset(tri[:], 1.0))
            k(g.affine_select(out=tri[:], in_=tri[:], compare_op=ALU.is_gt, fill=0.0, base=0,
                              pattern=[[1, P]], channel_multiplier=-1))
            k(g.memset(sel[:], 0.0))
            for part in range(3):
                k(g.affine_select(out=sel[:], in_=sel[:], compare_op=ALU.not_equal, fill=1.0, base=-32 * part,
                                  pattern=[[-1, 32]], channel_multiplier=1))
            k(g.memset(tiebreak[:], 1.0))
            g.affine_select(out=tiebreak[:], in_=tiebreak[:], compare_op=ALU.is_gt, fill=0.0, base=0,
                            pattern=[[1, EXP], [-1, EXP]], channel_multiplier=0).then_inc(s["const_ready"], 1)

            for i in range(NT):
                if i % TPQ == 0:
                    g.wait_ge(s["wx_ready"], i // TPQ + 1)
                if i >= 2:
                    g.wait_ge(s["st_psum"], 3 * i - 3)
                kk = slice(K2 - POOL_TAPS, K2)
                g.tensor_tensor(s_buf[i % 2][:, kk], wy[:, i, kk].unsqueeze(3).to_broadcast([P, POOL_TAPS, HEIGHT, WIDTH]),
                                wx[:, i, kk].unsqueeze(2).to_broadcast([P, POOL_TAPS, HEIGHT, WIDTH]), ALU.mult).then_inc(s["s2_ready"], 1)
            for d in range(2):
                g.wait_ge(s["mid_ready"], d + 1)
                g.tensor_tensor(bc3[d][0:32, :], r1[0:32, :], bc3[d][0:32, :], ALU.subtract).then_inc(s["bc_ready"], 1)
                g.wait_ge(s["dt_ready"], d + 1)
                g.tensor_tensor(uu[d], dtv[d], xs[d], ALU.mult).then_inc(s["uu_ready"], 1)
            g.wait_ge(s["bc_ready"], 2)
            for blk in range(4):
                with g.Fori(0, DS // 2) as it:
                    for e in range(2):
                        n = it * 2 + (16 * blk + e)
                        g.wait_ge(s["scan_ready"], n + 3)
                        g.wait_ge(s["c_ready"], n + 2)
                        g.wait_ge(s["g_used"], n + 1)
                        g.tensor_tensor(gg[e], hh[e], cs[e], ALU.mult).then_inc(s["g_ready"], 1)

            g.wait_ge(s["tab_out"], 16)
            g.wait_ge(s["idx_ready"], 1)
            for w in range(W):
                g.indirect_dma_start(out=nb[:, w, :], out_offset=None, in_=tab_d,
                                     in_offset=bass.IndirectOffsetOnAxis(ap=src_idx[:, w:w + 1], axis=0)).then_inc(s[f"nb_in{sum(w >= x for x in W_AT[1:])}"], 16)
            g.sem_inc(s["pause_step"], 1)
            g.wait_ge(s["left_known"], 1)
            rounds = g.value_load(nleft_i[0:1, 0:1], min_val=0, max_val=EPP)
            with g.If(rounds > 0):
                with g.Fori(0, rounds) as r:
                    with g.Fori(0, 8) as c:
                        n = r * 8 + c
                        g.wait_ge(s["left_idx_ready"], n + 1)
                        g.wait_ge(s["pause_step"], n * 3 + 1)
                        g.tensor_tensor(pause[:, 0:1], pause[:, 2:3], pause[:, 2:3], ALU.add).then_inc(s["pause_step"], 1)
                        g.indirect_dma_start(out=left_row[:, 0:ROW], out_offset=None, in_=tab_d,
                                             in_offset=bass.IndirectOffsetOnAxis(ap=left_idx[:, 0:1], axis=0)).then_inc(s["left_row_in"], 16)
                        g.wait_ge(s["left_row_in"], n * 16 + 16)
                        g.wait_ge(s["pause_step"], n * 3 + 2)
                        g.tensor_tensor(pause[:, 0:1], pause[:, 2:3], pause[:, 2:3], ALU.add).then_inc(s["pause_step"], 1)
                        g.dma_start(left_d.rearrange("o (p r) -> (o p) r", p=P), left_row[:]).then_inc(s["left_out"], 16)
                        g.wait_ge(s["left_out"], n * 16 + 16)
                        g.wait_ge(s["pause_step"], n * 3 + 3)
                        g.tensor_tensor(pause[:, 0:1], pause[:, 2:3], pause[:, 2:3], ALU.add).then_inc(s["pause_step"], 1)
                        g.dma_start(left_all.rearrange("p e r -> p (e r)"), left_d.to_broadcast([P, P * (ROW + 1)])).then_inc(s["left_in"], 16)
                        g.wait_ge(s["left_in"], n * 16 + 16)
            g.wait_ge(s["gate_ready"], 1)
            g.wait_ge(s["eo_read"], 4)
            jj = slice(DVE_NODES, NPO)
            ev = eo[:, jj].rearrange("p j e c -> p (j e) c")
            k(g.tensor_tensor(ev, ev, gate[:, jj].rearrange("p j e -> p (j e)").unsqueeze(2).to_broadcast([P, (NPO - DVE_NODES) * EXP, C]), ALU.mult))
            k(g.tensor_tensor(eo[:, jj, 0:2, :], eo[:, jj, 0:2, :], eo[:, jj, 2:4, :], ALU.add))
            k(g.tensor_tensor(t2[:, jj], t2[:, jj], eo[:, jj, 0, :], ALU.add))
            g.tensor_tensor(t2[:, jj], t2[:, jj], eo[:, jj, 1, :], ALU.add).then_inc(s["out2_ready"], 1)

        @block.tensor
        def _(pe):
            pe.wait_ge(s["ident_ready"], 1)
            pe.wait_ge(s["xdup_in"], 32)
            for i in range(NT):
                m = pe.transpose(ps[:, i // 4, (i % 4) * P:(i % 4) * P + P], x_dup[:, i].rearrange("p r c -> p (r c)"), ident[:])
                if i % 4 == 3:
                    m.then_inc(s["xt_ready"], 1)
            pe.wait_ge(s["const_ready"], 1)
            pe.wait_ge(s["stats_ready"], 1)
            pe.matmul(ps[:, 4, 0:2 * BATCH], pairmat[:], ms[:].rearrange("p b s -> p (b s)"), start=True, stop=True).then_inc(s["pair_ready"], 1)
            pe.wait_ge(s["wconv_in"], 96)

            def om_chunk(q):
                pe.wait_ge(s["xhat_ready"], 2 * q + 2)
                pe.wait_ge(s["xhat2_ready"], 2 * q + 2)
                if q >= 2:
                    pe.wait_ge(s["omt_ready"], q - 1)
                o = ps[0:OM, (4, 7)[q % 2], :]
                for ky in range(3):
                    pe.matmul(o, w_om2[:, ky, :], xpad[:, 2 * q:2 * q + 2, ky:ky + HEIGHT, 0:WIDTH], start=(ky == 0), stop=False)
                for ky in range(3):
                    m = pe.matmul(o, w_om1[:, ky, :], xpad[0:C, 2 * q:2 * q + 2, ky:ky + HEIGHT, 2:2 + WIDTH], start=False, stop=(ky == 2))
                m.then_inc(s["omt_psum"], 1)

            def om_turn(q):
                pe.wait_ge(s["omt_ready"], q + 1)
                if q >= 2:
                    pe.wait_ge(s["om_read"], q - 1)
                for i in range(TPQ):
                    m = pe.transpose(ps[:, 5 + q % 2, OM * i:OM * i + OM], om_t[:, P * (TPQ * q + i):P * (TPQ * q + i) + P], ident[0:OM, 0:OM])
                m.then_inc(s["om_ready"], 1)

            def xk_part(n):
                b, tau, hf = n // 4, (n // 2) % 2, n % 2
                if n >= 1:
                    pe.wait_ge(s["xk_ready"], n)
                pe.matmul(ps[:, 7, 0:288], xc[:, b, P * tau:P * tau + P],
                          w_cv[:].rearrange("p k n -> p (k n)")[:, 288 * hf:288 * hf + 288], start=True, stop=True).then_inc(s["xk_psum"], 1)

            def conv_tail(i):
                b = i // 2
                pe.wait_ge(s["st_ready"], 3 * i + 3)
                pe.wait_ge(s["xk_ready"], 4 * b + 4)
                if i >= 2:
                    pe.wait_ge(s["t1_ready"], i - 1)
                else:
                    pe.wait_ge(s["om_read"], OMQ)
                o = ps[:, 5 + i % 2, 0:C]
                pe.matmul(o, ones_f[:], b_cv[:], start=True, stop=False)
                for t in range(K2):
                    for tau in range(2):
                        m = pe.matmul(o, s_t[i % 2][:, 2 * t + tau, :], xk[b % 2][:, tau, C * t:C * t + C],
                                      start=False, stop=(t == K2 - 1 and tau == 1))
                m.then_inc(s["conv_out"], 1)

            def hist_chunk(ch):
                pe.wait_ge(s["onehot_ready"], ch + 1)
                for e in range(0, CHUNKS[ch][1], 4):
                    for q in range(4):
                        m = pe.matmul(ps[32 * q:32 * q + 32, 4, 0:LO], one_hi[:, :, e + q], one_lo[:, :, e + q],
                                      start=(ch == 0 and e == 0), stop=(ch == len(CHUNKS) - 1 and e == CHUNKS[ch][1] - 4),
                                      tile_position=(0, 32 * q))
                m.then_inc(s["onehot_used"], 1)

            om_chunk(0)
            om_chunk(1)
            om_turn(0)
            om_chunk(2)
            om_turn(1)
            om_chunk(3)
            om_turn(2)
            om_turn(3)
            pe.wait_ge(s["xc_ready"], 1)
            for n in range(4):
                xk_part(n)
            for i in range(NT):
                pe.wait_ge(s["s_ready"], i + 1)
                pe.wait_ge(s["s2_ready"], i + 1)
                for q in range(3):
                    n = 3 * i + q
                    if n >= 2:
                        pe.wait_ge(s["st_ready"], n - 1)
                    for v in range(6):
                        t = 6 * q + v
                        m = pe.transpose(ps[:, 2 * (n % 2) + v // 4, (v % 4) * P:(v % 4) * P + P],
                                         s_rows[i % 2][:, t // 2, (t % 2) * P:(t % 2) * P + P], ident[:])
                    m.then_inc(s["st_psum"], 1)
                if i < NT - 2:
                    xk_part(4 + 2 * i)
                if i:
                    conv_tail(i - 1)
                if i < NT - 2:
                    xk_part(5 + 2 * i)
                if i % 2 == 0 and 1 <= i // 2 < len(CHUNKS):
                    hist_chunk(i // 2 - 1)
            conv_tail(NT - 1)

            pe.wait_ge(s["own_ready"], 1)
            pe.wait_ge(s["t1_ready"], NT - 1)
            for c in range(CAP):
                m = pe.matmul(ps[:, 5, 0:P], tri[:], own1[:, c, :], start=(c == 0), stop=(c == CAP - 1))
            m.then_inc(s["base_psum"], 1)
            hist_chunk(len(CHUNKS) - 1)
            for i in range(NT):
                if i in (0, NT - TPQ):
                    pe.wait_ge(s["xn2_ready"], 1 + (i > 0))
                m = pe.transpose(ps[:, i // 4, (i % 4) * P:(i % 4) * P + P], xn2[:, i].rearrange("p r c -> p (r c)"), ident[:])
                if i in (NT - TPQ - 1, NT - 1):
                    m.then_inc(s["xnt_psum"], 1)
            pe.wait_ge(s["xnt_ready"], 4)
            pe.wait_ge(s["taps_ready"], 4)
            pe.wait_ge(s["wmamba_in"], 2 * 8 * 16)
            for d in range(2):
                pe.matmul(ps[:, 7, DI * d:DI * d + DI], xd_w[d][:], dp_w[d][:], start=True, stop=True).then_inc(s["dtw_psum"], 1)

            def project_x(d):
                for hf in range(2):
                    if d:
                        pe.wait_ge(s["rest_ready"], hf + 1)
                    for q in (2 * hf, 2 * hf + 1):
                        for j in range(TAPS // 2):
                            shift = 2 * j if d == 0 else TAPS + 1 - 2 * j
                            m = pe.matmul(ps[:, q, :], w_tap[d][:, j, :], xnt[:, 2 * q:2 * q + 2, shift:shift + SEQ],
                                          start=(j == 0), stop=(j == TAPS // 2 - 1))
                    m.then_inc(s["xs_psum"], 1)

            def project_z(d):
                for hf in range(2):
                    if d:
                        pe.wait_ge(s["sp_abs"], 2 + hf + 1)
                        pe.wait_ge(s["sp_relu"], 2 + hf + 1)
                    for q in (2 * hf, 2 * hf + 1):
                        m = pe.matmul(ps[:, 4 + q, :], in_w[d][0:C, DI:2 * DI], xnt[0:C, 2 * q:2 * q + 2, TAPS - 1:TAPS - 1 + SEQ],
                                      start=True, stop=True)
                    m.then_inc(s["z_psum"], 1)

            def project_bc_dt(d):
                for hf in range(2):
                    pe.wait_ge(s["xs_ready"], 2 * d + hf + 1)
                    for q in (2 * hf, 2 * hf + 1):
                        m = pe.matmul(ps[0:96, q, :], xp_w[d][:], xs[d][:, 512 * q:512 * q + 512], start=True, stop=True)
                    m.then_inc(s["dbc_psum"], 1)
                for hf in range(2):
                    if d == 0:
                        pe.wait_ge(s["z_ready"], hf + 1)
                    else:
                        pe.wait_ge(s["sp_abs"], hf + 1)
                        pe.wait_ge(s["sp_relu"], hf + 1)
                    for q in (2 * hf, 2 * hf + 1):
                        m = pe.matmul(ps[:, 4 + q, :], dt_w[d][:], xs[d][:, 512 * q:512 * q + 512], start=True, stop=True)
                    m.then_inc(s["dt_psum"], 1)

            project_x(0)
            pe.wait_ge(s["base_read"], 1)
            pe.wait_ge(s["dtw_ready"], 2)
            project_z(0)
            project_bc_dt(0)
            pe.wait_ge(s["rest_ready"], 1)
            pe.wait_ge(s["pay_ready"], 1)
            for c in range(CAP):
                m = pe.matmul(ps[:, 0, 0:2 * W], own1[:, c, :], pay[:, c, :, :].rearrange("p h w -> p (h w)"),
                              start=(c == 0), stop=(c == CAP - 1))
            m.then_inc(s["ell_psum"], 1)
            pe.wait_ge(s["left_count"], 1)
            pe.transpose(ps[0:1, 1, 0:P], nleft[:, 0:1], ident[:]).then_inc(s["left_psum"], 1)
            pe.wait_ge(s["idx_ready"], 1)
            pe.wait_ge(s["left_known"], 1)
            project_x(1)
            project_bc_dt(1)
            project_z(1)

            def rows(d, hf, i0, n, e):
                pe.wait_ge(s["b_used"], n + 1)
                for q in range(2):
                    m = pe.matmul(ps[:, 6 * e + q, :], sel[:, i0].to_broadcast([96, P]),
                                  bc3[d][0:96, hf * HALF + 512 * q:hf * HALF + 512 * q + 512], start=True, stop=True)
                m.then_inc(s["b_psum"], 1)

            def rows_c(d, hf, i0, n):
                pe.wait_ge(s["c_ready"], n + 1)
                for q in range(2):
                    m = pe.matmul(ps[:, 2 + q, :], sel[:, i0].to_broadcast([96, P]),
                                  bc3[d][0:96, hf * HALF + 512 * q:hf * HALF + 512 * q + 512], start=True, stop=True)
                m.then_inc(s["c_psum"], 1)

            def add_state(n, e):
                pe.wait_ge(s["g_ready"], n + 3)
                for q in range(2):
                    m = pe.matmul(ps[:, 4 + q, :], ident[:], gg[e][:, 512 * q:512 * q + 512], start=False, stop=True, skip_group_check=True)
                m.then_inc(s["g_used"], 1)

            def first_rows(blk):
                d, hf = blk // 2, blk % 2
                pe.wait_ge(s["bc_ready"], d + 1)
                for e in range(2):
                    rows(d, hf, slice(e, e + 1), 16 * blk + e, e)
                    rows_c(d, hf, slice(DS + e, DS + e + 1), 16 * blk + e)

            pe.wait_ge(s["z_ready"], 4)
            pe.wait_ge(s["rest_ready"], 4)
            pe.wait_ge(s["diag_ready"], 2)
            first_rows(0)
            for blk in range(4):
                d, hf = blk // 2, blk % 2
                for e in range(2):
                    rows(d, hf, slice(2 + e, 3 + e), 16 * blk + 2 + e, e)
                    rows_c(d, hf, slice(DS + 2 + e, DS + 3 + e), 16 * blk + 2 + e)
                if blk:
                    pe.wait_ge(s["yg_ready"], blk)
                for q in range(2):
                    c0 = hf * HALF + 512 * q
                    pe.matmul(ps[:, 4 + q, :], diag_d[d][:], xs[d][:, c0:c0 + 512], start=True, stop=True)
                for e in range(2):
                    add_state(16 * blk + e, e)
                with pe.Fori(0, DS // 2 - 2) as it:
                    for e in range(2):
                        n = it * 2 + (16 * blk + 2 + e)
                        rows(d, hf, bass.ds(it * 2 + (4 + e), 1), n + 2, e)
                        rows_c(d, hf, bass.ds(it * 2 + (DS + 4 + e), 1), n + 2)
                        add_state(n, e)
                if blk < 3:
                    first_rows(blk + 1)
                for e in range(2):
                    add_state(16 * blk + DS - 2 + e, e)

            pe.wait_ge(s["yg_ready"], 4)
            for j in range(NPO):
                o = ps[:, 0 + j // 8, C * (j % 8):C * (j % 8) + C]
                for d in range(2):
                    m = pe.matmul(o, zs[d][:, j:T:NPO], o_w[d][:], start=(d == 0), stop=(d == 1))
            m.then_inc(s["t2_psum"], 1)
            for j in range(NPO):
                if j % (NPO // 2) == 0:
                    pe.wait_ge(s["diff_ready"], 1 + j // (NPO // 2))
                m = pe.transpose(ps[0:C, 4 + j // 4, (j % 4) * P:(j % 4) * P + P], d_tok[:, j, :], ident[:])
                if j % 4 == 3:
                    m.then_inc(s["dt2_psum"], 1)
            pe.wait_ge(s["wffn_in"], 80)
            for j in range(NPO):
                if j % 4 == 0:
                    pe.wait_ge(s["dt2_ready"], j // 4 + 1)
                m = pe.matmul(ps[:, 2, HE * j:HE * j + HE], diff_t[:, P * j:P * j + P], w_gat[:], start=True, stop=True)
            m.then_inc(s["h_psum"], 1)
            pe.wait_ge(s["v_ready"], 1)
            for j in range(NPO):
                m = pe.transpose(ps[0:C, 4 + j // 4, (j % 4) * P:(j % 4) * P + P], v_tok[:, j, :], ident[:])
                if j % 4 == 3:
                    m.then_inc(s["vt_psum"], 1)
            def expert_out(n):
                q, e = n // EXP, n % EXP
                if e == 0:
                    if q >= 2:
                        pe.wait_ge(s["eo_read"], q - 1)
                    for bank in range(2):
                        for part in range(3):
                            pe.matmul(ps[:, 4 * (q % 2) + bank, :], ones_b[:], b2_part[:, part:part + 1, :].to_broadcast([1, 2, EXP * C]),
                                      start=(part == 0), stop=(part == 2))
                pe.wait_ge(s["hid_ready"], n + 1)
                for jj in range(4):
                    o = 256 * (jj % 2) + C * e
                    m = pe.matmul(ps[:, 4 * (q % 2) + jj // 2, o:o + C], hid[n % 2][:, P * jj:P * jj + P], w2[:, e, :],
                                  start=False, stop=True, skip_group_check=True)
                m.then_inc(s["eo_psum"], 1)

            pe.wait_ge(s["b2_ready"], 1)
            for n in range(4 * EXP):
                q, e = n // EXP, n % EXP
                if n >= 2:
                    pe.wait_ge(s["hid_ready"], n - 1)
                else:
                    pe.wait_ge(s["vt_ready"], 4)
                pe.matmul(ps[:, 6 + n % 2, :], w1[:, e, :], vt[:, 512 * q:512 * q + 512], start=True, stop=True).then_inc(s["hid_psum"], 1)
                if n:
                    expert_out(n - 1)
            expert_out(4 * EXP - 1)

        @block.scalar
        def _(act):
            f = act.activation
            k = Link(act, s["act_step"])
            act.wait_ge(s["var_ready"], 1)
            f(gnv[:, 1, :], gnv[:, 0, :], ACT.Sqrt).then_inc(s["std_ready"], 1)
            act.wait_ge(s["const_ready"], 1)
            act.wait_ge(s["gn_ready"], 1)
            for b in range(BATCH):
                f(xpad[C:P, b, 1:1 + HEIGHT, 0:WIDTH], ps[C:P, b // 2, (b % 2) * SEQ:(b % 2) * SEQ + SEQ].rearrange("p (y x) -> p y x", x=WIDTH),
                  ACT.Identity, scale=gnv[C:P, 1, b:b + 1], bias=gnv[C:P, 2, b:b + 1]).then_inc(s["xhat2_ready"], 1)
            act.wait_ge(s["xhat_ready"], BATCH)
            f(xc.rearrange("p b (y x) -> p b y x", x=WIDTH), xpad[0:C, :, 1:1 + HEIGHT, 1:1 + WIDTH], ACT.Copy).then_inc(s["xc_ready"], 1)

            def om_copy(q):
                act.wait_ge(s["omt_psum"], q + 1)
                f(om_t[:, 512 * q:512 * q + 512], ps[0:OM, (4, 7)[q % 2], :], ACT.Identity, bias=b_om[:]).then_inc(s["omt_ready"], 1)

            def hats(q):
                ii = slice(TPQ * q, TPQ * q + TPQ)
                act.wait_ge(s["off_ready"], q + 1)
                f(wx[:, ii], wx[:, ii], ACT.Abs, bias=pl[:]).then_inc(s["abs_step"], 1)
                f(wy[:, ii], wy[:, ii], ACT.Abs, bias=ph[:]).then_inc(s["abs_step"], 1)
                act.wait_ge(s["abs_step"], 2 * q + 1)
                f(wx[:, ii], wx[:, ii], ACT.Relu, scale=-1.0, bias=1.0)
                act.wait_ge(s["abs_step"], 2 * q + 2)
                f(wy[:, ii], wy[:, ii], ACT.Relu, scale=-1.0, bias=1.0)
                f(msk[:, ii], om[:, ii, 2 * K2:OM], ACT.Sigmoid).then_inc(s["hat_ready"], 1)

            om_copy(0)
            om_copy(1)
            hats(0)
            om_copy(2)
            om_copy(3)

            def xk_copy(n):
                b, tau, hf = n // 4, (n // 2) % 2, n % 2
                act.wait_ge(s["xk_psum"], n + 1)
                if b >= 2:
                    act.wait_ge(s["conv_out"], 2 * b - 2)
                f(xk[b % 2][:, tau, 288 * hf:288 * hf + 288], ps[:, 7, 0:288], ACT.Copy).then_inc(s["xk_ready"], 1)

            def ln_root(n):
                sl = slice(TPQ * (n // 2), TPQ * (n // 2) + TPQ)
                act.wait_ge(s["ln_var"], n + 1)
                f(lns[:, 4, sl], lns[:, 3, sl], ACT.Sqrt).then_inc(s["ln_std"], 1)

            for n in range(4):
                xk_copy(n)
            for i in range(NT):
                if i >= 2:
                    act.wait_ge(s["conv_out"], i - 1)
                for q in range(3):
                    n = 3 * i + q
                    act.wait_ge(s["st_psum"], n + 1)
                    f(s_t[i % 2][:, 6 * q:6 * q + 6, :].rearrange("p n q -> p (n q)"), banks(2 * (n % 2), 2)[:, 0:6 * P], ACT.Copy).then_inc(s["st_ready"], 1)
                if i < NT - 2:
                    xk_copy(4 + 2 * i)
                    xk_copy(5 + 2 * i)
                if 1 <= i < OMQ:
                    hats(i)
                if i >= 6 and i % TPQ in (2, 3):
                    ln_root(2 * (i // TPQ - 1) + i % 2)
            ln_root(6)
            act.wait_ge(s["s_ready"], NT)
            act.wait_ge(s["s2_ready"], NT)
            for part in range(2):
                sl = slice(0, NT - TPQ) if part == 0 else slice(NT - TPQ, NT)
                act.wait_ge(s["xn_ready"], 3 + part)
                f(xn2[:, sl, 0, :], x_tok[:, sl], ACT.Copy)
                f(xn2[:, sl, 1, :], x_tok[:, sl], ACT.Copy).then_inc(s["xn2_ready"], 1)
                if part == 0:
                    ln_root(7)
            act.wait_ge(s["gb_in"], 32)
            act.wait_ge(s["da_zero"], 1)
            for part in range(2):
                act.wait_ge(s["xnt_psum"], part + 1)
                bb = slice(0, 6) if part == 0 else slice(6, 8)
                for r in range(2):
                    rr = slice(C * r, C * r + C)
                    f(xnt[rr, bb, TAPS - 1 - r:TAPS - 1 - r + SEQ], ps[rr, 3 * part:3 + part, :].rearrange("p b n -> p (b n)").rearrange("p (b s) -> p b s", s=SEQ),
                      ACT.Identity, scale=gb[rr, 0:1], bias=gb[rr, 1:2]).then_inc(s["xnt_ready"], 1)
            act.wait_ge(s["wmamba_in"], 2 * 8 * 16)
            for d in range(2):
                f(neg_a[d][:], neg_a[d][:], ACT.Exp).then_inc(s["nega_ready"], 1)
            for d in range(2):
                act.wait_ge(s["dtw_psum"], 2)
                f(dt_w[d][:], ps[:, 7, DI * d:DI * d + DI], ACT.Copy).then_inc(s["dtw_ready"], 1)
            cols = [slice(HALF * hf, HALF * hf + HALF) for hf in range(2)]

            def silu_z(d):
                for hf in range(2):
                    act.wait_ge(s["z_psum"], 2 * d + hf + 1)
                    f(zs[d][:, cols[hf]], banks(4 + 2 * hf, 2), ACT.Silu).then_inc(s["z_ready"], 1)

            for d in range(2):
                for hf in range(2):
                    act.wait_ge(s["xs_psum"], 2 * d + hf + 1)
                    f(xs[d][:, cols[hf]], banks(2 * hf, 2), ACT.Silu, bias=vec[d][:, 0:1]).then_inc(s["xs_ready"], 1)
                if d == 0:
                    silu_z(d)
                for hf in range(2):
                    act.wait_ge(s["dbc_psum"], 2 * d + hf + 1)
                    f(bc3[d][0:96, cols[hf]], banks(2 * hf, 2, 96), ACT.Copy).then_inc(s["hi_ready"], 1)
                if d:
                    act.wait_ge(s["dt_ready"], d)
                for hf in range(2):
                    act.wait_ge(s["dt_psum"], 2 * d + hf + 1)
                    if d == 0:
                        f(dtv[d][:, cols[hf]], banks(4 + 2 * hf, 2), ACT.Relu, bias=vec[d][:, 1:2]).then_inc(s["sp_relu"], 1)
                    f(sp_t[:, cols[hf]], banks(4 + 2 * hf, 2), ACT.Abs, bias=vec[d][:, 1:2]).then_inc(s["sp_abs"], 1)
                act.wait_ge(s["sp_abs"], 2 * d + 2)
                f(sp_t, sp_t, ACT.Exp, scale=-1.0).then_inc(s["sp_exp"], 1)
                act.wait_ge(s["sp_exp"], d + 1)
                f(uu[d], sp_t, ACT.Ln, bias=1.0).then_inc(s["sp_ln"], 1)
                act.wait_ge(s["rest_ready"], 2 * d + 2)
                f(bc3[d][0:64, :], r1, ACT.Copy).then_inc(s["mid_ready"], 1)
            silu_z(1)
            for d in range(2):
                act.wait_ge(s["dt_ready"], d + 1)
                act.wait_ge(s["da_zero"], 2 + d)
                lo = 1 - d
                for hf in range(2):
                    blk, c0 = 2 * d + hf, hf * HALF
                    src = dtv[d][:, c0:c0 + HALF].rearrange("p (b s) -> p b s", s=SEQ)[:, :, lo:lo + SEQ - 1]
                    with act.Fori(0, DS // 2) as it:
                        for e in range(2):
                            n = it * 2 + (16 * blk + e)
                            act.wait_ge(s["scan_ready"], n + 1)
                            f(da[e].rearrange("p (b s) -> p b s", s=SEQ)[:, :, lo:lo + SEQ - 1], src, ACT.Exp,
                              scale=neg_a[d][:, bass.ds(it * 2 + e, 1)]).then_inc(s["da_ready"], 1)
                            act.wait_ge(s["c_psum"], n + 1)
                            act.wait_ge(s["g_ready"], n + 1)
                            f(cs[e], banks(2, 2), ACT.Copy).then_inc(s["c_ready"], 1)
            f(pause[:, 3:4], ident[:, 0:1], ACT.Sqrt)
            for q in range(4):
                act.wait_ge(s["dt2_psum"], q + 1)
                f(diff_t[:, 512 * q:512 * q + 512], ps[0:C, 4 + q, :], ACT.Copy).then_inc(s["dt2_ready"], 1)
            act.wait_ge(s["ln_var"], 9)
            f(lns[:, 4, :], lns[:, 3, :], ACT.Sqrt).then_inc(s["ln_std"], 1)
            for q in range(4):
                act.wait_ge(s["vt_psum"], q + 1)
                f(vt[:, 512 * q:512 * q + 512], ps[0:C, 4 + q, :], ACT.Copy).then_inc(s["vt_ready"], 1)
            act.wait_ge(s["e_in"], 1)
            f(g1[:], g1[:], ACT.Exp).then_inc(s["exp_ready"], 1)
            f(g2[:], g2[:], ACT.Exp).then_inc(s["exp_ready"], 1)

            def hidden(n):
                q, e = n // EXP, n % EXP
                act.wait_ge(s["hid_psum"], n + 1)
                if n >= 2:
                    act.wait_ge(s["eo_psum"], n - 1)
                f(hid[n % 2], ps[:, 6 + n % 2, :], ACT.Gelu, bias=b1[:, e:e + 1]).then_inc(s["hid_ready"], 1)
                if e == 0 and q:
                    act.wait_ge(s["eo_psum"], 4 * q)
                    f(eo[:, 4 * q - 4:4 * q].rearrange("p j e c -> p (j e c)"), banks(4 * ((q - 1) % 2), 2), ACT.Copy).then_inc(s["eo_read"], 1)

            done = 0
            for c in range(WCH):
                upto = (2, 6, 10, 14)[c]
                for n in range(done, upto):
                    hidden(n)
                done = upto
                act.wait_ge(s["e_in"], c + 2)
                f(g1[:], g1[:], ACT.Exp).then_inc(s["exp_ready"], 1)
                e_w = chunk_weights(W_AT[c + 1] - W_AT[c])
                f(e_w, e_w, ACT.Exp).then_inc(s["exp_ready"], 1)
            for n in range(done, 4 * EXP):
                hidden(n)
            act.wait_ge(s["eo_psum"], 4 * EXP)
            f(eo[:, 12:16].rearrange("p j e c -> p (j e c)"), banks(4, 2), ACT.Copy).then_inc(s["eo_read"], 1)
            rounds = act.value_load(nleft_i[0:1, 0:1], min_val=0, max_val=EPP)
            with act.If(rounds > 0):
                with act.Fori(0, rounds) as r:
                    with act.Fori(0, 8 * (P // LW)) as c:
                        n = r * (8 * (P // LW)) + c
                        act.wait_ge(s["left_e"], n + 1)
                        f(g1[:], g1[:], ACT.Exp).then_inc(s["left_exp"], 1)
                        f(left_w, left_w, ACT.Exp).then_inc(s["left_exp"], 1)
            act.wait_ge(s["ln_var"], 10)
            f(gs[:, 4, :], gs[:, 3, :], ACT.Sqrt).then_inc(s["ln_std"], 1)
            act.wait_ge(s["ln_var"], 11)
            f(gate[:], gate[:], ACT.Exp).then_inc(s["ln_std"], 1)

        @block.vector
        def _(v):
            k = Link(v, s["dve_step"])

            def bc(ap, axis, n):
                shape = list(ap.unsqueeze(axis).shape)
                shape[axis] = n
                return ap.unsqueeze(axis).to_broadcast(shape)

            tt, ts, stt = v.tensor_tensor, v.tensor_scalar, v.scalar_tensor_tensor

            v.sem_inc(s["b_used"], 2)
            v.sem_inc(s["c_ready"], 1)
            v.sem_inc(s["g_ready"], 2)
            v.sem_inc(s["g_used"], 2)
            v.sem_inc(s["scan_ready"], 2)

            v.memset(pause[:], 0.0)
            for b in range(BATCH):
                if b % 2 == 0:
                    v.wait_ge(s["xt_ready"], b // 2 + 1)
                k.go(v.bn_stats(out=st6[:, b, :], in_=ps[:, b // 2, (b % 2) * SEQ:(b % 2) * SEQ + SEQ]))
            k.wait()
            for b in range(BATCH):
                k.go(v.bn_aggr(out=mv[:, b, :], in_=st6[:, b, :]))
            k.wait()
            k(v.tensor_copy(ms[:, :, 0], mv[:, :, 0]))
            k(tt(ms[:, :, 1], mv[:, :, 0], mv[:, :, 0], ALU.mult))
            tt(ms[:, :, 1], ms[:, :, 1], mv[:, :, 1], ALU.add).then_inc(s["stats_ready"], 1)
            v.wait_ge(s["pair_ready"], 1)
            k(v.tensor_copy(gnm[:].rearrange("p b s -> p (b s)"), ps[:, 4, 0:2 * BATCH]))
            k(tt(gnv[:, 0, :], gnm[:, :, 0], gnm[:, :, 0], ALU.mult))
            k(tt(gnv[:, 0, :], gnm[:, :, 1], gnv[:, 0, :], ALU.subtract))
            ts(gnv[:, 0, :], gnv[:, 0, :], 1e-5, None, ALU.add).then_inc(s["var_ready"], 1)
            v.wait_ge(s["std_ready"], 1)
            k(v.reciprocal(gnv[:, 1, :], gnv[:, 1, :]))
            stt(out=gnv[:, 2, :], in0=gnm[:, :, 0], scalar=-1.0, in1=gnv[:, 1, :], op0=ALU.mult, op1=ALU.mult).then_inc(s["gn_ready"], 1)
            v.wait_ge(s["const_ready"], 1)
            for b in range(BATCH):
                ts(xpad[0:C, b, 1:1 + HEIGHT, 1:1 + WIDTH], ps[0:C, b // 2, (b % 2) * SEQ:(b % 2) * SEQ + SEQ].rearrange("p (y x) -> p y x", x=WIDTH),
                   gnm[0:C, b, 0:1], gnv[0:C, 1, b:b + 1], ALU.subtract, ALU.mult).then_inc(s["xhat_ready"], 1)
            k(ts(pi_tmp[:, 0:1], iota_pi[:], 4, None, ALU.arith_shift_right))
            k(ts(pi_tmp[:, 1:2], iota_pi[:], 15, None, ALU.bitwise_and))
            k(v.tensor_copy(ph[:], pi_tmp[:, 0:1]))
            k(v.tensor_copy(pl[:], pi_tmp[:, 1:2]))
            k(v.tensor_copy(pf[:], iota_pi[:]))
            v.wait_ge(s["cw_in"], 96)
            for d in range(2):
                for r in range(2):
                    rr, tap = slice(C * r, C * r + C), (r if d == 0 else 1 - r)
                    tt(w_tap[d][rr], bc(in_w[d][rr, 0:DI], 1, TAPS // 2), cw_b[d][rr, tap:TAPS:2, :], ALU.mult).then_inc(s["taps_ready"], 1)
            v.wait_ge(s["wmamba_in"], 2 * 8 * 16)
            for d in range(2):
                ts(diag_d[d][:], ident[:], vec[d][:, 2:3], None, ALU.mult).then_inc(s["diag_ready"], 1)

            v.wait_ge(s["edge_in"], 32)
            k.go(v.tensor_copy(e_tmp, src_i))
            k.go(v.tensor_copy(e_tm2, dst_i))
            k(ts(e_int, dst_i, LO - 1, None, ALU.bitwise_and))
            k(stt(out=keys[:, 0:EPP], in0=e_tm2, scalar=float(T), in1=e_tmp, op0=ALU.mult, op1=ALU.add))

            def read_om(q):
                v.wait_ge(s["om_ready"], q + 1)
                v.tensor_copy(om[:, TPQ * q:TPQ * q + TPQ].rearrange("p t n -> p (t n)"), ps[:, 5 + q % 2, 0:TPQ * OM]).then_inc(s["om_read"], 1)

            def offsets(q):
                ii = slice(TPQ * q, TPQ * q + TPQ)
                for i2 in range(2):
                    jj = slice(TPQ * q + i2, TPQ * q + TPQ, 2)
                    k.go(tt(wy[:, jj], bc(om[:, jj, 0:2 * K2:2], 3, HEIGHT),
                            bc(iota_y[:, i2, :].rearrange("p (k y) -> p k y", k=K2), 1, TPQ // 2), ALU.add))
                tt(wx[:, ii], bc(om[:, ii, 1:2 * K2:2], 3, WIDTH), bc(iota_x[:], 1, TPQ), ALU.add).then_inc(s["off_ready"], 1)

            def masks(q):
                ii = slice(TPQ * q, TPQ * q + TPQ)
                v.wait_ge(s["hat_ready"], q + 1)
                k(ts(msk[:, ii], msk[:, ii], 2.0, None, ALU.mult))
                tt(wx[:, ii], wx[:, ii], bc(msk[:, ii], 3, WIDTH), ALU.mult).then_inc(s["wx_ready"], 1)

            read_om(0)
            v.wait_ge(s["om_read"], 1)
            offsets(0)
            k(ts(e_tmp, e_tmp, float(LAST), None, ALU.is_lt))
            k.go(stt(out=lo_b[:], in0=e_tmp, scalar=float(LO), in1=e_int, op0=ALU.mult, op1=ALU.add))
            k(stt(out=e_tm2, in0=e_tm2, scalar=float(T), in1=e_tmp, op0=ALU.is_lt, op1=ALU.mult))
            k(stt(out=keys[:, 0:EPP], in0=keys[:, 0:EPP], scalar=1.0, in1=e_tm2, op0=ALU.add, op1=ALU.mult))
            k(ts(e_int, dst_i, 6, None, ALU.arith_shift_right))
            k.go(v.tensor_copy(hi_b[:], e_int))
            read_om(1)

            def conv_sum(i):
                v.wait_ge(s["conv_out"], i + 1)
                tt(x_tok[:, i, :], x_tok[:, i, :], ps[:, 5 + i % 2, 0:C], ALU.add).then_inc(s["t1_ready"], 1)

            def norm(dst, src, diff, sq, st, n, width, out_sem):
                k(v.tensor_reduce(out=st[:, 0, :], in_=src, axis=AX, op=ALU.add))
                k(ts(st[:, 1, :], st[:, 0, :], 1.0 / width, None, ALU.mult))
                k(tt(diff, src, bc(st[:, 1, :], 2, width), ALU.subtract))
                k(tt(sq, diff, diff, ALU.mult))
                k(v.tensor_reduce(out=st[:, 2, :], in_=sq, axis=AX, op=ALU.add))
                ts(st[:, 3, :], st[:, 2, :], 1.0 / width, 1e-5, ALU.mult, ALU.add).then_inc(s["ln_var"], 1)
                v.wait_ge(s["ln_std"], n)
                k(v.reciprocal(st[:, 5, :], st[:, 4, :]))
                m = tt(dst, diff, bc(st[:, 5, :], 2, width), ALU.mult)
                if out_sem is None:
                    k(m)
                else:
                    m.then_inc(out_sem, 1)

            def center(sl, src):
                k(v.tensor_reduce(out=lns[:, 0, sl], in_=src, axis=AX, op=ALU.add))
                k(ts(lns[:, 1, sl], lns[:, 0, sl], 1.0 / C, None, ALU.mult))
                k(tt(lnd, src, bc(lns[:, 1, sl], 2, C), ALU.subtract))
                k(tt(lsq, lnd, lnd, ALU.mult))
                k(v.tensor_reduce(out=lns[:, 2, sl], in_=lsq, axis=AX, op=ALU.add))
                ts(lns[:, 3, sl], lns[:, 2, sl], 1.0 / C, 1e-5, ALU.mult, ALU.add).then_inc(s["ln_var"], 1)

            def ln_first(g):
                sl = slice(TPQ * g, TPQ * g + TPQ)
                center(sl, x_tok[:, sl])

            def ln_second(g):
                sl = slice(TPQ * g, TPQ * g + TPQ)
                v.wait_ge(s["ln_std"], 2 * g + 1)
                k(v.reciprocal(lns[:, 5, sl], lns[:, 4, sl]))
                k(tt(un, lnd, bc(lns[:, 5, sl], 2, C), ALU.mult))
                tt(x_tok[:, sl], x_tok[:, sl], un, ALU.add).then_inc(s["res_ready"], 1)
                center(sl, un)

            def ln_end(g):
                sl = slice(TPQ * g, TPQ * g + TPQ)
                v.wait_ge(s["ln_std"], 2 * g + 2)
                k(v.reciprocal(lns[:, 5, sl], lns[:, 4, sl]))
                v.wait_ge(s["res_out"], 16 * g + 16)
                tt(x_tok[:, sl], lnd, bc(lns[:, 5, sl], 2, C), ALU.mult).then_inc(s["xn_ready"], 1)

            def onehots(ch, part):
                e0, en = CHUNKS[ch]
                if ch and part == 0:
                    v.wait_ge(s["onehot_used"], ch)
                for x in range(part * (HI + LO) // 2, (part + 1) * (HI + LO) // 2):
                    if x < HI:
                        m = ts(one_hi[:, x, 0:en], hi_b[:, e0:e0 + en], float(x), None, ALU.is_equal)
                    else:
                        m = ts(one_lo[:, x - HI, 0:en], lo_b[:, e0:e0 + en], float(x - HI), None, ALU.is_equal)
                    if x < HI + LO - 1:
                        k.go(m)
                    else:
                        m.then_inc(s["onehot_ready"], 1)

            def extract(r):
                k(v.max(out=comp[:, 8 * r:8 * r + 8], in_=keys[:, 0:EPP]))
                k.go(v.match_replace(out=keys[:, 0:EPP], in_to_replace=comp[:, 8 * r:8 * r + 8], in_values=keys[:, 0:EPP], imm_value=0.0))

            for i in range(NT):
                if i % TPQ == 0:
                    masks(i // TPQ)
                    v.wait_ge(s["wx_ready"], i // TPQ + 1)
                if i >= 2:
                    v.wait_ge(s["st_psum"], 3 * i - 3)
                kk = slice(0, K2 - POOL_TAPS)
                tt(s_buf[i % 2][:, kk], bc(wy[:, i, kk], 3, WIDTH), bc(wx[:, i, kk], 2, HEIGHT), ALU.mult).then_inc(s["s_ready"], 1)
                if i == 0:
                    v.wait_ge(s["x_in"], 16)
                    read_om(2)
                    read_om(3)
                    v.wait_ge(s["om_read"], OMQ)
                if 1 <= i < OMQ:
                    offsets(i)
                if i >= 3:
                    conv_sum(i - 3)
                g = i // TPQ - 1
                if g >= 0 and i % TPQ == 2:
                    v.wait_ge(s["t1_ready"], TPQ * g + TPQ)
                    ln_first(g)
                elif g >= 0 and i % TPQ == 3:
                    ln_second(g)
                elif g >= 1 and i % TPQ == 0:
                    ln_end(g - 1)
                if i % 2 and 1 <= i // 2 <= ROUNDS:
                    k.wait()
                    extract(i // 2 - 1)
                if 1 <= i <= 2 * len(CHUNKS):
                    onehots((i - 1) // 2, (i - 1) % 2)
            k.wait()
            k(ts(key_i[:], comp, -1.0, None, ALU.add))
            k(ts(int_a[:, 0, :], key_i[:], 15, None, ALU.arith_shift_right))
            k(v.tensor_copy(owner[:], int_a[:, 0, :]))
            k(v.tensor_copy(owner_b[:], owner[:]))
            k(ts(int_a[:, 0, :], key_i[:], 4, 127, ALU.arith_shift_right, ALU.bitwise_and))
            k(ts(dig[:, 0, :], int_a[:, 0, :], 1.0, None, ALU.add))
            k(ts(int_a[:, 1, :], key_i[:], 11, 15, ALU.arith_shift_right, ALU.bitwise_and))
            k(ts(int_a[:, 2, :], key_i[:], 15, None, ALU.bitwise_and))
            k(stt(out=dig[:, 1, :], in0=int_a[:, 2, :], scalar=16.0, in1=int_a[:, 1, :], op0=ALU.mult, op1=ALU.add))
            k(v.memset(same[:, 0:1], 0.0))
            k(tt(same[:, 1:CAP], owner[:, 1:CAP], owner[:, 0:CAP - 1], ALU.is_equal))
            k(v.tensor_tensor_scan(run[:], same[:], same[:], 0.0, ALU.mult, ALU.add))
            conv_sum(NT - 3)
            v.wait_ge(s["st_psum"], 3 * NT)
            tt(own1, bc(iota_n[:], 1, CAP), bc(owner_b[:], 2, P), ALU.is_equal).then_inc(s["own_ready"], 1)
            conv_sum(NT - 2)
            ln_end(2)
            conv_sum(NT - 1)
            v.wait_ge(s["t1_ready"], NT)
            ln_first(3)
            ln_second(3)
            ln_end(3)
            v.wait_ge(s["base_psum"], 1)
            k(ts(base_b[:], ps[:, 5, 0:P], float(P), None, ALU.min))
            v.sem_inc(s["base_read"], 1)
            k(tt(look, own1, bc(base_b[:], 1, CAP), ALU.mult))
            v.wait_ge(s["onehot_used"], len(CHUNKS))
            v.tensor_copy(hist_s[:], ps[:, 4, 0:LO]).then_inc(s["hist_ready"], 1)
            for r in range(2):
                rr = slice(C * r, C * r + C)
                k(v.memset(xnt[rr, :, 0:TAPS - 1 - r], 0.0))
                m = v.memset(xnt[rr, :, TAPS - 1 - r + SEQ:SEQP], 0.0)
                if r:
                    m.then_inc(s["da_zero"], 1)
                else:
                    k(m)

            k(v.tensor_reduce(out=slot[:], in_=look, axis=AX, op=ALU.add))
            k(tt(slot[:], slot[:], run[:], ALU.add))
            k(tt(slot1, bc(iota_n[:, 0:W], 1, CAP), bc(slot[:], 2, W), ALU.is_equal))
            k(tt(pay[:, :, 0, :], slot1, bc(dig[:, 0, :], 2, W), ALU.mult))
            tt(pay[:, :, 1, :], slot1, bc(dig[:, 1, :], 2, W), ALU.mult).then_inc(s["pay_ready"], 1)
            k(stt(out=comp, in0=slot[:], scalar=float(W) - 0.5, in1=comp, op0=ALU.is_gt, op1=ALU.mult))
            ts(key_tmp, keys[:], 0.5, 0.0, ALU.is_gt, ALU.add, accum_out=nleft[:, 0:1]).then_inc(s["left_count"], 1)
            for d in range(2):
                for hf in range(2):
                    cols = slice(HALF * hf, HALF * hf + HALF)
                    v.wait_ge(s["hi_ready"], 2 * d + hf + 1)
                    tt(r1[:, cols], banks(2 * hf, 2, 64), bc3[d][0:64, cols], ALU.subtract).then_inc(s["rest_ready"], 1)
                if d == 0:
                    v.wait_ge(s["left_psum"], 1)
                    k(v.reduce_max(nleft[0:1, 1:2], ps[0:1, 1, 0:P], AX))
                    k(ts(nleft_i[0:1, 1:2], nleft[0:1, 1:2], 7.0, None, ALU.add))
                    ts(nleft_i[0:1, 0:1], nleft_i[0:1, 1:2], 3, None, ALU.arith_shift_right).then_inc(s["left_known"], 1)
                    v.wait_ge(s["ell_psum"], 1)
                    k(v.tensor_copy(ell[:].rearrange("p h w -> p (h w)"), ps[:, 0, 0:2 * W]))
                    k(v.tensor_copy(ell_i[:, 0, :], ell[:, 1, :]))
                    k(ts(ell_i[:, 1, :], ell_i[:, 0, :], 4, None, ALU.arith_shift_right))
                    k(ts(ell_i[:, 2, :], ell_i[:, 0, :], 15, None, ALU.bitwise_and))
                    k(ts(jslot[:, 1, :], ell[:, 0, :], 1.0, 0.0, ALU.subtract, ALU.max))
                    k(ts(jslot[:, 0, :], ell[:, 0, :], 0.5, -100.0, ALU.is_lt, ALU.mult))
                    k(tt(jslot[:, 0, :], jslot[:, 0, :], ell_i[:, 2, :], ALU.add))
                    stt(out=src_idx[:], in0=jslot[:, 1, :], scalar=16.0, in1=ell_i[:, 1, :], op0=ALU.mult, op1=ALU.add).then_inc(s["idx_ready"], 1)
                    k(tt(pen[:], bc(jslot[:, 0, :], 1, NPO), bc(iota_j[:], 2, W), ALU.is_equal))
                    k(ts(pen[:], pen[:], 1.0, BIG, ALU.subtract, ALU.mult))
                if d:
                    for hf in range(2):
                        cols = slice(HALF * hf, HALF * hf + HALF)
                        v.wait_ge(s["sp_abs"], 2 * d + hf + 1)
                        ts(dtv[d][:, cols], banks(4 + 2 * hf, 2), vec[d][:, 1:2], 0.0, ALU.add, ALU.max).then_inc(s["sp_relu"], 1)
                v.wait_ge(s["sp_exp"], d + 1)
                k(ts(sp_c, sp_t, 1.0, 1.0, ALU.add, ALU.subtract))
                k(tt(sp_c, sp_t, sp_c, ALU.subtract))
                v.wait_ge(s["sp_ln"], d + 1)
                k(tt(sp_c, sp_c, uu[d], ALU.add))
                v.wait_ge(s["sp_relu"], 2 * d + 2)
                tt(dtv[d], dtv[d], sp_c, ALU.add).then_inc(s["dt_ready"], 1)
                if d == 0:
                    v.wait_ge(s["bc_ready"], 1)
                    v.wait_ge(s["nega_ready"], 2)
                    for dd in range(2):
                        k(ts(neg_a[dd][:], neg_a[dd][:], -1.0, None, ALU.mult))

            def no_decay(d):
                first = 0 if d == 0 else SEQ - 1
                k(v.memset(da[0].rearrange("p (b s) -> p b s", s=SEQ)[:, :, first:first + 1], 0.0))
                v.memset(da[1].rearrange("p (b s) -> p b s", s=SEQ)[:, :, first:first + 1], 0.0).then_inc(s["da_zero"], 1)

            def scan_state(blk, n, e):
                d, c0 = blk // 2, (blk % 2) * HALF
                v.wait_ge(s["b_psum"], n + 1)
                v.wait_ge(s["g_ready"], n + 1)
                tt(hh[e], uu[d][:, c0:c0 + HALF], banks(6 * e, 2), ALU.mult).then_inc(s["b_used"], 1)
                v.wait_ge(s["da_ready"], n + 1)
                v.wait_ge(s["b_used"], n + 3)
                o, x0, x1 = hh[e], da[e], hh[e]
                if d:
                    o, x0, x1 = o[:, ::-1], x0[:, ::-1], x1[:, ::-1]
                v.tensor_tensor_scan(o, x0, x1, 0.0, ALU.mult, ALU.add).then_inc(s["scan_ready"], 1)

            def gated(blk):
                d, c0 = blk // 2, (blk % 2) * HALF
                v.wait_ge(s["g_used"], 16 * blk + 18)
                tt(zs[d][:, c0:c0 + HALF], zs[d][:, c0:c0 + HALF], banks(4, 2), ALU.mult).then_inc(s["yg_ready"], 1)

            v.wait_ge(s["dt_ready"], 2)
            v.wait_ge(s["uu_ready"], 1)
            no_decay(0)
            for blk in range(4):
                if blk == 2:
                    v.wait_ge(s["uu_ready"], 2)
                    v.wait_ge(s["scan_ready"], 34)
                    no_decay(1)
                for e in range(2):
                    scan_state(blk, 16 * blk + e, e)
                if blk:
                    gated(blk - 1)
                with v.Fori(0, DS // 2 - 1) as it:
                    for e in range(2):
                        scan_state(blk, it * 2 + (16 * blk + 2 + e), e)
            gated(3)

            v.wait_ge(s["wffn_in"], 80)
            k(v.tensor_copy(b2_part[:, 0, :], b2[:]))
            k(tt(b2_rest, b2[:], b2_part[:, 0, :], ALU.subtract))
            k(v.tensor_copy(b2_part[:, 1, :], b2_rest))
            tt(b2_part[:, 2, :], b2_rest, b2_part[:, 1, :], ALU.subtract).then_inc(s["b2_ready"], 1)
            v.wait_ge(s["t2_psum"], 1)
            v.wait_ge(s["res_back"], 16)
            k(tt(t2.rearrange("p j c -> p (j c)"), resb.rearrange("p j c -> p (j c)"), banks(0, 2), ALU.add))
            k(v.tensor_reduce(out=lns[:, 0, :], in_=t2, axis=AX, op=ALU.add))
            k(ts(lns[:, 1, :], lns[:, 0, :], 1.0 / C, None, ALU.mult))
            for jj in (slice(0, NPO // 2), slice(NPO // 2, NPO)):
                tt(d_tok[:, jj], t2[:, jj], bc(lns[:, 1, jj], 2, C), ALU.subtract).then_inc(s["diff_ready"], 1)
            v.wait_ge(s["diff_ready"], 2)
            k(tt(v_tok, d_tok, d_tok, ALU.mult))
            k(v.tensor_reduce(out=lns[:, 2, :], in_=v_tok, axis=AX, op=ALU.add))
            ts(lns[:, 3, :], lns[:, 2, :], 1.0 / C, 1e-5, ALU.mult, ALU.add).then_inc(s["ln_var"], 1)
            v.wait_ge(s["ln_std"], 9)
            k(v.reciprocal(lns[:, 5, :], lns[:, 4, :]))
            v.wait_ge(s["att_in"], 32)
            v.wait_ge(s["h_psum"], 1)
            k(tt(hrow[:, :, 0:HE], ps[:, 2, 0:NPO * HE].rearrange("p (j n) -> p j n", j=NPO), bc(lns[:, 5, :], 2, HE), ALU.mult))
            k(tt(atmp[:], hrow[:, :, 0:HE], bc(att[:, 0, :], 1, NPO), ALU.mult))
            v.tensor_reduce(out=hrow[:, :, HE:ROW], in_=atmp[:].rearrange("p j (h x) -> p j h x", h=HEADS), axis=AX, op=ALU.add).then_inc(s["h_ready"], 1)
            tt(v_tok, d_tok, bc(lns[:, 5, :], 2, C), ALU.mult).then_inc(s["v_ready"], 1)
            v.wait_ge(s["h_ready"], 1)
            k(tt(atmp[:], hrow[:, :, 0:HE], bc(att[:, 1, :], 1, NPO), ALU.mult))
            k(v.tensor_reduce(out=adst[:].rearrange("p h j -> p j h"), in_=atmp[:].rearrange("p j (h x) -> p j h x", h=HEADS), axis=AX, op=ALU.add))
            k(tt(a_e, bc(pen[:], 1, HEADS), bc(adst[:], 3, W), ALU.add))

            def lrelu(dst, src):
                return stt(out=dst, in0=src, scalar=0.2, in1=src, op0=ALU.mult, op1=ALU.max)

            v.wait_ge(s["hist_back"], 16)
            v.wait_ge(s["last_in"], 16)
            k(v.tensor_reduce(out=cnt[:], in_=cnt4[:].rearrange("p g j -> p j g"), axis=AX, op=ALU.add))
            k(ts(gs[:, 0, :], cnt[:], 0.5, 1.0, ALU.is_gt, ALU.subtract))
            k(ts(gs[:, 0, :], gs[:, 0, :], BIG, None, ALU.mult))
            k(tt(g2[:], bc(gs[:, 0, :], 1, HEADS), bc(last[:, HE:ROW], 2, NPO), ALU.add))
            k(tt(g2[:], g2[:], adst[:], ALU.add))
            k(tt(g1[:], hrow[:, :, HE:ROW].rearrange("p j h -> p h j"), adst[:], ALU.add))
            k(tt(amax[:], g1[:], g2[:], ALU.max))
            k(lrelu(mcur[:], amax[:]))
            for t in (g1, g2):
                k(lrelu(t[:], t[:]))
                m = tt(t[:], t[:], mcur[:], ALU.subtract)
                if t is g1:
                    k(m)
                else:
                    m.then_inc(s["e_in"], 1)
            v.wait_ge(s["exp_ready"], 2)
            k(tt(g2[:], g2[:], bc(cnt[:], 1, HEADS), ALU.mult))
            k(tt(den[:], g1[:], g2[:], ALU.add))
            hself = hrow[:, :, 0:HE].rearrange("p j (h x) -> p h x j", h=HEADS)
            k.go(tt(acc[:], bc(g1[:], 2, EXP), hself, ALU.mult))
            k(tt(g4[:], bc(g2[:], 2, EXP), bc(last[:, 0:HE].rearrange("p (h x) -> p h x", h=HEADS), 3, NPO), ALU.mult))
            k(tt(acc[:], acc[:], g4[:], ALU.add))

            def flat(x):
                return x.rearrange("p h j w -> p (h j) w")

            ad2, mc2 = adst[:].rearrange("p h j -> p (h j)"), mcur[:].rearrange("p h j -> p (h j)")
            for c in range(WCH):
                ww, wc = slice(W_AT[c], W_AT[c + 1]), W_AT[c + 1] - W_AT[c]
                e_w, p_w = chunk_weights(wc), chunk_products(wc)
                v.wait_ge(s[f"nb_in{c}"], 16 * wc)
                k(tt(e_w, a_e[:, :, :, ww], bc(nb[:, ww, HE:ROW].rearrange("p w h -> p h w"), 2, NPO), ALU.add))
                k(v.tensor_reduce(out=mx[:], in_=e_w, axis=AX, op=ALU.max))
                k(tt(amax[:], amax[:], mx[:], ALU.max))
                k(lrelu(mx[:], amax[:]))
                k(tt(g1[:], mcur[:], mx[:], ALU.subtract))
                k.go(v.tensor_copy(mcur[:], mx[:]))
                k(lrelu(flat(e_w), flat(e_w)))
                tt(flat(e_w), flat(e_w), bc(mc2, 2, wc), ALU.subtract).then_inc(s["e_in"], 1)
                v.wait_ge(s["exp_ready"], 2 * c + 3)
                k.go(tt(den[:], den[:], g1[:], ALU.mult))
                k(tt(acc[:], acc[:], bc(g1[:], 2, EXP), ALU.mult))
                v.wait_ge(s["exp_ready"], 2 * c + 4)
                k(v.tensor_reduce(out=mx[:], in_=e_w, axis=AX, op=ALU.add))
                k.go(tt(den[:], den[:], mx[:], ALU.add))
                for h in range(HEADS):
                    k.go(tt(p_w[:, h], bc(e_w[:, h], 1, EXP), bc(nb[:, ww, EXP * h:EXP * h + EXP].rearrange("p w x -> p x w"), 2, NPO), ALU.mult))
                k.wait()
                k(v.tensor_reduce(out=g4[:], in_=p_w, axis=AX, op=ALU.add))
                k(tt(acc[:], acc[:], g4[:], ALU.add))

            def left_edges(n, c, at):
                done = [0]

                def step(ins):
                    done[0] += 1
                    ins.then_inc(s["left_step"], 1)
                    v.wait_ge(s["left_step"], at + done[0])

                step(v.tensor_copy(left_row[:, ROW:ROW + 1], m8[:, bass.ds(c, 1)]))
                step(ts(left_idx[:, 1:2], left_row[:, ROW:ROW + 1], -1.0, None, ALU.add))
                ts(left_idx[:, 0:1], left_idx[:, 1:2], LAST, None, ALU.bitwise_and).then_inc(s["left_idx_ready"], 1)
                v.wait_ge(s["left_in"], n * 16 + 16)
                step(ts(lk[:, 0, :], left_all[:, :, ROW], -1.0, None, ALU.add))
                step(ts(lk[:, 1, :], lk[:, 0, :], 15, None, ALU.arith_shift_right))
                step(ts(lkf[:, 0, :], lk[:, 1, :], pf[:], None, ALU.is_equal))
                step(ts(lk[:, 1, :], lk[:, 0, :], 11, 15, ALU.arith_shift_right, ALU.bitwise_and))
                step(stt(out=lkf[:, 1, :], in0=lk[:, 1, :], scalar=1.0, in1=lkf[:, 0, :], op0=ALU.add, op1=ALU.mult))
                step(ts(lkf[:, 1, :], lkf[:, 1, :], -1.0, None, ALU.add))
                for q in range(P // LW):
                    e0 = q * LW
                    step(tt(left_pen, bc(lkf[:, 1, e0:e0 + LW], 1, NPO), bc(iota_j[:], 2, LW), ALU.is_equal))
                    step(ts(left_pen, left_pen, 1.0, BIG, ALU.subtract, ALU.mult))
                    for h in range(HEADS):
                        step(tt(left_w[:, h], left_pen, bc(left_all[:, e0:e0 + LW, HE + h], 1, NPO), ALU.add))
                    step(v.tensor_reduce(out=mx[:], in_=left_w, axis=AX, op=ALU.max))
                    step(tt(mx[:], mx[:], adst[:], ALU.add))
                    step(tt(amax[:], amax[:], mx[:], ALU.max))
                    step(lrelu(mx[:], amax[:]))
                    step(tt(g1[:], mcur[:], mx[:], ALU.subtract))
                    step(v.tensor_copy(mcur[:], mx[:]))
                    step(tt(flat(left_w), flat(left_w), bc(ad2, 2, LW), ALU.add))
                    step(lrelu(flat(left_w), flat(left_w)))
                    tt(flat(left_w), flat(left_w), bc(mc2, 2, LW), ALU.subtract).then_inc(s["left_e"], 1)
                    v.wait_ge(s["left_exp"], n * (2 * (P // LW)) + (2 * q + 2))
                    step(tt(den[:], den[:], g1[:], ALU.mult))
                    step(v.tensor_reduce(out=mx[:], in_=left_w, axis=AX, op=ALU.add))
                    step(tt(den[:], den[:], mx[:], ALU.add))
                    for h in range(HEADS):
                        step(tt(left_p, bc(left_w[:, h], 1, EXP),
                                bc(left_all[:, e0:e0 + LW, EXP * h:EXP * h + EXP].rearrange("p w x -> p x w"), 2, NPO), ALU.mult))
                        step(v.tensor_reduce(out=g4[:, h], in_=left_p, axis=AX, op=ALU.add))
                        step(tt(acc[:, h], acc[:, h], bc(g1[:, h], 1, EXP), ALU.mult))
                        step(tt(acc[:, h], acc[:, h], g4[:, h], ALU.add))
                assert done[0] == LEFT_COLUMN, done[0]

            rounds = v.value_load(nleft_i[0:1, 0:1], min_val=0, max_val=EPP)
            with v.If(rounds > 0):
                with v.Fori(0, rounds) as r:
                    ls = s["left_step"]
                    v.max(out=m8[:], in_=keys[:]).then_inc(ls, 1)
                    v.wait_ge(ls, r * LEFT_ROUND + 1)
                    v.memset(pause[:, 1:2], 0.0).then_inc(ls, 1)
                    v.match_replace(out=keys[:], in_to_replace=m8[:], in_values=keys[:], imm_value=0.0).then_inc(ls, 1)
                    v.wait_ge(ls, r * LEFT_ROUND + 3)
                    v.memset(pause[:, 1:2], 0.0).then_inc(ls, 1)
                    with v.Fori(0, 8) as c:
                        at = r * LEFT_ROUND + c * LEFT_COLUMN + 4
                        left_edges(r * 8 + c, c, at)
            k(ts(den[:], den[:], 1e-16, None, ALU.add))
            k(v.reciprocal(den[:], den[:]))
            aggv = agg[:].rearrange("p j (h x) -> p h x j", h=HEADS)
            k(tt(aggv, acc[:], bc(den[:], 2, EXP), ALU.mult))
            k(tt(agg[:], agg[:], bc(rows16[:, 0, :], 1, NPO), ALU.add))
            norm(agg[:], agg[:], agg[:], atmp[:], gs[:], 10, HE, None)
            k(tt(agg[:], agg[:], bc(rows16[:, 1, :], 1, NPO), ALU.mult))
            k(tt(agg[:], agg[:], bc(rows16[:, 2, :], 1, NPO), ALU.add))
            k(v.tensor_reduce(out=sc[:], in_=agg[:].rearrange("p j (h x) -> p j x h", h=HEADS), axis=AX, op=ALU.add))
            k(ts(sc[:], sc[:], 1.0 / HEADS, None, ALU.mult))
            k(tt(cmp1, bc(sc[:], 2, EXP), bc(sc[:], 3, EXP), ALU.is_gt))
            k(tt(cmp2, bc(sc[:], 2, EXP), bc(sc[:], 3, EXP), ALU.is_equal))
            k(tt(cmp2.rearrange("p j a b -> p j (a b)"), cmp2.rearrange("p j a b -> p j (a b)"),
                 bc(tiebreak[:].rearrange("p a b -> p (a b)"), 1, NPO), ALU.mult))
            k(tt(cmp1, cmp1, cmp2, ALU.add))
            k(v.tensor_reduce(out=atmp[:, :, 0:EXP], in_=cmp1, axis=AX, op=ALU.add))
            k(v.tensor_reduce(out=gs[:, 0, :], in_=sc[:], axis=AX, op=ALU.max))
            tt(gate[:], sc[:], bc(gs[:, 0, :], 2, EXP), ALU.subtract).then_inc(s["ln_var"], 1)
            v.wait_ge(s["ln_std"], 11)
            k(stt(out=gate[:], in0=atmp[:, :, 0:EXP], scalar=1.5, in1=gate[:], op0=ALU.is_lt, op1=ALU.mult))
            k(v.tensor_reduce(out=gs[:, 1, :], in_=gate[:], axis=AX, op=ALU.add))
            k(v.reciprocal(gs[:, 1, :], gs[:, 1, :]))
            tt(gate[:], gate[:], bc(gs[:, 1, :], 2, EXP), ALU.mult).then_inc(s["gate_ready"], 1)
            v.wait_ge(s["gate_ready"], 1)
            v.wait_ge(s["eo_read"], 4)
            jj = slice(0, DVE_NODES)
            ev = eo[:, jj].rearrange("p j e c -> p (j e) c")
            k(tt(ev, ev, bc(gate[:, jj].rearrange("p j e -> p (j e)"), 2, C), ALU.mult))
            k(v.tensor_reduce(out=d_tok[:, jj], in_=eo[:, jj].rearrange("p j e c -> p j c e"), axis=AX, op=ALU.add))
            tt(t2[:, jj], t2[:, jj], d_tok[:, jj], ALU.add).then_inc(s["out_ready"], 1)


INS = ["x", "om_kernel", "om_bias", "kernel", "bias", "edges", "ln_gb", "w_gat", "att", "rows16", "w1", "b1", "w2", "b2"] + [
    p + n for p in ("f_", "b_") for n in ("in_w", "conv_w", "vec", "xp_w", "xd_w", "dp_w", "a_log", "o_w")]


def laid_out(x, **w):
    import numpy as np

    def c(v):
        return np.ascontiguousarray(v)

    r = {
        "x": c(x).reshape(T, C), "om_kernel": c(w["L0_conv_om_kernel"]).reshape(K2, C, OM),
        "om_bias": c(w["L0_conv_om_bias"]).reshape(OM, 1), "kernel": c(w["L0_conv_kernel"]),
        "bias": c(w["L0_conv_bias"]).reshape(1, C), "edges": c(w["L1_ffn_edge_index"]),
        "ln_gb": c(np.stack([w["L1_attn_ln_gamma"], w["L1_attn_ln_beta"]], 1)),
        "w_gat": c(w["L1_ffn_W_gat"]),
        "att": c(np.stack([w["L1_ffn_att_src"], w["L1_ffn_att_dst"]])).reshape(1, 2 * HE),
        "rows16": c(np.stack([w["L1_ffn_b_gat"], w["L1_ffn_ln_gamma"], w["L1_ffn_ln_beta"]])).reshape(1, 3 * HE),
        "w1": c(w["L1_ffn_W1"]), "b1": c(np.asarray(w["L1_ffn_b1"]).T), "w2": c(w["L1_ffn_W2"]),
        "b2": c(w["L1_ffn_b2"]).reshape(1, EXP * C),
    }
    for p in ("f_", "b_"):
        def m(n):
            return np.asarray(w["L1_attn_" + p + n])
        r[p + "in_w"] = c(m("in_proj_w").T)
        r[p + "conv_w"] = c(m("conv_w")[:, 0, :].T).reshape(1, TAPS * DI)
        r[p + "vec"] = c(np.stack([m("conv_b"), m("dt_proj_b"), m("D")], 1))
        r[p + "xp_w"] = c(m("x_proj_w").T)
        r[p + "xd_w"] = c(m("x_proj_w")[0:DTR])
        r[p + "dp_w"] = c(m("dt_proj_w").T)
        r[p + "a_log"] = c(m("A_log"))
        r[p + "o_w"] = c(m("out_proj_w").T)
    return r


def kernel(**inputs):
    import numpy as np
    import concourse.bacc as bacc
    from concourse.bass_utils import run_bass_kernel_spmd

    nc = bacc.Bacc("TRN2", target_bir_lowering=False, num_devices=1)
    arrays = laid_out(**{n: np.asarray(v) for n, v in inputs.items()})
    a = {n: nc.dram_tensor("dram_" + n, arrays[n].shape, mybir.dt.from_np(arrays[n].dtype), kind="ExternalInput").ap() for n in INS}
    out = nc.dram_tensor("out", [T, C], F32, kind="ExternalOutput").ap()
    program(nc, a, out)
    r = run_bass_kernel_spmd(nc, [{"dram_" + n: arrays[n] for n in INS}], core_ids=[0])
    return r.results[0]["out"].reshape(BATCH, HEIGHT, WIDTH, C)
```
